# Optimizing a Trainium2 kernel written in Bass

```python
import numpy as np
import jax
import jax.numpy as jnp

def _softmax(x, axis=-1):
    return jax.nn.softmax(x, axis=axis)

def _gelu(x):
    return jax.nn.gelu(x, approximate=True)

def _silu(x):
    return jax.nn.silu(x)

def _sigmoid(x):
    return jax.nn.sigmoid(x)

def _layernorm(x, axis=-1, eps=1e-05):
    m = jnp.mean(x, axis=axis, keepdims=True)
    v = jnp.var(x, axis=axis, keepdims=True)
    return (x - m) / jnp.sqrt(v + eps)

def _scatter_add(tgt, idx, src, axis=0):
    return tgt.at[idx].add(src)

def _segment_sum(src, seg, n):
    return jax.ops.segment_sum(src, seg, n)
kernel_name = 'mk_cond_seq_d4_seqx_r4_8a67de'

def setup_inputs(seed: int=0):
    np.random.seed(seed)
    _w = jnp.asarray

    def _rec_inputs():
        import jax
        import jax.numpy as jnp
        _rk = jax.random.key(seed)
        x = -0.000125 + 0.9999 * jax.random.normal(jax.random.fold_in(_rk, 1), (128, 64, 256), jnp.float32)
        _lenS = 64 - jax.random.randint(jax.random.fold_in(_rk, 7), (128,), 0, max(1, 64 // 4) + 1, jnp.int32)
        _lenS2 = 64 - jax.random.randint(jax.random.fold_in(_rk, 8), (128,), 0, max(1, 64 // 4) + 1, jnp.int32)
        itok_B_0_15 = jax.random.randint(jax.random.fold_in(_rk, 11), (128,), 0, 16, jnp.int32)
        itok_B_34_63 = jax.random.randint(jax.random.fold_in(_rk, 13), (128,), 34, 64, jnp.int32)
        fside_Bx16xSxS_0 = -1.47943e-05 + 1.00017 * jax.random.normal(jax.random.fold_in(_rk, 14), (128, 16, 64, 64), jnp.float32)
        condB_theta = jax.random.uniform(jax.random.fold_in(_rk, 15), (128,), jnp.float32, 0.0, 0.983423)
        condB_phi = jax.random.uniform(jax.random.fold_in(_rk, 16), (128,), jnp.float32, 0.0, 0.961312)
        condB_safetyscore = -0.927215 + 0.920279 * jax.random.normal(jax.random.fold_in(_rk, 17), (128,), jnp.float32)
        _validS = jnp.arange(64)[None, :] < _lenS[:, None]
        _validS2 = jnp.arange(64)[None, :] < _lenS2[:, None]
        _causal = jnp.tril(jnp.ones((64, 64), dtype=bool))
        mask_Bx1xSxS_bk0 = jnp.logical_not(jnp.broadcast_to(_validS[:, None, None, :], (128, 1, 64, 64)))
        return (x, itok_B_0_15, itok_B_34_63, fside_Bx16xSxS_0, condB_theta, condB_phi, condB_safetyscore, mask_Bx1xSxS_bk0)
    x, itok_B_0_15, itok_B_34_63, fside_Bx16xSxS_0, condB_theta, condB_phi, condB_safetyscore, mask_Bx1xSxS_bk0 = _rec_inputs()

    def _L0_cond_setup():
        import jax, jax.numpy as jnp
        import numpy as np
        B, S, D = (32, 256, 256)
        A = 64
        E = 16
        LN_EPS = 1e-05
        key = jax.random.key(seed)
        ks = jax.random.split(key, 10)
        s = lambda fan_in: 1.0 / np.sqrt(fan_in)
        return {'hidden_states': jax.random.normal(ks[0], (B, S, D), dtype=jnp.float32), 'domain_id': jax.random.randint(ks[1], (B,), 0, E, dtype=jnp.int64), 'down_W': jax.random.uniform(ks[2], (A, D), jnp.float32, -s(D), s(D)), 'down_b': jax.random.uniform(ks[3], (A,), jnp.float32, -s(D), s(D)), 'up_W': jax.random.uniform(ks[4], (D, A), jnp.float32, -s(A), s(A)), 'up_b': jax.random.uniform(ks[5], (D,), jnp.float32, -s(A), s(A)), 'expert_W': jax.random.uniform(ks[6], (E, A, A), jnp.float32, -s(A), s(A)), 'expert_b': jax.random.uniform(ks[7], (E, A), jnp.float32, -s(A), s(A)), 'domain_emb': jax.random.normal(ks[8], (E, A), dtype=jnp.float32), 'ln_gamma': jnp.ones((D,), jnp.float32), 'ln_beta': jnp.zeros((D,), jnp.float32)}
    _L0_cond_all = _L0_cond_setup()
    _L0_cond_in = {k: v for k, v in _L0_cond_all.items() if k in ('down_W', 'down_b', 'up_W', 'up_b', 'expert_W', 'expert_b', 'domain_emb', 'ln_gamma', 'ln_beta')}
    del _L0_cond_all

    def _L1_cond_setup():
        import jax, jax.numpy as jnp
        import numpy as np
        import math
        D_MODEL = 256
        N_HEAD = 16
        HEAD_DIM = D_MODEL // N_HEAD
        D_FF = 1024
        NUM_STEPS = 100.0
        RESCALE = 4000.0
        EPS = 1e-05

        def _sin_emb(t):
            half = D_MODEL // 2
            x = t.astype(jnp.float32) / NUM_STEPS * RESCALE
            freqs = jnp.exp(jnp.arange(half, dtype=jnp.float32) * (-math.log(10000.0) / (half - 1)))
            e = x[:, None] * freqs[None, :]
            return jnp.concatenate([jnp.sin(e), jnp.cos(e)], axis=-1)

        def _ln(x):
            m = jnp.mean(x, axis=-1, keepdims=True)
            v = jnp.var(x, axis=-1, keepdims=True)
            return (x - m) / jnp.sqrt(v + EPS)

        def _gelu2(x):
            return x * jax.nn.sigmoid(1.702 * x)
        key = jax.random.key(seed)
        ks = jax.random.split(key, 24)
        B, S, D, F = (4, 128, D_MODEL, D_FF)
        std = 0.02
        inp = {'src': jax.random.normal(ks[0], (B, S, D), dtype=jnp.float32), 'src_mask': jax.random.randint(ks[1], (B, 1, S, S), 0, 2).astype(bool), 'timestep': jax.random.randint(ks[2], (B,), 0, 100, dtype=jnp.int32), 'attention_bias': jax.random.normal(ks[3], (B, N_HEAD, S, S), dtype=jnp.float32), 'W_ada': jax.random.normal(ks[4], (D, 2 * D), dtype=jnp.float32) * std, 'b_ada': jnp.zeros((2 * D,), dtype=jnp.float32), 'Wq': jax.random.normal(ks[5], (D, D), dtype=jnp.float32) * std, 'bq': jnp.zeros((D,), dtype=jnp.float32), 'Wk': jax.random.normal(ks[6], (D, D), dtype=jnp.float32) * std, 'bk': jnp.zeros((D,), dtype=jnp.float32), 'Wv': jax.random.normal(ks[7], (D, D), dtype=jnp.float32) * std, 'bv': jnp.zeros((D,), dtype=jnp.float32), 'Wo': jax.random.normal(ks[8], (D, D), dtype=jnp.float32) * std, 'bo': jnp.zeros((D,), dtype=jnp.float32), 'W1': jax.random.normal(ks[9], (D, F), dtype=jnp.float32) * std, 'b1': jnp.zeros((F,), dtype=jnp.float32), 'W2': jax.random.normal(ks[10], (F, D), dtype=jnp.float32) * std, 'b2': jnp.zeros((D,), dtype=jnp.float32), 'g2': jnp.ones((D,), dtype=jnp.float32), 'beta2': jnp.zeros((D,), dtype=jnp.float32)}
        return inp
    _L1_cond_all = _L1_cond_setup()
    _L1_cond_in = {k: v for k, v in _L1_cond_all.items() if k in ('W_ada', 'b_ada', 'Wq', 'bq', 'Wk', 'bk', 'Wv', 'bv', 'Wo', 'bo', 'W1', 'b1', 'W2', 'b2', 'g2', 'beta2')}
    del _L1_cond_all

    def _L2_cond_setup():
        import jax, jax.numpy as jnp
        import numpy as np
        key = jax.random.key(seed)
        k1, k2, k3 = jax.random.split(key, 3)
        B, N, D = (16, 1024, 256)
        embeddings = jax.random.normal(k1, (B, N, D), dtype=jnp.float32)
        theta = jax.random.uniform(k2, (B,), dtype=jnp.float32)
        phi = jax.random.uniform(k3, (B,), dtype=jnp.float32)
        return {'embeddings': embeddings, 'theta': theta, 'phi': phi}
    _L2_cond_all = _L2_cond_setup()
    _L2_cond_in = {k: v for k, v in _L2_cond_all.items() if k in ()}
    del _L2_cond_all

    def _L3_cond_setup():
        import jax, jax.numpy as jnp
        import numpy as np
        TEMPERATURE = 1.0
        ACT_THRESHOLD = 0.1
        MAX_ACT = 1.0
        SAFETY_KNOB = 1.0
        EPS = 1e-08

        def gram_schmidt(X):
            r = X.shape[1]
            Q = X
            for i in range(r):
                q = Q[:, i]
                q = q / (jnp.linalg.norm(q) + EPS)
                Q = Q.at[:, i].set(q)
                coeffs = q @ Q[:, i + 1:]
                Q = Q.at[:, i + 1:].add(-jnp.outer(q, coeffs))
            return Q
        key = jax.random.key(seed)
        ks = jax.random.split(key, 8)
        B, S, D, R = (8, 1024, 256, 32)
        init_std = 0.02
        return {'hidden_states': jax.random.normal(ks[0], (B, S, D), jnp.float32), 'safety_score': jax.random.normal(ks[1], (B,), jnp.float32), 'U': jax.random.normal(ks[2], (D, R), jnp.float32) * init_std, 'V': jax.random.normal(ks[3], (D, R), jnp.float32) * init_std, 'safety_bias': jnp.zeros((D,), jnp.float32), 'gate_w1': jax.random.normal(ks[4], (D // 4, D), jnp.float32) * (1.0 / np.sqrt(D)), 'gate_b1': jnp.zeros((D // 4,), jnp.float32), 'gate_w2': jax.random.normal(ks[5], (1, D // 4), jnp.float32) * (1.0 / np.sqrt(D // 4)), 'gate_b2': jnp.zeros((1,), jnp.float32), 'resp_w': jax.random.normal(ks[6], (D, R), jnp.float32) * (1.0 / np.sqrt(R)), 'resp_b': jnp.zeros((D,), jnp.float32)}
    _L3_cond_all = _L3_cond_setup()
    _L3_cond_in = {k: v for k, v in _L3_cond_all.items() if k in ('U', 'V', 'safety_bias', 'gate_w1', 'gate_b1', 'gate_w2', 'gate_b2', 'resp_w', 'resp_b')}
    del _L3_cond_all
    return {'x': x, 'itok_B_0_15': itok_B_0_15, 'itok_B_34_63': itok_B_34_63, 'fside_Bx16xSxS_0': fside_Bx16xSxS_0, 'condB_theta': condB_theta, 'condB_phi': condB_phi, 'condB_safetyscore': condB_safetyscore, 'mask_Bx1xSxS_bk0': mask_Bx1xSxS_bk0, 'L0_cond_down_W': _L0_cond_in['down_W'], 'L0_cond_down_b': _L0_cond_in['down_b'], 'L0_cond_up_W': _L0_cond_in['up_W'], 'L0_cond_up_b': _L0_cond_in['up_b'], 'L0_cond_expert_W': _L0_cond_in['expert_W'], 'L0_cond_expert_b': _L0_cond_in['expert_b'], 'L0_cond_domain_emb': _L0_cond_in['domain_emb'], 'L0_cond_ln_gamma': _L0_cond_in['ln_gamma'], 'L0_cond_ln_beta': _L0_cond_in['ln_beta'], 'L1_cond_W_ada': _L1_cond_in['W_ada'], 'L1_cond_b_ada': _L1_cond_in['b_ada'], 'L1_cond_Wq': _L1_cond_in['Wq'], 'L1_cond_bq': _L1_cond_in['bq'], 'L1_cond_Wk': _L1_cond_in['Wk'], 'L1_cond_bk': _L1_cond_in['bk'], 'L1_cond_Wv': _L1_cond_in['Wv'], 'L1_cond_bv': _L1_cond_in['bv'], 'L1_cond_Wo': _L1_cond_in['Wo'], 'L1_cond_bo': _L1_cond_in['bo'], 'L1_cond_W1': _L1_cond_in['W1'], 'L1_cond_b1': _L1_cond_in['b1'], 'L1_cond_W2': _L1_cond_in['W2'], 'L1_cond_b2': _L1_cond_in['b2'], 'L1_cond_g2': _L1_cond_in['g2'], 'L1_cond_beta2': _L1_cond_in['beta2'], 'L3_cond_U': _L3_cond_in['U'], 'L3_cond_V': _L3_cond_in['V'], 'L3_cond_safety_bias': _L3_cond_in['safety_bias'], 'L3_cond_gate_w1': _L3_cond_in['gate_w1'], 'L3_cond_gate_b1': _L3_cond_in['gate_b1'], 'L3_cond_gate_w2': _L3_cond_in['gate_w2'], 'L3_cond_gate_b2': _L3_cond_in['gate_b2'], 'L3_cond_resp_w': _L3_cond_in['resp_w'], 'L3_cond_resp_b': _L3_cond_in['resp_b']}

def reference(x, itok_B_0_15, itok_B_34_63, fside_Bx16xSxS_0, condB_theta, condB_phi, condB_safetyscore, mask_Bx1xSxS_bk0, L0_cond_down_W, L0_cond_down_b, L0_cond_up_W, L0_cond_up_b, L0_cond_expert_W, L0_cond_expert_b, L0_cond_domain_emb, L0_cond_ln_gamma, L0_cond_ln_beta, L1_cond_W_ada, L1_cond_b_ada, L1_cond_Wq, L1_cond_bq, L1_cond_Wk, L1_cond_bk, L1_cond_Wv, L1_cond_bv, L1_cond_Wo, L1_cond_bo, L1_cond_W1, L1_cond_b1, L1_cond_W2, L1_cond_b2, L1_cond_g2, L1_cond_beta2, L3_cond_U, L3_cond_V, L3_cond_safety_bias, L3_cond_gate_w1, L3_cond_gate_b1, L3_cond_gate_w2, L3_cond_gate_b2, L3_cond_resp_w, L3_cond_resp_b):
    import jax
    import jax.numpy as jnp

    def _L0_cond_ref(hidden_states, domain_id, down_W, down_b, up_W, up_b, expert_W, expert_b, domain_emb, ln_gamma, ln_beta):
        import jax, jax.numpy as jnp
        import numpy as np
        B, S, D = (32, 256, 256)
        A = 64
        E = 16
        LN_EPS = 1e-05
        residual = hidden_states
        hidden = jnp.einsum('bsd,ad->bsa', hidden_states, down_W) + down_b
        hidden = jax.nn.gelu(hidden, approximate=False)
        valid = (domain_id >= 0) & (domain_id < E)
        idx = jnp.clip(domain_id, 0, E - 1)
        Wsel = expert_W[idx]
        bsel = expert_b[idx]
        expert_out = jnp.einsum('bsa,boa->bso', hidden, Wsel) + bsel[:, None, :]
        domain_output = jnp.where(valid[:, None, None], expert_out, hidden)
        hidden = domain_output + domain_emb[idx][:, None, :]
        hidden = jnp.einsum('bsa,da->bsd', hidden, up_W) + up_b
        x = hidden + residual
        mu = jnp.mean(x, axis=-1, keepdims=True)
        var = jnp.mean(jnp.square(x - mu), axis=-1, keepdims=True)
        return (x - mu) * jax.lax.rsqrt(var + LN_EPS) * ln_gamma + ln_beta

    def _L1_cond_ref(src, src_mask, timestep, attention_bias, W_ada, b_ada, Wq, bq, Wk, bk, Wv, bv, Wo, bo, W1, b1, W2, b2, g2, beta2):
        import jax, jax.numpy as jnp
        import numpy as np
        import math
        D_MODEL = 256
        N_HEAD = 16
        HEAD_DIM = D_MODEL // N_HEAD
        D_FF = 1024
        NUM_STEPS = 100.0
        RESCALE = 4000.0
        EPS = 1e-05

        def _sin_emb(t):
            half = D_MODEL // 2
            x = t.astype(jnp.float32) / NUM_STEPS * RESCALE
            freqs = jnp.exp(jnp.arange(half, dtype=jnp.float32) * (-math.log(10000.0) / (half - 1)))
            e = x[:, None] * freqs[None, :]
            return jnp.concatenate([jnp.sin(e), jnp.cos(e)], axis=-1)

        def _ln(x):
            m = jnp.mean(x, axis=-1, keepdims=True)
            v = jnp.var(x, axis=-1, keepdims=True)
            return (x - m) / jnp.sqrt(v + EPS)

        def _gelu2(x):
            return x * jax.nn.sigmoid(1.702 * x)
        B, S, D = src.shape
        emb = jax.nn.silu(_sin_emb(timestep)) @ W_ada + b_ada
        scale, shift = jnp.split(emb[:, None, :], 2, axis=-1)
        x = _ln(src) * (1.0 + scale) + shift
        q = (x @ Wq + bq).reshape(B, S, N_HEAD, HEAD_DIM).transpose(0, 2, 1, 3)
        k = (x @ Wk + bk).reshape(B, S, N_HEAD, HEAD_DIM).transpose(0, 2, 1, 3)
        v = (x @ Wv + bv).reshape(B, S, N_HEAD, HEAD_DIM).transpose(0, 2, 1, 3)
        scores = jnp.einsum('bhqd,bhkd->bhqk', q / math.sqrt(HEAD_DIM), k)
        scores = scores + attention_bias
        scores = jnp.where(src_mask, -jnp.inf, scores.astype(jnp.float32))
        probs = jax.nn.softmax(scores, axis=-1).astype(v.dtype)
        ctx = jnp.einsum('bhqk,bhkd->bhqd', probs, v)
        ctx = ctx.transpose(0, 2, 1, 3).reshape(B, S, D)
        x = x + (ctx @ Wo + bo)
        h = _ln(x) * g2 + beta2
        ff = _gelu2(h @ W1 + b1) @ W2 + b2
        return x + ff

    def _L2_cond_ref(embeddings, theta, phi):
        import jax, jax.numpy as jnp
        import numpy as np
        B, N, D = embeddings.shape
        e = embeddings.reshape(B, N, D // 4, 4)
        ct = jnp.cos(theta)[:, None, None]
        st = jnp.sin(theta)[:, None, None]
        cp = jnp.cos(phi)[:, None, None]
        sp = jnp.sin(phi)[:, None, None]
        x0, x1, x2, x3 = (e[..., 0], e[..., 1], e[..., 2], e[..., 3])
        out = jnp.stack([x0 * ct + x1 * st, -x0 * st + x1 * ct, x2 * cp + x3 * sp, -x2 * sp + x3 * cp], axis=-1)
        return out.reshape(B, N, D)

    def _L3_cond_ref(hidden_states, safety_score, U, V, safety_bias, gate_w1, gate_b1, gate_w2, gate_b2, resp_w, resp_b):
        import jax, jax.numpy as jnp
        import numpy as np
        TEMPERATURE = 1.0
        ACT_THRESHOLD = 0.1
        MAX_ACT = 1.0
        SAFETY_KNOB = 1.0
        EPS = 1e-08

        def gram_schmidt(X):
            r = X.shape[1]
            Q = X
            for i in range(r):
                q = Q[:, i]
                q = q / (jnp.linalg.norm(q) + EPS)
                Q = Q.at[:, i].set(q)
                coeffs = q @ Q[:, i + 1:]
                Q = Q.at[:, i + 1:].add(-jnp.outer(q, coeffs))
            return Q
        R = resp_w.shape[1]
        U_o = gram_schmidt(U)
        V_o = gram_schmidt(V)
        basis = U_o @ V_o.T
        pooled = hidden_states.mean(axis=1)
        h1 = jax.nn.relu(pooled @ gate_w1.T + gate_b1)
        base_act = jax.nn.sigmoid(h1 @ gate_w2.T + gate_b2)
        mod = jax.nn.sigmoid(safety_score[:, None] / TEMPERATURE)
        knob = jnp.clip(jnp.asarray(SAFETY_KNOB, hidden_states.dtype), ACT_THRESHOLD, MAX_ACT)
        strength = (base_act * mod * knob)[:, None, :]
        proj = hidden_states @ basis
        feats = proj @ basis.T[:, :R]
        response = feats @ resp_w.T + resp_b + safety_bias
        return hidden_states + strength * response
    x = _L0_cond_ref(x, itok_B_0_15, L0_cond_down_W, L0_cond_down_b, L0_cond_up_W, L0_cond_up_b, L0_cond_expert_W, L0_cond_expert_b, L0_cond_domain_emb, L0_cond_ln_gamma, L0_cond_ln_beta)
    x = _L1_cond_ref(x, mask_Bx1xSxS_bk0, itok_B_34_63, fside_Bx16xSxS_0, L1_cond_W_ada, L1_cond_b_ada, L1_cond_Wq, L1_cond_bq, L1_cond_Wk, L1_cond_bk, L1_cond_Wv, L1_cond_bv, L1_cond_Wo, L1_cond_bo, L1_cond_W1, L1_cond_b1, L1_cond_W2, L1_cond_b2, L1_cond_g2, L1_cond_beta2)
    x = _L2_cond_ref(x, condB_theta, condB_phi)
    x = _L3_cond_ref(x, condB_safetyscore, L3_cond_U, L3_cond_V, L3_cond_safety_bias, L3_cond_gate_w1, L3_cond_gate_b1, L3_cond_gate_w2, L3_cond_gate_b2, L3_cond_resp_w, L3_cond_resp_b)
    return x

_drawn_inputs = setup_inputs


def setup_inputs(seed=0):
    import zlib

    import numpy as np

    out = dict(_drawn_inputs(seed))
    spreads = {'L0_cond_ln_gamma': (1.0, 0.2),
     'L0_cond_ln_beta': (0.0, 0.1),
     'L1_cond_b_ada': (0.0, 0.1),
     'L1_cond_bq': (0.0, 0.8),
     'L1_cond_bk': (0.0, 0.8),
     'L1_cond_bv': (0.0, 0.267),
     'L1_cond_bo': (0.0, 0.1),
     'L1_cond_b1': (0.0, 0.1),
     'L1_cond_b2': (0.0, 0.1),
     'L1_cond_g2': (1.0, 0.6),
     'L1_cond_beta2': (0.0, 0.681),
     'L3_cond_safety_bias': (0.0, 0.363),
     'L3_cond_gate_b1': (0.0, 0.8),
     'L3_cond_resp_b': (0.0, 0.398)}
    factors = {'fside_Bx16xSxS_0': 4.042,
     'L0_cond_down_b': 8.0,
     'L1_cond_Wq': 8.0,
     'L1_cond_Wk': 8.0,
     'L3_cond_V': 8.0,
     'L3_cond_gate_w1': 3.679,
     'L3_cond_gate_w2': 5.707}
    for name, (base, spread) in spreads.items():
        noise = np.random.default_rng([zlib.crc32(name.encode()), seed]).standard_normal(out[name].shape)
        drawn = base * np.exp(spread * noise) if base else spread * noise
        out[name] = jnp.asarray(drawn.astype(out[name].dtype))
    for name, factor in factors.items():
        out[name] = (out[name] * factor).astype(out[name].dtype)
    return out
```

```python
from contextlib import ExitStack

import numpy as np

import concourse.bass as bass
from concourse import mybir

ALU = mybir.AluOpType
ACT = mybir.ActivationFunctionType
AX = mybir.AxisListType.X
F32 = mybir.dt.float32
BF16 = mybir.dt.bfloat16
I32 = mybir.dt.int32
U8 = mybir.dt.uint8

P = 128
B, S, D = 128, 64, 256
H, DH = 16, 16
A = 64
E = 16
F = 1024
R = 32
KC = D // P
FC = F // P
TILE_B = P // S
NT = B // TILE_B
ST = 4
NST = NT // ST
STB = ST * TILE_B
N = ST * P
SLOTS = 4
GRP = 4
VW = DH + 1
LN_EPS = 1e-5
GS_EPS = 1e-8
MASKED = -1e30
TWO_PI = (6.28125, 1.93500518798828125e-3, 3.0199159819567e-7)
PI_IN = 3.1415925

COLS = {}
_at = 0
for _name, _n in (("bk", SLOTS), ("bq", 2 * SLOTS), ("bv", KC), ("bo", KC), ("b1", FC), ("b2", KC), ("g2", KC),
                  ("beta2", KC), ("b_scale", KC), ("b_shift", KC), ("gate_b1", 1), ("down_b", 1), ("gate_b2", 1),
                  ("freq", 1), ("gate_w2", 1)):
    COLS[_name] = slice(_at, _at + _n)
    _at += _n
NCOL = _at


class Done:

    def __init__(self, sem, steps):
        self.sem, self.steps, self.per, self.next = sem, steps, len(steps), 0

    def at(self, step, rnd):
        return rnd * self.per + (self.steps.index(step) + 1)

    def step(self, step):
        assert self.steps[self.next % self.per] == step, (step, self.steps[self.next % self.per])
        self.next += 1
        return self.sem, 1


def tiles(*names, n=ST):
    return [f"{name}{i}" for i in range(n) for name in names]


def build(nc, a, out):
    ctx = ExitStack()
    with ctx:
        def sb(name, shape, dt=F32):
            return ctx.enter_context(nc.sbuf_tensor(name, shape, dt))

        def sem(name):
            return ctx.enter_context(nc.semaphore(name))

        ps_s = ctx.enter_context(nc.psum_tensor("ps_s", [P, 2, 512], F32))
        ps_t = ctx.enter_context(nc.psum_tensor("ps_t", [P, 2, 512], F32))
        ps_o = ctx.enter_context(nc.psum_tensor("ps_o", [P, 2, 512], F32))
        ps_l = ctx.enter_context(nc.psum_tensor("ps_l", [P, 2, 512], F32))

        wq, wk, wv, wo = (sb(n, [P, KC, D]) for n in ("wq", "wk", "wv", "wo"))
        w1 = sb("w1", [P, KC, F])
        w2 = sb("w2", [P, FC, D])
        wdown = sb("wdown", [P, KC, A])
        wup = sb("wup", [P, D])
        gate_w1 = sb("gate_w1", [P, KC, A])
        resp = sb("resp", [R + 2, D])
        basis_p = sb("basis_p", [P, KC, R])
        cols = sb("cols", [P, NCOL])
        rows = sb("rows", [P, 3, D])
        ident = sb("ident", [P, P])
        ident16 = sb("ident16", [P, P], BF16)
        fold = sb("fold", [P, S])
        tanh_b1 = sb("tanh_b1", [P, FC])
        half_b1 = sb("half_b1", [P, FC])
        half_gb2 = sb("half_gb2", [P, 1])
        scale1 = sb("scale1", [P, KC, B])
        shift = sb("shift", [P, KC, B])
        bias_e = sb("bias_e", [P, NT])
        gidx = sb("gidx", [P, NT], I32)
        maskneg = sb("maskneg", [P, NT, S], BF16)
        rot_c = sb("rot_c", [P, NT, 4])
        rot_s = sb("rot_s", [P, NT, 4])
        modh = sb("modh", [P, NT])
        neghalf = sb("neghalf", [P, ST])
        eps = sb("eps", [P, ST])
        spare = sb("spare", [P, 6])
        gel = sb("gel", [P, NST, ST * S])
        xin = sb("xin", [P, 2, ST, D])
        big = sb("big", [P, FC, N])

        scr = ExitStack()
        with scr, nc.Block() as block:
            def tmp(name, shape, dt=F32):
                return scr.enter_context(nc.sbuf_tensor(name, shape, dt))

            loaded = scr.enter_context(nc.semaphore("loaded"))
            made = scr.enter_context(nc.semaphore("made"))
            dchain = scr.enter_context(nc.semaphore("dchain"))
            pchain = scr.enter_context(nc.semaphore("pchain"))
            achain = scr.enter_context(nc.semaphore("achain"))
            tchain = scr.enter_context(nc.semaphore("tchain"))
            gs_row = scr.enter_context(nc.semaphore("gs_row"))
            gs_sel = scr.enter_context(nc.semaphore("gs_sel"))
            gs_sq = scr.enter_context(nc.semaphore("gs_sq"))
            gs_norm = scr.enter_context(nc.semaphore("gs_norm"))
            gs_dve = scr.enter_context(nc.semaphore("gs_dve"))
            gs_neg = scr.enter_context(nc.semaphore("gs_neg"))

            wada = tmp("wada", [P, KC, 2 * D])
            mask8 = tmp("mask8", [P, NT, S], U8)
            uv = tmp("uv", [2 * R, D])
            vcopy = tmp("vcopy", [R, D])
            basis_t = tmp("basis_t", [P, KC, D])
            basis_r = tmp("basis_r", [P, KC, R])
            gmask = tmp("gmask", [2 * R, P])
            rmod = tmp("rmod", [2 * R, 1])
            cnt = tmp("cnt", [2 * R, 1])
            sel_e = tmp("sel_e", [2 * R, 1])
            later = tmp("later", [2 * R, 1])
            sel = tmp("sel", [2 * R, P])
            sq = tmp("sq", [2 * R, D])
            pr = tmp("pr", [2 * R, D])
            g = tmp("g", [2 * R, 12])
            halfs = tmp("halfs", [2 * R, 1])
            gseps = tmp("gseps", [2 * R, 1])
            ti = tmp("ti", [P, B], I32)
            ang = tmp("ang", [P, 3, B])
            red = tmp("red", [P, 3, B])
            kf = tmp("kf", [P, 3, B])
            ki = tmp("ki", [P, 3, B], I32)
            sc = tmp("sc", [P, 2, 3, B])
            th = tmp("th", [P, 2, B])
            emb = tmp("emb", [P, 2, B])
            tokf = tmp("tokf", [P, 3, NT])
            idi = tmp("idi", [P, NT], I32)
            idf = tmp("idf", [P, 4, NT])
            oi = tmp("oi", [P, 1])
            eri = tmp("eri", [E, B], I32)
            erf_ = tmp("erf", [E, 3, B])
            etab = tmp("etab", [E, 2, A])
            eno = tmp("eno", [E, 1])

            LOADS = 0
            loads = [
                (wq[:], a["wq"].rearrange("(c p) n -> p c n", p=P)), (wk[:], a["wk"].rearrange("(c p) n -> p c n", p=P)),
                (wv[:], a["wv"].rearrange("(c p) n -> p c n", p=P)), (wo[:], a["wo"].rearrange("(c p) n -> p c n", p=P)),
                (w1[:], a["w1"].rearrange("(c p) n -> p c n", p=P)), (w2[:], a["w2"].rearrange("(c p) n -> p c n", p=P)),
                (wdown[:], a["wdown"].rearrange("(c p) n -> p c n", p=P)),
                (gate_w1[:], a["gate_w1"].rearrange("(c p) n -> p c n", p=P)),
                (wada[:], a["wada"].rearrange("(c p) n -> p c n", p=P)),
                (wup[0:A, :], a["wup"]), (wup[A:P, :], a["wup"]), (resp[:], a["resp"]), (cols[:], a["cols"]),
                (rows[:], a["rows"]), (mask8[:], a["mask"]), (uv[:], a["uv"]), (ti[:], a["tstep"]),
                (tokf[:], a["tokf"]), (idi[:], a["ids_tok"]), (eri[:], a["ids_row"]), (etab[:], a["etab"]),
            ]
            LOADS = 16 * len(loads)

            @block.sync
            def _(sp):
                for dst, src in loads:
                    sp.dma_start(dst, src).then_inc(loaded, 16)

            @block.gpsimd
            def _(pool):
                n = [0]

                def link(ins):
                    n[0] += 1
                    ins.then_inc(pchain, 1)
                    pool.wait_ge(pchain, n[0])

                link(nc.gpsimd.memset(ident[:], 0.0))
                link(nc.gpsimd.affine_select(out=ident[:], in_=ident[:], compare_op=ALU.not_equal, fill=1.0, base=0,
                                             pattern=[[-1, P]], channel_multiplier=1))
                link(nc.gpsimd.tensor_copy(ident16[:], ident[:]))
                link(nc.gpsimd.tensor_copy(fold[0:S, :], ident[0:S, 0:S]))
                link(nc.gpsimd.tensor_copy(fold[S:P, :], ident[S:P, S:P]))
                link(nc.gpsimd.memset(gmask[:], 0.0))
                link(nc.gpsimd.memset(gmask[0:R, 0:R], 1.0))
                link(nc.gpsimd.memset(gmask[R:2 * R, R:2 * R], 1.0))
                link(nc.gpsimd.iota(rmod[0:R, :], pattern=[[0, 1]], base=0, channel_multiplier=1,
                                    allow_small_or_imprecise_dtypes=True))
                link(nc.gpsimd.iota(rmod[R:2 * R, :], pattern=[[0, 1]], base=0, channel_multiplier=1,
                                    allow_small_or_imprecise_dtypes=True))
                link(nc.gpsimd.iota(oi[0:A, :], pattern=[[0, 1]], base=0, channel_multiplier=1,
                                    allow_small_or_imprecise_dtypes=True))
                link(nc.gpsimd.iota(oi[A:P, :], pattern=[[0, 1]], base=0, channel_multiplier=1,
                                    allow_small_or_imprecise_dtypes=True))
                link(nc.gpsimd.iota(eno[:], pattern=[[0, 1]], base=0, channel_multiplier=1,
                                    allow_small_or_imprecise_dtypes=True))
                link(nc.gpsimd.memset(cnt[:], 0.0))
                link(nc.gpsimd.memset(neghalf[:], -0.5))
                link(nc.gpsimd.memset(eps[:], LN_EPS))
                link(nc.gpsimd.memset(gseps[:], GS_EPS))
                nc.gpsimd.memset(halfs[:], 0.5).then_inc(made, 1)
                pool.wait_ge(made, 1)
                with pool.Fori(0, R) as i:
                    pool.wait_ge(gs_sq, i + 1)
                    nc.gpsimd.tensor_tensor(g[:, 1:2], g[:, 0:1], halfs[:], ALU.pow).then_inc(gs_norm, 1)
                    pool.wait_ge(gs_norm, i * 2 + 1)
                    nc.gpsimd.tensor_tensor(g[:, 2:3], g[:, 1:2], gseps[:], ALU.add).then_inc(gs_norm, 1)
                pool.wait_ge(gs_sq, R + 1)
                nc.gpsimd.tensor_tensor(g[:, 9:10], g[:, 8:9], halfs[:], ALU.pow).then_inc(gs_norm, 1)
                pool.wait_ge(gs_norm, 2 * R + 1)
                nc.gpsimd.tensor_tensor(g[:, 10:11], g[:, 9:10], gseps[:], ALU.add).then_inc(gs_norm, 1)

            @block.tensor
            def _(pe):
                pe.wait_ge(loaded, LOADS)
                pe.wait_ge(made, 1)
                pe.wait_ge(dchain, D_EMB)
                for m in range(2 * KC):
                    for k in range(KC):
                        last = nc.tensor.matmul(ps_l[:, 0, m * B:(m + 1) * B], wada[:, k, m * P:(m + 1) * P], emb[:, k, :],
                                                start=(k == 0), stop=(k == KC - 1))
                last.then_inc(tchain, 1)
                hot = erf_[:].rearrange("e t (j h) -> e t j h", h=TILE_B)
                for h in range(TILE_B):
                    for t in range(2):
                        last = nc.tensor.matmul(ps_l[h * A:(h + 1) * A, 1, 0:NT], etab[:, t, :], hot[:, t, :, h],
                                                start=(t == 0), stop=(t == 1))
                last.then_inc(tchain, 1)
                with pe.Fori(0, R) as i:
                    pe.wait_ge(gs_sel, i + 1)
                    nc.tensor.matmul(ps_s[:, 0, 0:D], sel[:], uv[:], start=True, stop=True)
                    nc.tensor.matmul(ps_s[:, 1, 0:D], sel[:], uv[:], start=True, stop=True).then_inc(gs_row, 1)
                pe.wait_ge(dchain, D_ORTHO)
                for m in range(KC):
                    nc.tensor.matmul(ps_s[:, 0, m * R:(m + 1) * R], vcopy[:, m * P:(m + 1) * P], uv[0:R, 0:R],
                                     start=True, stop=True)
                for m in range(KC):
                    last = nc.tensor.matmul(ps_s[:, 1, m * D:(m + 1) * D], vcopy[:, m * P:(m + 1) * P], uv[0:R, :],
                                            start=True, stop=True)
                last.then_inc(tchain, 1)
                pe.wait_ge(dchain, D_BASIS)
                for m in range(KC):
                    for k in range(KC):
                        last = nc.tensor.matmul(ps_l[:, 0, m * R:(m + 1) * R], basis_t[:, k, m * P:(m + 1) * P],
                                                basis_r[:, k, :], start=(k == 0), stop=(k == KC - 1))
                last.then_inc(tchain, 1)

            @block.scalar
            def _(act):
                act.wait_ge(dchain, D_RED)
                nc.scalar.activation(sc[:, 0], red[:], ACT.Sin).then_inc(achain, 1)
                nc.scalar.activation(sc[:, 1], kf[:], ACT.Sin).then_inc(achain, 1)
                act.wait_ge(achain, 2)
                nc.scalar.activation(th[:], sc[:, :, 0, :], ACT.Tanh, scale=0.5).then_inc(achain, 1)
                nc.scalar.activation(modh[:], tokf[:, 2, :], ACT.Tanh, scale=0.5).then_inc(achain, 1)
                with act.Fori(0, R) as i:
                    act.wait_ge(gs_row, i + 1)
                    nc.scalar.activation(sq[:], ps_s[0:2 * R, 1, 0:D], ACT.Square, accum_out=g[:, 0:1]).then_inc(gs_sq, 1)
                act.wait_ge(gs_dve, R * GSD)
                nc.scalar.activation(sq[:], uv[:], ACT.Square, accum_out=g[:, 8:9]).then_inc(gs_sq, 1)

            @block.vector
            def _(dve):
                n = [0]

                def link(ins):
                    n[0] += 1
                    ins.then_inc(dchain, 1)
                    dve.wait_ge(dchain, n[0])

                v = nc.vector
                dve.wait_ge(loaded, LOADS)
                dve.wait_ge(made, 1)
                link(v.tensor_scalar(maskneg[:], mask8[:], MASKED, None, ALU.mult))
                link(v.tensor_copy(ang[:, 0, :], ti[:]))
                link(v.tensor_scalar(ang[:, 0, :], ang[:, 0, :], 40.0, cols[:, COLS["freq"]], ALU.mult, ALU.mult))
                link(v.memset(ang[:, 1:3, NT:B], 0.0))
                link(v.tensor_copy(ang[:, 1:3, 0:NT], tokf[:, 0:2, :]))
                link(v.tensor_scalar(kf[:], ang[:], 1.0 / (2.0 * np.pi), None, ALU.mult))
                link(v.tensor_copy(ki[:], kf[:]))
                link(v.tensor_copy(kf[:], ki[:]))
                src = ang
                for part in TWO_PI:
                    link(v.scalar_tensor_tensor(red[:], kf[:], -part, src[:], ALU.mult, ALU.add))
                    src = red
                link(v.tensor_scalar(red[:], red[:], PI_IN, -PI_IN, ALU.min, ALU.max))
                link(v.scalar_tensor_tensor(kf[:], red[:], -1.0, red[:], ALU.mult, ALU.max))
                link(v.tensor_scalar(kf[:], kf[:], -1.0, float(np.pi / 2), ALU.mult, ALU.add))
                assert n[0] == D_RED, n[0]
                dve.wait_ge(achain, 4)
                link(v.tensor_scalar(th[:], th[:], 0.5, 0.5, ALU.mult, ALU.add))
                link(v.tensor_tensor(emb[:], th[:], sc[:, :, 0, :], ALU.mult))
                link(v.tensor_scalar(modh[:], modh[:], 0.25, 0.25, ALU.mult, ALU.add))
                for j, ang_no in ((0, 1), (2, 2)):
                    for q in range(2):
                        link(v.tensor_copy(rot_c[:, :, j + q], sc[:, 1, ang_no, 0:NT]))
                        link(v.tensor_scalar(rot_s[:, :, j + q], sc[:, 0, ang_no, 0:NT], 1.0 if q == 0 else -1.0, None, ALU.mult))
                link(v.tensor_copy(idf[:, 0, :], idi[:]))
                link(v.tensor_scalar(idf[:, 1, :], idf[:, 0, :], 0.0, None, ALU.is_ge))
                link(v.tensor_scalar(idf[:, 2, :], idf[:, 0, :], float(E - 1), None, ALU.is_le))
                link(v.tensor_tensor(idf[:, 1, :], idf[:, 1, :], idf[:, 2, :], ALU.mult))
                link(v.tensor_scalar(idf[:, 0, :], idf[:, 0, :], 0.0, float(E), ALU.max, ALU.min))
                link(v.tensor_scalar(idf[:, 0, :], idf[:, 0, :], float(-E), None, ALU.add))
                link(v.tensor_tensor(idf[:, 0, :], idf[:, 0, :], idf[:, 1, :], ALU.mult))
                link(v.tensor_scalar(idf[:, 0, :], idf[:, 0, :], float(E), float(A), ALU.add, ALU.mult))
                link(v.tensor_scalar(gidx[:], idf[:, 0, :], oi[:], None, ALU.add))
                link(v.tensor_copy(erf_[:, 2, :], eri[:]))
                link(v.tensor_scalar(erf_[:, 0, :], erf_[:, 2, :], eno[:], None, ALU.is_equal))
                link(v.tensor_scalar(erf_[:, 2, :], erf_[:, 2, :], 0.0, float(E - 1), ALU.max, ALU.min))
                link(v.tensor_scalar(erf_[:, 1, :], erf_[:, 2, :], eno[:], None, ALU.is_equal))
                assert n[0] == D_EMB, n[0]
                link(v.tensor_scalar(tanh_b1[:], cols[:, COLS["b1"]], 0.851, None, ALU.mult))
                link(v.tensor_scalar(half_b1[:], cols[:, COLS["b1"]], 0.5, None, ALU.mult))
                link(v.tensor_scalar(half_gb2[:], cols[:, COLS["gate_b2"]], 0.5, None, ALU.mult))
                link(v.tensor_scalar(cols[:, COLS["bq"]], cols[:, COLS["bq"]], 0.25, None, ALU.mult))
                dve.wait_ge(tchain, 2)
                for k in range(KC):
                    link(v.tensor_scalar(scale1[:, k, :], ps_l[:, 0, k * B:(k + 1) * B],
                                         cols[:, COLS["b_scale"].start + k:COLS["b_scale"].start + k + 1], 1.0, ALU.add, ALU.add))
                    link(v.tensor_scalar(shift[:, k, :], ps_l[:, 0, (KC + k) * B:(KC + k + 1) * B],
                                         cols[:, COLS["b_shift"].start + k:COLS["b_shift"].start + k + 1], None, ALU.add))
                link(v.tensor_copy(bias_e[:], ps_l[:, 1, 0:NT]))
                with dve.Fori(0, R) as i:
                    base = i * GSD
                    v.tensor_scalar(sel_e[:], rmod[:], cnt[:], None, ALU.is_equal).then_inc(gs_dve, 1)
                    v.tensor_scalar(later[:], rmod[:], cnt[:], None, ALU.is_gt).then_inc(gs_dve, 1)
                    dve.wait_ge(gs_dve, base + 2)
                    v.tensor_scalar(sel[:], gmask[:], sel_e[:], None, ALU.mult).then_inc(gs_sel, 1)
                    v.tensor_scalar(cnt[:], cnt[:], 1.0, None, ALU.add).then_inc(gs_dve, 1)
                    dve.wait_ge(gs_row, i + 1)
                    v.tensor_tensor(pr[:], ps_s[0:2 * R, 0, 0:D], uv[:], ALU.mult).then_inc(gs_dve, 1)
                    dve.wait_ge(gs_dve, base + 4)
                    v.reduce_sum(g[:, 3:4], pr[:], axis=AX).then_inc(gs_dve, 1)
                    dve.wait_ge(gs_norm, i * 2 + 2)
                    v.reciprocal(g[:, 4:5], g[:, 2:3]).then_inc(gs_dve, 1)
                    dve.wait_ge(gs_dve, base + 6)
                    v.tensor_scalar(g[:, 5:6], g[:, 3:4], g[:, 4:5], -1.0, ALU.mult, ALU.mult).then_inc(gs_dve, 1)
                    dve.wait_ge(gs_dve, base + 7)
                    v.tensor_scalar(g[:, 6:7], g[:, 5:6], g[:, 4:5], later[:], ALU.mult, ALU.mult).then_inc(gs_dve, 1)
                    dve.wait_ge(gs_dve, base + 8)
                    v.scalar_tensor_tensor(uv[:], ps_s[0:2 * R, 0, 0:D], g[:, 6:7], uv[:], ALU.mult, ALU.add).then_inc(gs_dve, 1)
                    dve.wait_ge(gs_dve, base + 9)
                dve.wait_ge(gs_norm, 2 * R + 2)
                link(v.reciprocal(g[:, 11:12], g[:, 10:11]))
                link(v.tensor_scalar(uv[:], uv[:], g[:, 11:12], None, ALU.mult))
                link(v.tensor_copy(vcopy[:], uv[R:2 * R, :]))
                assert n[0] == D_ORTHO, n[0]
                dve.wait_ge(tchain, 3)
                link(v.tensor_copy(basis_r[:], ps_s[:, 0, 0:KC * R].rearrange("p (k r) -> p k r", k=KC)))
                link(v.tensor_copy(basis_t[:], ps_s[:, 1, :].rearrange("p (k d) -> p k d", k=KC)))
                assert n[0] == D_BASIS, n[0]
                dve.wait_ge(tchain, 4)
                link(v.tensor_copy(basis_p[:], ps_l[:, 0, 0:KC * R].rearrange("p (k r) -> p k r", k=KC)))

        with ExitStack() as scr, nc.Block() as block:
            xta = scr.enter_context(nc.sbuf_tensor("xta", [P, 2, KC, N], F32))
            x_in = [scr.enter_context(nc.semaphore(f"dn_x{b}")) for b in range(2)]
            dn_tr = scr.enter_context(nc.semaphore("dn_tr"))
            dn_xt = scr.enter_context(nc.semaphore("dn_xt"))
            dn_mm = scr.enter_context(nc.semaphore("dn_mm"))
            dn_act = scr.enter_context(nc.semaphore("dn_act"))

            @block.sync
            def _(sp):
                for b in range(2):
                    sp.dma_start(xin[:, b], a["x"][b]).then_inc(x_in[b], 16)
                with sp.Fori(1, NST // 2) as t:
                    for b in range(2):
                        sp.wait_ge(dn_tr, t * (2 * KC) + (b - 1) * KC)
                        sp.dma_start(xin[:, b], a["x"][bass.ds(t * 2 + b, 1)].rearrange("o p i d -> (o p) i d")).then_inc(x_in[b], 16)

            @block.tensor
            def _(pe):
                with pe.Fori(0, NST // 2) as t:
                    for b in range(2):
                        s = t * 2 + b
                        pe.wait_ge(x_in[b], (t + 1) * 16)
                        for k in range(KC):
                            for i in range(ST):
                                last = nc.tensor.transpose(ps_s[:, k, i * P:(i + 1) * P] if b == 0 else ps_t[:, k, i * P:(i + 1) * P],
                                                           xin[:, b, i, k * P:(k + 1) * P], ident[:])
                            last.then_inc(dn_tr, 1)
                        pe.wait_ge(dn_xt, (s + 1) * KC)
                        pe.wait_ge(dn_act, t * 2 + 1)
                        ps = ps_l[:, b]
                        for h in range(TILE_B):
                            for k in range(KC):
                                xv = xta[:, b, k].rearrange("p (i h q) -> p i h q", i=ST, h=TILE_B)
                                last = nc.tensor.matmul(ps[h * A:(h + 1) * A, 0:ST * S], wdown[:, k, :], xv[:, :, h, :],
                                                        start=(k == 0), stop=(k == KC - 1))
                        last.then_inc(dn_mm, 1)

            @block.vector
            def _(dve):
                with dve.Fori(0, NST // 2) as t:
                    for b in range(2):
                        s = t * 2 + b
                        for k in range(KC):
                            dve.wait_ge(dn_tr, s * KC + (k + 1))
                            nc.vector.tensor_copy(xta[:, b, k, :], (ps_s if b == 0 else ps_t)[:, k, :]).then_inc(dn_xt, 1)

            @block.scalar
            def _(act):
                nc.scalar.activation(spare[:, 0:1], cols[:, COLS["down_b"]], ACT.Gelu).then_inc(dn_act, 1)
                with act.Fori(0, NST // 2) as t:
                    for b in range(2):
                        s = t * 2 + b
                        act.wait_ge(dn_mm, s + 1)
                        nc.scalar.activation(gel[:, bass.ds(s, 1), :], ps_l[:, b:b + 1, 0:ST * S], ACT.Gelu,
                                             bias=cols[:, COLS["down_b"]]).then_inc(dn_act, 1)


        fs = [sb(f"fs{i}", [P, H, S]) for i in range(ST)]
        wsel = sb("wsel", [P, ST, A])
        gnow = sb("gnow", [P, ST], I32)
        gcur = sb("gcur", [P, ST * S])
        eh = sb("eh", [P, ST, P])
        tok = sb("tok", [P, ST, D])
        xt = sb("xt", [P, KC, N])
        xres = sb("xres", [P, KC, N])
        qtok = sb("qtok", [P, ST, H, TILE_B, DH])
        ktok = sb("ktok", [P, ST, H, TILE_B, DH])
        qbd = sb("qbd", [P, ST, SLOTS, P])
        kst = sb("kst", [P, ST, SLOTS, S])
        vbd = sb("vbd", [P, ST, H // 2, TILE_B, 2, VW])
        ptr = sb("ptr", [P, 2, H // 2, P])
        ctok = sb("ctok", [P, ST, D])
        ctx_t = sb("ctx_t", [P, KC, N])
        yt = sb("yt", [P, KC, N])
        ptok = sb("ptok", [P, ST, D])
        ht = sb("ht", [P, KC, N])
        tz = sb("tz", [P, 2, 2, N])
        x2 = sb("x2", [P, ST, D])
        swp = sb("swp", [P, ST, D])
        x2t = ht
        pj = sb("pj", [R + 2, N])
        ob = sb("ob", [P, ST, D])
        mx = sb("mx", [P, ST, H])
        rc = sb("rc", [P, 2, H // 2])
        fst, pst = sb("fst", [P, 2, ST, 6]), sb("pst", [P, ST, 6])
        fmv, pmv = sb("fmv", [P, 2, ST, 2]), sb("pmv", [P, ST, 2])
        frs, prs = sb("frs", [P, 2, 2, ST]), sb("prs", [P, 2, ST])
        pooled = sb("pooled", [P, KC, STB])
        h1 = sb("h1", [A, STB])
        h1x = sb("h1x", [A, STB, S])
        gt = sb("gt", [P, ST])
        stren = sb("stren", [P, ST])

        zeroed = sem("zeroed")
        x_in, g_in, o_out = sem("x_in"), sem("g_in"), sem("o_out")
        f_in = [sem(f"f_in{i}") for i in range(ST)]
        T = range(ST)
        front_pe = Done(sem("front_pe"), ["ex", "up0", "up1", "xr0", "xr1", "q0", "q1", "k0", "k1", "v0", "v1",
                                          "qt0", "qt1", "qt2", "qt3", "kt0", "kt1"])
        front_dve = Done(sem("front_dve"), ["ex", "up0", "up1", "stat0", "aggr0", "norm0", "stat1", "aggr1", "norm1",
                                            "xs0", "xs1", "v0", "v1", "qt0", "qt1", "qt2", "qt3", "kt0", "kt1"])
        front_pool = Done(sem("front_pool"), ["gnow", "gcur", "upb", "eps0", "rstd0", "gamma", "beta", "eps1", "rstd1",
                                              "sh0", "sh1"])
        front_act = Done(sem("front_act"), ["q0", "q1", "k0", "k1"])
        att_pe = Done(sem("att_pe"), ["sh0", "sc0", "sh1", "sc1", "ta0", "tb0", "oa0", "ob0", "sh2", "sc2", "ta1", "tb1", "oa1", "ob1",
                                      "sh3", "sc3", "ta2", "tb2", "oa2", "ob2", "ta3", "tb3", "oa3", "ob3", "ct0", "ct1"])
        att_dve = Done(sem("att_dve"), ["add0", "max0", "add1", "max1", "ra0", "ca0", "rb0", "cb0", "add2", "max2",
                                        "ra1", "ca1", "rb1", "cb1", "add3", "max3", "ra2", "ca2", "rb2", "cb2",
                                        "ra3", "ca3", "rb3", "cb3"])
        att_pool = Done(sem("att_pool"), ["xres", "sub0", "sub1", "sub2", "sub3"])
        att_act = Done(sem("att_act"), ["exp0", "exp1", "ta0", "tb0", "exp2", "ta1", "tb1", "exp3", "ta2", "tb2",
                                        "ta3", "tb3", "ct0", "ct1"])
        post_pe = Done(sem("post_pe"), ["wo0", "wo1", "yr0", "yr1", "hr0", "hr1"] + [f"w1_{f}" for f in range(FC)]
                       + ["w2_0", "w2_1", "y2r0", "y2r1", "x2r0", "x2r1", "g1", "proj", "g2", "resp0", "resp1"])
        post_dve = Done(sem("post_dve"), ["wo0", "wo1", "stat", "aggr", "norm", "h0", "h1"]
                        + [f"ff{f}" for f in range(FC)] + ["w2_0", "w2_1", "rot0", "rot1", "pool", "h1x", "str",
                                                           "resp0", "resp1"])
        post_pool = Done(sem("post_pool"), ["eps", "rstd", "x2"])
        post_act = Done(sem("post_act"), ["y0", "y1"] + [f"w1_{f}" for f in range(FC)] + ["x2t0", "x2t1", "h1", "pj", "g2"])

        block = ctx.enter_context(nc.Block())

        def col(name, k=0):
            c = COLS[name].start + k
            return cols[:, c:c + 1]

        def pos(slot, g):
            return g % 2, (g // 2) * SLOTS * S + slot * S

        @block.sync
        def _(sp):
            def bias_load(i, tile):
                sp.dma_start(fs[i][:], a["fside"][bass.ds(tile, 1)].rearrange("o p h k -> (o p) h k")).then_inc(f_in[i], 16)

            def x_load(s):
                sp.dma_start(xin[:, 0], a["x"][bass.ds(s, 1)].rearrange("o p i d -> (o p) i d")).then_inc(x_in, 16)

            def rnd(j, front, att_next, post):
                if front:
                    sp.wait_ge(front_dve.sem, front_dve.at("up1", j))
                    x_load(j + 1)
                for i in T:
                    if att_next:
                        sp.wait_ge(att_pe.sem, att_pe.at(f"tb{i}", j))
                        bias_load(i, (j + 1) * ST + i)
                if post:
                    store(j - 1)

            def store(s):
                sp.wait_ge(post_dve.sem, post_dve.at("resp1", s))
                sp.dma_start(out[bass.ds(s, 1)].rearrange("o p i d -> (o p) i d"), ob[:]).then_inc(o_out, 16)

            x_load(0)
            for i in T:
                bias_load(i, i)
            rnd(0, True, True, False)
            with sp.Fori(1, NST - 1) as j:
                rnd(j, True, True, True)
            rnd(NST - 1, False, False, True)
            store(NST - 1)
            sp.wait_ge(o_out, 16 * (NST + 1))

        @block.tensor
        def _(pe):
            mm, tr = nc.tensor.matmul, nc.tensor.transpose
            user = {}

            def bank(b, done, step, s, j):
                if b in user:
                    last, last_step, back = user[b]
                    pe.wait_ge(last.sem, last.at(last_step, j + back))
                user[b] = (done, step, s - j if isinstance(j, int) else BACK[id(done)])
                return ps_l[:, b]

            BACK = {id(front_dve): 1, id(front_act): 1, id(att_act): 0, id(post_dve): -1, id(post_act): -1}

            def scores(i, s, j):
                if i == 0:
                    pe.wait_ge(front_dve.sem, front_dve.at("kt1", s))
                    prev = ("add3", s - 1)
                else:
                    prev = (f"add{i - 1}", s)
                if not (isinstance(s, int) and s == 0 and i == 0):
                    pe.wait_ge(att_dve.sem, att_dve.at(*prev))
                mv = maskneg[:, bass.ds(s * ST + i, 1), :].to_broadcast([P, SLOTS, S])
                for g2 in range(GRP // 2):
                    for b in range(2):
                        mm(ps_s[:, b, g2 * 256:(g2 + 1) * 256], ident16[:], mv, start=True, stop=False)
                    if g2 == 1:
                        pe.wait_ge(att_pe.sem, att_pe.at(f"sh{i}", s))
                    for slot in range(SLOTS):
                        for b in range(2):
                            g = g2 * 2 + b
                            c = pos(slot, g)[1]
                            last = mm(ps_s[:, b, c:c + S], qbd[32 * g:32 * g + 32, i, slot, :],
                                      kst[32 * g:32 * g + 32, i, slot, :], start=False, stop=(slot == SLOTS - 1))
                    last.then_inc(*att_pe.step(f"{('sh', 'sc')[g2]}{i}"))

            def probs_t(i, s, j):
                pe.wait_ge(att_act.sem, att_act.at(f"exp{i}", s))
                p2 = fs[i][:].rearrange("p (m t) k -> p m (t k)", t=2)
                for b, n in ((0, "ta"), (1, "tb")):
                    if i > 0:
                        pe.wait_ge(att_act.sem, att_act.at(f"{n}{i - 1}", s))
                    elif not (isinstance(s, int) and s == 0):
                        pe.wait_ge(att_act.sem, att_act.at(f"{n}3", s - 1))
                    for m in range(4):
                        last = tr(ps_t[:, b, m * P:(m + 1) * P], p2[:, b * 4 + m, :], ident[:])
                    last.then_inc(*att_pe.step(f"{n}{i}"))

            def context(i, s, j):
                if i == 0:
                    pe.wait_ge(front_dve.sem, front_dve.at("v1", s))
                for b, n, r in ((0, "oa", "a"), (1, "ob", "b")):
                    pe.wait_ge(att_act.sem, att_act.at(f"t{r}{i}", s))
                    if i > 0:
                        pe.wait_ge(att_dve.sem, att_dve.at(f"c{r}{i - 1}", s))
                    elif not (isinstance(s, int) and s == 0):
                        pe.wait_ge(att_dve.sem, att_dve.at(f"c{r}3", s - 1))
                    for m in range(4):
                        w = TILE_B * 2 * VW
                        last = mm(ps_o[:, b, m * w:(m + 1) * w], ptr[:, i % 2, b * 4 + m, :],
                                  vbd[:, i, b * 4 + m], start=True, stop=True)
                    last.then_inc(*att_pe.step(f"{n}{i}"))

            def context_t(s, j):
                for c in range(KC):
                    ps = bank(c, att_act, f"ct{c}", s, j)
                    pe.wait_ge(att_dve.sem, att_dve.at("cb3", s))
                    for i in T:
                        last = tr(ps[:, i * P:(i + 1) * P], ctok[:, i, c * P:(c + 1) * P], ident[:])
                    last.then_inc(*att_pe.step(f"ct{c}"))

            def expert(s, j):
                ps = bank(0, front_dve, "ex", s, j)
                pe.wait_ge(g_in, (s + 1) * (16 * ST))
                pe.wait_ge(front_pool.sem, front_pool.at("gcur", s))
                tr(ps[:, ST * S:ST * S + P], ident[:], ident[:])
                for i in T:
                    for h in range(TILE_B):
                        r = slice(h * A, (h + 1) * A)
                        last = mm(ps[r, i * S:(i + 1) * S], wsel[r, i, :], gcur[r, i * S:(i + 1) * S], start=True, stop=True)
                last.then_inc(*front_pe.step("ex"))

            def up(s, j):
                pe.wait_ge(front_dve.sem, front_dve.at("ex", s))
                for b in range(2):
                    ps = bank(b, front_dve, f"up{b}", s, j)
                    for i in range(2):
                        last = mm(ps[:, i * D:(i + 1) * D], eh[:, 2 * b + i, :], wup[:], start=True, stop=True)
                    last.then_inc(*front_pe.step(f"up{b}"))

            def x_by_feature(s, j):
                pe.wait_ge(front_dve.sem, front_dve.at("norm1", s))
                for c in range(KC):
                    ps = bank(c, front_dve, f"xs{c}", s, j)
                    for i in T:
                        last = tr(ps[:, i * P:(i + 1) * P], tok[:, i, c * P:(c + 1) * P], ident[:])
                    last.then_inc(*front_pe.step(f"xr{c}"))

            def project(name, w, done, s, j):
                pe.wait_ge(front_pool.sem, front_pool.at("sh1", s))
                for b in range(2):
                    ps = bank(b, done, f"{name}{b}", s, j)
                    for i in range(2):
                        for k in range(KC):
                            last = mm(ps[:, i * D:(i + 1) * D], xt[:, k, (2 * b + i) * P:(2 * b + i + 1) * P], w[:, k, :],
                                      start=(k == 0), stop=(k == KC - 1))
                    last.then_inc(*front_pe.step(f"{name}{b}"))

            def queries_t(s, j):
                for i in T:
                    ps = bank(i % 2, front_dve, f"qt{i}", s, j)
                    pe.wait_ge(front_act.sem, front_act.at(f"q{i // 2}", s))
                    for slot in range(SLOTS):
                        last = tr(ps[:, slot * P:(slot + 1) * P],
                                  qtok[:, i, slot * GRP:(slot + 1) * GRP].rearrange("p g h d -> p (g h d)"), ident[:])
                    last.then_inc(*front_pe.step(f"qt{i}"))

            def keys_t(s, j):
                for b in range(2):
                    ps = bank(b, front_dve, f"kt{b}", s, j)
                    pe.wait_ge(front_act.sem, front_act.at(f"k{b}", s))
                    for i in range(2):
                        for slot in range(SLOTS):
                            c = (i * SLOTS + slot) * S
                            last = mm(ps[:, c:c + S], ktok[:, 2 * b + i, slot * GRP:(slot + 1) * GRP].rearrange("p g h d -> p (g h d)"),
                                      fold[:], start=True, stop=True)
                    last.then_inc(*front_pe.step(f"kt{b}"))

            def by_feature(name, w, src, kc, done, out_name, m, s, j):
                ps = bank(m % 2, done, out_name, s, j)
                for k in range(kc):
                    last = mm(ps[:], w[:, k, m * P:(m + 1) * P], src[:, k, :], start=(k == 0), stop=(k == kc - 1))
                last.then_inc(*post_pe.step(name))

            def out_proj(s, j):
                pe.wait_ge(att_act.sem, att_act.at("ct1", s))
                for m in range(KC):
                    by_feature(f"wo{m}", wo, ctx_t, KC, post_dve, f"wo{m}", m, s, j)

            def to_tokens(name, done, out_name, need, s, j):
                pe.wait_ge(post_dve.sem, post_dve.at(need, s))
                for b in range(2):
                    ps = bank(b, done, f"{out_name}{b}", s, j)
                    for i in range(2):
                        for c in range(KC):
                            t = 2 * b + i
                            last = tr(ps[:, (i * KC + c) * P:(i * KC + c + 1) * P], yt[:, c, t * P:(t + 1) * P], ident[:])
                    last.then_inc(*post_pe.step(f"{name}{b}"))

            def to_features(name, src, done, out_name, s, j):
                for c in range(KC):
                    ps = bank(c, done, f"{out_name}{c}", s, j)
                    for i in T:
                        last = tr(ps[:, i * P:(i + 1) * P], src[:, i, c * P:(c + 1) * P], ident[:])
                    last.then_inc(*post_pe.step(f"{name}{c}"))

            def ff1(fr, s, j):
                for f in fr:
                    if f == 0:
                        pe.wait_ge(post_dve.sem, post_dve.at("h1", s))
                    by_feature(f"w1_{f}", w1, ht, KC, post_act, f"w1_{f}", f, s, j)

            def ff2(s, j):
                pe.wait_ge(post_dve.sem, post_dve.at(f"ff{FC - 1}", s))
                for m in range(KC):
                    by_feature(f"w2_{m}", w2, big, FC, post_dve, f"w2_{m}", m, s, j)

            def gate1(s, j):
                ps = bank(0, post_act, "h1", s, j)
                pe.wait_ge(post_dve.sem, post_dve.at("pool", s))
                for k in range(KC):
                    last = mm(ps[0:A, 0:STB], gate_w1[:, k, :], pooled[:, k, :], start=(k == 0), stop=(k == KC - 1))
                last.then_inc(*post_pe.step("g1"))

            def basis_proj(s, j):
                ps = bank(1, post_act, "pj", s, j)
                for k in range(KC):
                    last = mm(ps[0:R, :], basis_p[:, k, :], x2t[:, k, :], start=(k == 0), stop=(k == KC - 1))
                last.then_inc(*post_pe.step("proj"))

            def gate2(s, j):
                ps = bank(0, post_act, "g2", s, j)
                pe.wait_ge(post_dve.sem, post_dve.at("h1x", s))
                hx = h1x[:].rearrange("a b q -> a (b q)")
                for i in T:
                    last = mm(ps[:, i:i + 1], hx[:, i * P:(i + 1) * P], cols[0:A, COLS["gate_w2"]], start=True, stop=True)
                last.then_inc(*post_pe.step("g2"))

            def response(s, j):
                for b in range(2):
                    ps = bank(b, post_dve, f"resp{b}", s, j)
                    pe.wait_ge(post_act.sem, post_act.at("pj", s))
                    for i in range(2):
                        t = 2 * b + i
                        last = mm(ps[:, i * D:(i + 1) * D], pj[:, t * P:(t + 1) * P], resp[:], start=True, stop=True)
                    last.then_inc(*post_pe.step(f"resp{b}"))

            def rnd(j, front, att, post):
                f, p = j + 1, j - 1
                for b, (done, step, back) in user.items():
                    user[b] = done, step, back - 1
                if att: scores(0, j, j)
                if post: out_proj(p, j)
                if att: scores(1, j, j)
                if front: expert(f, j)
                if post: to_tokens("yr", post_act, "y", "wo1", p, j)
                if att: probs_t(0, j, j)
                if front: up(f, j)
                if att: context(0, j, j); scores(2, j, j)
                if post:
                    pe.wait_ge(post_dve.sem, post_dve.at("norm", p))
                    to_features("hr", ptok, post_dve, "h", p, j)
                if att: probs_t(1, j, j)
                if post: ff1(range(0, 4), p, j)
                if att: context(1, j, j); scores(3, j, j)
                if front: x_by_feature(f, j)
                if att: probs_t(2, j, j)
                if post: ff1(range(4, FC), p, j)
                if att: context(2, j, j); probs_t(3, j, j)
                if front: project("q", wq, front_act, f, j); project("k", wk, front_act, f, j)
                if att: context(3, j, j)
                if post: ff2(p, j)
                if front: project("v", wv, front_dve, f, j)
                if att: context_t(j, j)
                if post: to_tokens("y2r", post_dve, "rot", "w2_1", p, j)
                if front: queries_t(f, j)
                if post:
                    pe.wait_ge(post_pool.sem, post_pool.at("x2", p))
                    to_features("x2r", x2, post_act, "x2t", p, j)
                    pe.wait_ge(post_act.sem, post_act.at("x2t1", p))
                    gate1(p, j)
                    basis_proj(p, j)
                    gate2(p, j)
                    response(p, j)
                if front: keys_t(f, j)

            pe.wait_ge(zeroed, 5)
            rnd(-1, True, False, False)
            rnd(0, True, True, False)
            with pe.Fori(1, NST - 1) as j:
                rnd(j, True, True, True)
            rnd(NST - 1, False, True, True)
            rnd(NST, False, False, True)

        @block.vector
        def _(dve):
            v = nc.vector

            def softmax(i, s):
                dve.wait_ge(att_pe.sem, att_pe.at(f"sc{i}", s))
                dve.wait_ge(f_in[i], (s + 1) * 16)
                flat = fs[i][:].rearrange("p h k -> p (h k)")
                v.tensor_tensor(flat, ps_s[:].rearrange("p b n -> p (b n)"), flat, ALU.add).then_inc(*att_dve.step(f"add{i}"))
                dve.wait_ge(att_dve.sem, att_dve.at(f"add{i}", s))
                v.reduce_max(mx[:, i, :], fs[i][:], axis=AX).then_inc(*att_dve.step(f"max{i}"))

            def context(i, s):
                for b, r in ((0, "a"), (1, "b")):
                    dve.wait_ge(att_pe.sem, att_pe.at(f"o{r}{i}", s))
                    o = ps_o[:, b, 0:4 * TILE_B * 2 * VW].rearrange("p (m h t w) -> p m h t w", m=4, h=TILE_B, t=2)
                    for h in range(TILE_B):
                        rows_h = slice(h * S, (h + 1) * S)
                        last = v.reciprocal(rc[rows_h, b, :].rearrange("p (m t) -> p m t", t=2), o[rows_h, :, h, :, DH])
                    last.then_inc(*att_dve.step(f"r{r}{i}"))
                    dve.wait_ge(att_dve.sem, att_dve.at(f"r{r}{i}", s))
                    for h in range(TILE_B):
                        rows_h = slice(h * S, (h + 1) * S)
                        last = v.tensor_tensor(
                            ctok[rows_h, i, b * P:(b + 1) * P].rearrange("p (m t w) -> p m t w", m=4, t=2),
                            o[rows_h, :, h, :, 0:DH],
                            rc[rows_h, b, :].rearrange("p (m t) -> p m t", t=2).unsqueeze(3).to_broadcast([S, 4, 2, DH]), ALU.mult)
                    last.then_inc(*att_dve.step(f"c{r}{i}"))

            def expert(s):
                dve.wait_ge(front_pe.sem, front_pe.at("ex", s))
                for h in range(TILE_B):
                    r = slice(h * A, (h + 1) * A)
                    last = v.tensor_tensor(eh[r, :, h * S:(h + 1) * S], ps_l[r, 0, 0:ST * S].rearrange("p (i q) -> p i q", i=ST),
                                           bias_e[r, bass.ds(s * ST, ST)].unsqueeze(2).to_broadcast([A, ST, S]), ALU.add)
                last.then_inc(*front_dve.step("ex"))

            def up(s):
                dve.wait_ge(front_pool.sem, front_pool.at("upb", s))
                for b in range(2):
                    dve.wait_ge(front_pe.sem, front_pe.at(f"up{b}", s))
                    v.tensor_tensor(tok[:, 2 * b:2 * b + 2, :], ps_l[:, b, :].rearrange("p (i d) -> p i d", i=2),
                                    xin[:, 0, 2 * b:2 * b + 2, :], ALU.add).then_inc(*front_dve.step(f"up{b}"))

            def stats(src, st, mv, done, n, s, need):
                dve.wait_ge(*need)
                for i in T:
                    last = v.bn_stats(st[:, i, :], src[:, i, :])
                last.then_inc(*done.step(f"stat{n}"))
                dve.wait_ge(done.sem, done.at(f"stat{n}", s))
                v.memset(spare[:, 3 + (0 if n == "" else 1 + n):4 + (0 if n == "" else 1 + n)], 0.0)
                for i in T:
                    last = v.bn_aggr(mv[:, i, :], st[:, i, :])
                last.then_inc(*done.step(f"aggr{n}"))

            def norm(src, mv, rs, done, n, pool, s):
                dve.wait_ge(pool.sem, pool.at(f"rstd{n}", s))
                for i in T:
                    last = v.tensor_scalar(src[:, i, :], src[:, i, :], mv[:, i, 0:1], rs[:, i:i + 1], ALU.subtract, ALU.mult)
                last.then_inc(*done.step(f"norm{n}"))

            def modulate(s):
                for c in range(KC):
                    dve.wait_ge(front_pe.sem, front_pe.at(f"xr{c}", s))
                    v.tensor_tensor(xt[:, c, :].rearrange("p (b q) -> p b q", b=STB), ps_l[:, c, :].rearrange("p (b q) -> p b q", b=STB),
                                    scale1[:, c, bass.ds(s * STB, STB)].unsqueeze(2).to_broadcast([P, STB, S]),
                                    ALU.mult).then_inc(*front_dve.step(f"xs{c}"))

            def values(s):
                for b in range(2):
                    dve.wait_ge(front_pe.sem, front_pe.at(f"v{b}", s))
                    ps = ps_l[:, b, :].rearrange("p (i m t w) -> p i m t w", i=2, t=2, w=DH)
                    for h in range(TILE_B):
                        for t in range(2):
                            last = v.tensor_copy(vbd[t * S:(t + 1) * S, 2 * b:2 * b + 2, :, h, t, 0:DH], ps[h * S:(h + 1) * S, :, :, t, :])
                    last.then_inc(*front_dve.step(f"v{b}"))

            def queries(s):
                for i in T:
                    dve.wait_ge(front_pe.sem, front_pe.at(f"qt{i}", s))
                    v.scalar_tensor_tensor(qbd[:, i].rearrange("p s (h q) -> p (s h) q", h=TILE_B),
                                           ps_l[:, i % 2, :].rearrange("p (s q) -> p s q", q=S), 0.25,
                                           cols[:, COLS["bq"]].unsqueeze(2).to_broadcast([P, 2 * SLOTS, S]),
                                           ALU.mult, ALU.add).then_inc(*front_dve.step(f"qt{i}"))

            def keys(s):
                for b in range(2):
                    dve.wait_ge(front_pe.sem, front_pe.at(f"kt{b}", s))
                    v.tensor_tensor(kst[:, 2 * b:2 * b + 2], ps_l[:, b, :].rearrange("p (i s q) -> p i s q", i=2, q=S),
                                    cols[:, COLS["bk"]].unsqueeze(1).unsqueeze(3).to_broadcast([P, 2, SLOTS, S]),
                                    ALU.add).then_inc(*front_dve.step(f"kt{b}"))

            def out_proj(s):
                dve.wait_ge(att_pool.sem, att_pool.at("xres", s))
                for m in range(KC):
                    dve.wait_ge(post_pe.sem, post_pe.at(f"wo{m}", s))
                    v.scalar_tensor_tensor(yt[:, m, :], ps_l[:, m, :], col("bo", m), xres[:, m, :], ALU.add,
                                           ALU.add).then_inc(*post_dve.step(f"wo{m}"))

            def h_t(s):
                for c in range(KC):
                    dve.wait_ge(post_pe.sem, post_pe.at(f"hr{c}", s))
                    v.tensor_scalar(ht[:, c, :], ps_l[:, c, :], col("g2", c), col("beta2", c), ALU.mult,
                                    ALU.add).then_inc(*post_dve.step(f"h{c}"))

            def ff(fr, s):
                for f in fr:
                    dve.wait_ge(post_act.sem, post_act.at(f"w1_{f}", s))
                    v.scalar_tensor_tensor(big[:, f, :], tz[:, f % 2, 0, :], 1.0, tz[:, f % 2, 1, :], ALU.add,
                                           ALU.mult).then_inc(*post_dve.step(f"ff{f}"))

            def ff2(s):
                for m in range(KC):
                    dve.wait_ge(post_pe.sem, post_pe.at(f"w2_{m}", s))
                    v.scalar_tensor_tensor(yt[:, m, :], ps_l[:, m, :], col("b2", m), yt[:, m, :], ALU.add,
                                           ALU.add).then_inc(*post_dve.step(f"w2_{m}"))

            def rotate(s):
                for b in range(2):
                    dve.wait_ge(post_pe.sem, post_pe.at(f"y2r{b}", s))
                    v.tensor_tensor(x2[:, 2 * b:2 * b + 2, :].rearrange("p i (n w) -> p i n w", w=4),
                                    ps_l[:, b, :].rearrange("p (i n w) -> p i n w", i=2, w=4),
                                    rot_c[:, bass.ds(s * ST + 2 * b, 2), :].unsqueeze(2).to_broadcast([P, 2, D // 4, 4]), ALU.mult)
                    for i in range(2):
                        last = v.tensor_tensor(swp[:, 2 * b + i, :].rearrange("p (n r w) -> p n r w", r=2, w=2),
                                               ps_l[:, b, i * D:(i + 1) * D].rearrange("p (n r w) -> p n r w", r=2, w=2)[:, :, :, ::-1],
                                               rot_s[:, bass.ds(s * ST + 2 * b + i, 1), :].rearrange("p o (r w) -> p o r w", r=2)
                                               .to_broadcast([P, D // 4, 2, 2]), ALU.mult)
                    last.then_inc(*post_dve.step(f"rot{b}"))

            def pool(s):
                dve.wait_ge(post_act.sem, post_act.at("x2t1", s))
                v.reduce_sum(pooled[:], x2t[:].rearrange("p k (b q) -> p k b q", q=S), axis=AX).then_inc(*post_dve.step("pool"))

            def strength(s):
                dve.wait_ge(post_act.sem, post_act.at("h1", s))
                v.tensor_copy(h1x[:], h1[:].unsqueeze(2).to_broadcast([A, STB, S])).then_inc(*post_dve.step("h1x"))
                dve.wait_ge(post_act.sem, post_act.at("g2", s))
                v.scalar_tensor_tensor(stren[:], gt[:], 1.0, modh[:, bass.ds(s * ST, ST)], ALU.add,
                                       ALU.mult).then_inc(*post_dve.step("str"))

            def response(s):
                dve.wait_ge(post_dve.sem, post_dve.at("str", s))
                dve.wait_ge(o_out, (s + 1) * 16)
                for b in range(2):
                    dve.wait_ge(post_pe.sem, post_pe.at(f"resp{b}", s))
                    for i in range(2):
                        t = 2 * b + i
                        last = v.scalar_tensor_tensor(ob[:, t, :], ps_l[:, b, i * D:(i + 1) * D], stren[:, t:t + 1], x2[:, t, :],
                                                      ALU.mult, ALU.add)
                    last.then_inc(*post_dve.step(f"resp{b}"))

            def rnd(j, front, att, post):
                f, p = j + 1, j - 1
                if att: softmax(0, j)
                if post: out_proj(p)
                if att: softmax(1, j)
                if front: expert(f)
                if post:
                    stats(ptok, pst, pmv, post_dve, "", p, (post_act.sem, post_act.at("y1", p)))
                if front:
                    up(f)
                    stats(tok, fst[:, 0], fmv[:, 0], front_dve, 0, f, (front_dve.sem, front_dve.at("up1", f)))
                if post: norm(ptok, pmv, prs[:, 1], post_dve, "", post_pool, p)
                if att: context(0, j); softmax(2, j)
                if front: norm(tok, fmv[:, 0], frs[:, 0, 1], front_dve, 0, front_pool, f)
                if post:
                    h_t(p)
                    ff(range(0, 4), p)
                if front:
                    stats(tok, fst[:, 1], fmv[:, 1], front_dve, 1, f, (front_pool.sem, front_pool.at("beta", f)))
                if att: context(1, j); softmax(3, j)
                if front:
                    norm(tok, fmv[:, 1], frs[:, 1, 1], front_dve, 1, front_pool, f)
                    modulate(f)
                if post: ff(range(4, FC), p)
                if att: context(2, j); context(3, j)
                if post: ff2(p)
                if front: values(f)
                if post: rotate(p)
                if front: queries(f)
                if post:
                    pool(p)
                    strength(p)
                    response(p)
                if front: keys(f)

            v.memset(eh[:], 0.0).then_inc(zeroed, 1)
            v.memset(ob[:, 0, 0:1], 0.0).then_inc(o_out, 16)
            v.memset(vbd[:], 0.0).then_inc(zeroed, 1)
            v.memset(pj[:], 1.0)
            v.memset(qtok[:], 0.0)
            v.memset(ktok[:], 0.0).then_inc(zeroed, 1)
            dve.wait_ge(zeroed, 3)
            for h in range(TILE_B):
                for t in range(2):
                    last = v.memset(vbd[t * S:(t + 1) * S, :, :, h, t, DH:VW], 1.0)
            last.then_inc(zeroed, 2)
            dve.wait_ge(zeroed, 5)
            rnd(-1, True, False, False)
            rnd(0, True, True, False)
            with dve.Fori(1, NST - 1) as j:
                rnd(j, True, True, True)
            rnd(NST - 1, False, True, True)
            rnd(NST, False, False, True)

        @block.scalar
        def _(act):
            fn = nc.scalar.activation

            def exp(i, s):
                act.wait_ge(att_pool.sem, att_pool.at(f"sub{i}", s))
                fn(fs[i][:], fs[i][:], ACT.Exp).then_inc(*att_act.step(f"exp{i}"))

            def probs(i, s):
                for b, n in ((0, "ta"), (1, "tb")):
                    act.wait_ge(att_pe.sem, att_pe.at(f"{n}{i}", s))
                    fn(ptr[:, i % 2, b * 4:(b + 1) * 4, :].rearrange("p m q -> p (m q)"), ps_t[:, b, :], ACT.Copy).then_inc(*att_act.step(f"{n}{i}"))

            def context_t(s):
                for c in range(KC):
                    act.wait_ge(att_pe.sem, att_pe.at(f"ct{c}", s))
                    fn(ctx_t[:, c, :], ps_l[:, c, :], ACT.Identity, bias=col("bv", c)).then_inc(*att_act.step(f"ct{c}"))

            def tokens(name, dst, s):
                for b in range(2):
                    act.wait_ge(front_pe.sem, front_pe.at(f"{name}{b}", s))
                    for h in range(TILE_B):
                        r = slice(h * S, (h + 1) * S)
                        last = fn(dst[r, 2 * b:2 * b + 2, :, h, :], ps_l[r, b, :].rearrange("p (i n w) -> p i n w", i=2, w=DH), ACT.Copy)
                    last.then_inc(*front_act.step(f"{name}{b}"))

            def y(s):
                for b in range(2):
                    act.wait_ge(post_pe.sem, post_pe.at(f"yr{b}", s))
                    fn(ptok[:, 2 * b:2 * b + 2, :], ps_l[:, b, :].rearrange("p (i d) -> p i d", i=2), ACT.Copy).then_inc(*post_act.step(f"y{b}"))

            def ff(fr, s):
                for f in fr:
                    act.wait_ge(post_pe.sem, post_pe.at(f"w1_{f}", s))
                    if f >= 2:
                        act.wait_ge(post_dve.sem, post_dve.at(f"ff{f - 2}", s))
                    fn(tz[:, f % 2, 0, :], ps_l[:, f % 2, :], ACT.Tanh, bias=tanh_b1[:, f:f + 1], scale=0.851)
                    fn(tz[:, f % 2, 1, :], ps_l[:, f % 2, :], ACT.Identity, bias=half_b1[:, f:f + 1], scale=0.5).then_inc(*post_act.step(f"w1_{f}"))

            def x2_t(s):
                for c in range(KC):
                    act.wait_ge(post_pe.sem, post_pe.at(f"x2r{c}", s))
                    fn(x2t[:, c, :], ps_l[:, c, :], ACT.Copy).then_inc(*post_act.step(f"x2t{c}"))

            def gate(s):
                act.wait_ge(post_pe.sem, post_pe.at("g1", s))
                fn(h1[:], ps_l[0:A, 0, 0:STB], ACT.Relu, bias=cols[0:A, COLS["gate_b1"]], scale=1.0 / S).then_inc(*post_act.step("h1"))
                act.wait_ge(post_pe.sem, post_pe.at("proj", s))
                fn(pj[0:R, :], ps_l[0:R, 1, :], ACT.Copy).then_inc(*post_act.step("pj"))
                act.wait_ge(post_pe.sem, post_pe.at("g2", s))
                fn(gt[:], ps_l[:, 0, 0:ST], ACT.Tanh, bias=half_gb2[:], scale=0.5).then_inc(*post_act.step("g2"))

            def rnd(j, front, att, post):
                f, p = j + 1, j - 1
                if att: exp(0, j); exp(1, j)
                if post: y(p)
                if att: probs(0, j); exp(2, j); probs(1, j)
                if post: ff(range(0, 4), p)
                if att: exp(3, j); probs(2, j)
                if post: ff(range(4, FC), p)
                if att: probs(3, j)
                if front: tokens("q", qtok, f); tokens("k", ktok, f)
                if att: context_t(j)
                if post: x2_t(p); gate(p)

            act.wait_ge(zeroed, 5)
            rnd(-1, True, False, False)
            rnd(0, True, True, False)
            with act.Fori(1, NST - 1) as j:
                rnd(j, True, True, True)
            rnd(NST - 1, False, True, True)
            rnd(NST, False, False, True)

        @block.gpsimd
        def _(pool):
            gp = nc.gpsimd

            def carry_pool(k):
                gp.tensor_tensor(spare[:, k:k + 1], neghalf[:, 0:1], neghalf[:, 0:1], ALU.mult)

            def gather(s):
                if not (isinstance(s, int) and s == 0):
                    pool.wait_ge(front_pe.sem, front_pe.at("ex", s - 1))
                    carry_pool(0)
                gp.tensor_copy(gnow[:], gidx[:, bass.ds(s * ST, ST)]).then_inc(*front_pool.step("gnow"))
                pool.wait_ge(front_pool.sem, front_pool.at("gnow", s))
                carry_pool(1)
                for i in T:
                    gp.indirect_dma_start(out=wsel[:, i, :], out_offset=None, in_=a["expert_w"],
                                          in_offset=bass.IndirectOffsetOnAxis(ap=gnow[:, i:i + 1], axis=0)
                                          ).then_inc(g_in, 16)
                gp.tensor_copy(gcur[:], gel[:, bass.ds(s, 1), :].rearrange("p o n -> p (o n)")).then_inc(*front_pool.step("gcur"))
                pool.wait_ge(x_in, (s + 1) * 16)
                gp.tensor_tensor(xin[:, 0], xin[:, 0], rows[:, 2:3, :].to_broadcast([P, ST, D]), ALU.add).then_inc(*front_pool.step("upb"))

            def rstd(mv, rs, dve_done, pool_done, n, s):
                pool.wait_ge(dve_done.sem, dve_done.at(f"aggr{n}", s))
                gp.tensor_tensor(rs[:, 0, :], mv[:, :, 1], eps[:], ALU.add).then_inc(*pool_done.step(f"eps{n}"))
                pool.wait_ge(pool_done.sem, pool_done.at(f"eps{n}", s))
                gp.tensor_tensor(rs[:, 1, :], rs[:, 0, :], neghalf[:], ALU.pow).then_inc(*pool_done.step(f"rstd{n}"))

            def affine(s):
                pool.wait_ge(front_dve.sem, front_dve.at("norm0", s))
                gp.tensor_tensor(tok[:], tok[:], rows[:, 0:1, :].to_broadcast([P, ST, D]), ALU.mult).then_inc(*front_pool.step("gamma"))
                pool.wait_ge(front_pool.sem, front_pool.at("gamma", s))
                gp.tensor_tensor(tok[:], tok[:], rows[:, 1:2, :].to_broadcast([P, ST, D]), ALU.add).then_inc(*front_pool.step("beta"))

            def shifts(s):
                for c in range(KC):
                    pool.wait_ge(front_dve.sem, front_dve.at(f"xs{c}", s))
                    xv = xt[:, c, :].rearrange("p (b q) -> p b q", b=STB)
                    gp.tensor_tensor(xv, xv, shift[:, c, bass.ds(s * STB, STB)].unsqueeze(2).to_broadcast([P, STB, S]),
                                     ALU.add).then_inc(*front_pool.step(f"sh{c}"))

            def sub(i, s):
                pool.wait_ge(att_dve.sem, att_dve.at(f"max{i}", s))
                gp.tensor_tensor(fs[i][:], fs[i][:], mx[:, i, :].unsqueeze(2).to_broadcast([P, H, S]),
                                 ALU.subtract).then_inc(*att_pool.step(f"sub{i}"))

            def residual(s):
                if not (isinstance(s, int) and s == 0):
                    pool.wait_ge(post_dve.sem, post_dve.at("wo1", s - 1))
                    carry_pool(2)
                gp.tensor_copy(xres[:], xt[:]).then_inc(*att_pool.step("xres"))

            def x2_sum(s):
                pool.wait_ge(post_dve.sem, post_dve.at("rot1", s))
                gp.tensor_tensor(x2[:], x2[:], swp[:], ALU.add).then_inc(*post_pool.step("x2"))

            def rnd(j, front, att, post):
                f, p = j + 1, j - 1
                if front: gather(f)
                if att: residual(j); sub(0, j); sub(1, j)
                if post: rstd(pmv, prs, post_dve, post_pool, "", p)
                if front: rstd(fmv[:, 0], frs[:, 0], front_dve, front_pool, 0, f)
                if att: sub(2, j)
                if front:
                    affine(f)
                    rstd(fmv[:, 1], frs[:, 1], front_dve, front_pool, 1, f)
                if att: sub(3, j)
                if front: shifts(f)
                if post: x2_sum(p)

            rnd(-1, True, False, False)
            rnd(0, True, True, False)
            with pool.Fori(1, NST - 1) as j:
                rnd(j, True, True, True)
            rnd(NST - 1, False, True, True)
            rnd(NST, False, False, True)


D_RED = 14
D_EMB = 38
D_ORTHO = 50
D_BASIS = 52
GSD = 9


def kernel(x, itok_B_0_15, itok_B_34_63, fside_Bx16xSxS_0, condB_theta, condB_phi, condB_safetyscore, mask_Bx1xSxS_bk0,
           L0_cond_down_W, L0_cond_down_b, L0_cond_up_W, L0_cond_up_b, L0_cond_expert_W, L0_cond_expert_b,
           L0_cond_domain_emb, L0_cond_ln_gamma, L0_cond_ln_beta, L1_cond_W_ada, L1_cond_b_ada, L1_cond_Wq, L1_cond_bq,
           L1_cond_Wk, L1_cond_bk, L1_cond_Wv, L1_cond_bv, L1_cond_Wo, L1_cond_bo, L1_cond_W1, L1_cond_b1, L1_cond_W2,
           L1_cond_b2, L1_cond_g2, L1_cond_beta2, L3_cond_U, L3_cond_V, L3_cond_safety_bias, L3_cond_gate_w1,
           L3_cond_gate_b1, L3_cond_gate_w2, L3_cond_gate_b2, L3_cond_resp_w, L3_cond_resp_b):
    import concourse.bacc as bacc
    from concourse.bass_utils import run_bass_kernel_spmd

    f32 = np.float32
    arr = lambda t: np.asarray(t)
    slots = np.arange(H).reshape(SLOTS, GRP)
    n_of = np.empty((SLOTS, GRP), int)
    for slot in range(SLOTS):
        for g in range(GRP):
            n_of[slot, g] = (g % 2) * (H // 2) + (g // 2) * SLOTS + slot
    order = np.argsort(n_of.ravel())
    block_head = n_of.ravel()
    qk_cols = (block_head[:, None] * DH + np.arange(DH)).ravel()

    def by_slot(vec):
        v = arr(vec).astype(f32)[qk_cols].reshape(SLOTS, GRP, 1, DH)
        return np.broadcast_to(v, (SLOTS, GRP, TILE_B, DH)).transpose(1, 2, 3, 0).reshape(P, SLOTS)

    def chunks(vec):
        return arr(vec).reshape(-1, P).T

    def padded(vec):
        c = np.zeros((P, 1), f32)
        c[:len(vec), 0] = vec
        return c

    bq = np.zeros((GRP, TILE_B, DH, SLOTS, TILE_B), f32)
    bq_rows = by_slot(L1_cond_bq).reshape(GRP, TILE_B, DH, SLOTS)
    for h in range(TILE_B):
        bq[:, h, :, :, h] = bq_rows[:, h]
    half = D // 2
    freq = np.exp(np.arange(half, dtype=f32) * f32(-np.log(10000.0) / (half - 1))).astype(f32)
    parts = {
        "bk": by_slot(L1_cond_bk), "bq": bq.reshape(P, 2 * SLOTS), "bv": chunks(L1_cond_bv), "bo": chunks(L1_cond_bo),
        "b1": chunks(L1_cond_b1), "b2": chunks(L1_cond_b2), "g2": chunks(L1_cond_g2), "beta2": chunks(L1_cond_beta2),
        "b_scale": chunks(arr(L1_cond_b_ada)[:D]), "b_shift": chunks(arr(L1_cond_b_ada)[D:]),
        "gate_b1": padded(arr(L3_cond_gate_b1)), "down_b": np.tile(arr(L0_cond_down_b), TILE_B)[:, None],
        "gate_b2": np.broadcast_to(arr(L3_cond_gate_b2)[None], (P, 1)), "freq": freq[:, None],
        "gate_w2": padded(arr(L3_cond_gate_w2)[0]),
    }
    by_tile = lambda t: np.repeat(arr(t).reshape(NT, TILE_B), S, axis=1).T
    data = {
        "x": arr(x).reshape(NST, ST, P, D).transpose(0, 2, 1, 3),
        "fside": arr(fside_Bx16xSxS_0).reshape(NT, TILE_B, H, S, S).transpose(0, 1, 3, 2, 4).reshape(NT, P, H, S),
        "mask": arr(mask_Bx1xSxS_bk0).reshape(NT, P, S).transpose(1, 0, 2),
        "tstep": np.broadcast_to(arr(itok_B_34_63)[None], (P, B)),
        "tokf": np.stack([by_tile(condB_theta), by_tile(condB_phi), by_tile(condB_safetyscore)], 1),
        "ids_tok": by_tile(itok_B_0_15),
        "ids_row": np.broadcast_to(arr(itok_B_0_15)[None], (E, B)),
        "etab": np.stack([arr(L0_cond_expert_b), arr(L0_cond_domain_emb)], 1),
        "expert_w": np.concatenate([arr(L0_cond_expert_W).transpose(0, 2, 1).reshape(E * A, A), np.eye(A, dtype=f32)]),
        "wdown": arr(L0_cond_down_W).T, "wup": arr(L0_cond_up_W).T,
        "rows": np.broadcast_to(np.stack([arr(L0_cond_ln_gamma), arr(L0_cond_ln_beta), arr(L0_cond_up_b)])[None], (P, 3, D)),
        "wada": arr(L1_cond_W_ada),
        "wq": arr(L1_cond_Wq)[:, qk_cols], "wk": arr(L1_cond_Wk)[:, qk_cols], "wv": arr(L1_cond_Wv), "wo": arr(L1_cond_Wo),
        "w1": arr(L1_cond_W1), "w2": arr(L1_cond_W2),
        "gate_w1": arr(L3_cond_gate_w1).T,
        "resp": np.concatenate([arr(L3_cond_resp_w).T, arr(L3_cond_resp_b)[None], arr(L3_cond_safety_bias)[None]]),
        "uv": np.concatenate([arr(L3_cond_U).T, arr(L3_cond_V).T]),
        "cols": np.concatenate([parts[n] for n in COLS], 1),
    }
    nc = bacc.Bacc("TRN2", target_bir_lowering=False, num_devices=1)
    arrays, args = {}, {}
    for name, t in data.items():
        t = np.ascontiguousarray(t)
        arrays[f"in_{name}"] = t
        args[name] = nc.dram_tensor(f"in_{name}", t.shape, mybir.dt.from_np(t.dtype), kind="ExternalInput").ap()
    out = nc.dram_tensor("out_0", (NST, P, ST, D), F32, kind="ExternalOutput").ap()
    build(nc, args, out)
    r = run_bass_kernel_spmd(nc, [arrays], core_ids=[0])
    got = r.results[0]["out_0"]
    return got.transpose(0, 2, 1, 3).reshape(B, S, D)
```

```python
from contextlib import ExitStack

import numpy as np

import concourse.bass as bass
from concourse import mybir

ALU = mybir.AluOpType
ACT = mybir.ActivationFunctionType
AX = mybir.AxisListType.X
F32 = mybir.dt.float32
BF16 = mybir.dt.bfloat16
I32 = mybir.dt.int32
U8 = mybir.dt.uint8

P = 128
B, S, D = 128, 64, 256
H, DH = 16, 16
A = 64
E = 16
F = 1024
R = 32
KC = D // P
FC = F // P
TILE_B = P // S
NT = B // TILE_B
ST = 4
NST = NT // ST
STB = ST * TILE_B
N = ST * P
SLOTS = 4
GRP = 4
VW = DH + 1
LN_EPS = 1e-5
GS_EPS = 1e-8
MASKED = -1e30
TWO_PI = (6.28125, 1.93500518798828125e-3, 3.0199159819567e-7)
PI_IN = 3.1415925

COLS = {}
_at = 0
for _name, _n in (("bk", SLOTS), ("bq", 2 * SLOTS), ("bv", KC), ("bo", KC), ("b1", FC), ("b2", KC), ("g2", KC),
                  ("beta2", KC), ("b_scale", KC), ("b_shift", KC), ("gate_b1", 1), ("down_b", 1), ("gate_b2", 1),
                  ("freq", 1), ("gate_w2", 1)):
    COLS[_name] = slice(_at, _at + _n)
    _at += _n
NCOL = _at


class Done:

    def __init__(self, sem, steps):
        self.sem, self.steps, self.per, self.next = sem, steps, len(steps), 0

    def at(self, step, rnd):
        return rnd * self.per + (self.steps.index(step) + 1)

    def step(self, step):
        assert self.steps[self.next % self.per] == step, (step, self.steps[self.next % self.per])
        self.next += 1
        return self.sem, 1


def tiles(*names, n=ST):
    return [f"{name}{i}" for i in range(n) for name in names]


def build(nc, a, out):
    ctx = ExitStack()
    with ctx:
        def sb(name, shape, dt=F32):
            return ctx.enter_context(nc.sbuf_tensor(name, shape, dt))

        def sem(name):
            return ctx.enter_context(nc.semaphore(name))

        ps_s = ctx.enter_context(nc.psum_tensor("ps_s", [P, 2, 512], F32))
        ps_o = ctx.enter_context(nc.psum_tensor("ps_o", [P, 2, 512], F32))
        ps_l = ctx.enter_context(nc.psum_tensor("ps_l", [P, 4, 512], F32))

        wq, wk, wv, wo = (sb(n, [P, KC, D]) for n in ("wq", "wk", "wv", "wo"))
        w1 = sb("w1", [P, KC, F])
        w2 = sb("w2", [P, FC, D])
        wdown = sb("wdown", [P, KC, A])
        wup = sb("wup", [P, D])
        gate_w1 = sb("gate_w1", [P, KC, A])
        resp = sb("resp", [R + 2, D])
        basis_p = sb("basis_p", [P, KC, R])
        cols = sb("cols", [P, NCOL])
        rows = sb("rows", [P, 3, D])
        ident = sb("ident", [P, P])
        ident16 = sb("ident16", [P, P], BF16)
        fold = sb("fold", [P, S])
        tanh_b1 = sb("tanh_b1", [P, FC])
        half_b1 = sb("half_b1", [P, FC])
        half_gb2 = sb("half_gb2", [P, 1])
        scale1 = sb("scale1", [P, KC, B])
        shift = sb("shift", [P, KC, B])
        bias_e = sb("bias_e", [P, NT])
        gidx = sb("gidx", [P, NT], I32)
        maskneg = sb("maskneg", [P, NT, S], BF16)
        rot_c = sb("rot_c", [P, NT, 4])
        rot_s = sb("rot_s", [P, NT, 4])
        modh = sb("modh", [P, NT])
        neghalf = sb("neghalf", [P, ST])
        eps = sb("eps", [P, ST])
        spare = sb("spare", [P, 6])
        gel = sb("gel", [P, NST, ST * S])
        xin = sb("xin", [P, 2, ST, D])
        big = sb("big", [P, FC, N])

        gs = ExitStack()
        uv = gs.enter_context(nc.sbuf_tensor("uv", [2 * R, D], F32))
        vcopy = gs.enter_context(nc.sbuf_tensor("vcopy", [R, D], F32))
        basis_t = gs.enter_context(nc.sbuf_tensor("basis_t", [P, KC, D], F32))
        basis_r = gs.enter_context(nc.sbuf_tensor("basis_r", [P, KC, R], F32))
        gmask = gs.enter_context(nc.sbuf_tensor("gmask", [2 * R, P], F32))
        rmod = gs.enter_context(nc.sbuf_tensor("rmod", [2 * R, 1], F32))
        cnt = gs.enter_context(nc.sbuf_tensor("cnt", [2 * R, 1], F32))
        halfs = gs.enter_context(nc.sbuf_tensor("halfs", [2 * R, 1], F32))
        gseps = gs.enter_context(nc.sbuf_tensor("gseps", [2 * R, 1], F32))
        scr = ExitStack()
        with scr, nc.Block() as block:
            def tmp(name, shape, dt=F32):
                return scr.enter_context(nc.sbuf_tensor(name, shape, dt))

            loaded = scr.enter_context(nc.semaphore("loaded"))
            made = scr.enter_context(nc.semaphore("made"))
            dchain = scr.enter_context(nc.semaphore("dchain"))
            pchain = scr.enter_context(nc.semaphore("pchain"))
            achain = scr.enter_context(nc.semaphore("achain"))
            tchain = scr.enter_context(nc.semaphore("tchain"))

            wada = tmp("wada", [P, KC, 2 * D])
            mask8 = tmp("mask8", [P, NT, S], U8)
            ti = tmp("ti", [P, B], I32)
            ang = tmp("ang", [P, 3, B])
            red = tmp("red", [P, 3, B])
            kf = tmp("kf", [P, 3, B])
            ki = tmp("ki", [P, 3, B], I32)
            sc = tmp("sc", [P, 2, 3, B])
            th = tmp("th", [P, 2, B])
            emb = tmp("emb", [P, 2, B])
            tokf = tmp("tokf", [P, 3, NT])
            idi = tmp("idi", [P, NT], I32)
            idf = tmp("idf", [P, 4, NT])
            oi = tmp("oi", [P, 1])
            eri = tmp("eri", [E, B], I32)
            erf_ = tmp("erf", [E, 3, B])
            etab = tmp("etab", [E, 2, A])
            eno = tmp("eno", [E, 1])

            LOADS = 0
            loads = [
                (wq[:], a["wq"].rearrange("(c p) n -> p c n", p=P)), (wk[:], a["wk"].rearrange("(c p) n -> p c n", p=P)),
                (wv[:], a["wv"].rearrange("(c p) n -> p c n", p=P)), (wo[:], a["wo"].rearrange("(c p) n -> p c n", p=P)),
                (w1[:], a["w1"].rearrange("(c p) n -> p c n", p=P)), (w2[:], a["w2"].rearrange("(c p) n -> p c n", p=P)),
                (wdown[:], a["wdown"].rearrange("(c p) n -> p c n", p=P)),
                (gate_w1[:], a["gate_w1"].rearrange("(c p) n -> p c n", p=P)),
                (wada[:], a["wada"].rearrange("(c p) n -> p c n", p=P)),
                (wup[0:A, :], a["wup"]), (wup[A:P, :], a["wup"]), (resp[:], a["resp"]), (cols[:], a["cols"]),
                (rows[:], a["rows"]), (mask8[:], a["mask"]), (uv[:], a["uv"]), (ti[:], a["tstep"]),
                (tokf[:], a["tokf"]), (idi[:], a["ids_tok"]), (eri[:], a["ids_row"]), (etab[:], a["etab"]),
            ]
            LOADS = 16 * len(loads)

            @block.sync
            def _(sp):
                for dst, src in loads:
                    sp.dma_start(dst, src).then_inc(loaded, 16)

            @block.gpsimd
            def _(pool):
                n = [0]

                def link(ins):
                    n[0] += 1
                    ins.then_inc(pchain, 1)
                    pool.wait_ge(pchain, n[0])

                link(nc.gpsimd.memset(ident[:], 0.0))
                link(nc.gpsimd.affine_select(out=ident[:], in_=ident[:], compare_op=ALU.not_equal, fill=1.0, base=0,
                                             pattern=[[-1, P]], channel_multiplier=1))
                link(nc.gpsimd.tensor_copy(ident16[:], ident[:]))
                link(nc.gpsimd.tensor_copy(fold[0:S, :], ident[0:S, 0:S]))
                link(nc.gpsimd.tensor_copy(fold[S:P, :], ident[S:P, S:P]))
                link(nc.gpsimd.memset(gmask[:], 0.0))
                link(nc.gpsimd.memset(gmask[0:R, 0:R], 1.0))
                link(nc.gpsimd.memset(gmask[R:2 * R, R:2 * R], 1.0))
                link(nc.gpsimd.iota(rmod[0:R, :], pattern=[[0, 1]], base=0, channel_multiplier=1,
                                    allow_small_or_imprecise_dtypes=True))
                link(nc.gpsimd.iota(rmod[R:2 * R, :], pattern=[[0, 1]], base=0, channel_multiplier=1,
                                    allow_small_or_imprecise_dtypes=True))
                link(nc.gpsimd.iota(oi[0:A, :], pattern=[[0, 1]], base=0, channel_multiplier=1,
                                    allow_small_or_imprecise_dtypes=True))
                link(nc.gpsimd.iota(oi[A:P, :], pattern=[[0, 1]], base=0, channel_multiplier=1,
                                    allow_small_or_imprecise_dtypes=True))
                link(nc.gpsimd.iota(eno[:], pattern=[[0, 1]], base=0, channel_multiplier=1,
                                    allow_small_or_imprecise_dtypes=True))
                link(nc.gpsimd.memset(cnt[:], 0.0))
                link(nc.gpsimd.memset(neghalf[:], -0.5))
                link(nc.gpsimd.memset(eps[:], LN_EPS))
                link(nc.gpsimd.memset(gseps[:], GS_EPS))
                nc.gpsimd.memset(halfs[:], 0.5).then_inc(made, 1)

            @block.tensor
            def _(pe):
                pe.wait_ge(loaded, LOADS)
                pe.wait_ge(made, 1)
                pe.wait_ge(dchain, D_EMB)
                for m in range(2 * KC):
                    for k in range(KC):
                        last = nc.tensor.matmul(ps_l[:, 0, m * B:(m + 1) * B], wada[:, k, m * P:(m + 1) * P], emb[:, k, :],
                                                start=(k == 0), stop=(k == KC - 1))
                last.then_inc(tchain, 1)
                hot = erf_[:].rearrange("e t (j h) -> e t j h", h=TILE_B)
                for h in range(TILE_B):
                    for t in range(2):
                        last = nc.tensor.matmul(ps_l[h * A:(h + 1) * A, 1, 0:NT], etab[:, t, :], hot[:, t, :, h],
                                                start=(t == 0), stop=(t == 1))
                last.then_inc(tchain, 1)

            @block.scalar
            def _(act):
                act.wait_ge(dchain, D_RED)
                nc.scalar.activation(sc[:, 0], red[:], ACT.Sin).then_inc(achain, 1)
                nc.scalar.activation(sc[:, 1], kf[:], ACT.Sin).then_inc(achain, 1)
                act.wait_ge(achain, 2)
                nc.scalar.activation(th[:], sc[:, :, 0, :], ACT.Tanh, scale=0.5).then_inc(achain, 1)
                nc.scalar.activation(modh[:], tokf[:, 2, :], ACT.Tanh, scale=0.5).then_inc(achain, 1)

            @block.vector
            def _(dve):
                n = [0]

                def link(ins):
                    n[0] += 1
                    ins.then_inc(dchain, 1)
                    dve.wait_ge(dchain, n[0])

                v = nc.vector
                dve.wait_ge(loaded, LOADS)
                dve.wait_ge(made, 1)
                link(v.tensor_scalar(maskneg[:], mask8[:], MASKED, None, ALU.mult))
                link(v.tensor_copy(ang[:, 0, :], ti[:]))
                link(v.tensor_scalar(ang[:, 0, :], ang[:, 0, :], 40.0, cols[:, COLS["freq"]], ALU.mult, ALU.mult))
                link(v.memset(ang[:, 1:3, NT:B], 0.0))
                link(v.tensor_copy(ang[:, 1:3, 0:NT], tokf[:, 0:2, :]))
                link(v.tensor_scalar(kf[:], ang[:], 1.0 / (2.0 * np.pi), None, ALU.mult))
                link(v.tensor_copy(ki[:], kf[:]))
                link(v.tensor_copy(kf[:], ki[:]))
                src = ang
                for part in TWO_PI:
                    link(v.scalar_tensor_tensor(red[:], kf[:], -part, src[:], ALU.mult, ALU.add))
                    src = red
                link(v.tensor_scalar(red[:], red[:], PI_IN, -PI_IN, ALU.min, ALU.max))
                link(v.scalar_tensor_tensor(kf[:], red[:], -1.0, red[:], ALU.mult, ALU.max))
                link(v.tensor_scalar(kf[:], kf[:], -1.0, float(np.pi / 2), ALU.mult, ALU.add))
                assert n[0] == D_RED, n[0]
                dve.wait_ge(achain, 4)
                link(v.tensor_scalar(th[:], th[:], 0.5, 0.5, ALU.mult, ALU.add))
                link(v.tensor_tensor(emb[:], th[:], sc[:, :, 0, :], ALU.mult))
                link(v.tensor_scalar(modh[:], modh[:], 0.25, 0.25, ALU.mult, ALU.add))
                for j, ang_no in ((0, 1), (2, 2)):
                    for q in range(2):
                        link(v.tensor_copy(rot_c[:, :, j + q], sc[:, 1, ang_no, 0:NT]))
                        link(v.tensor_scalar(rot_s[:, :, j + q], sc[:, 0, ang_no, 0:NT], 1.0 if q == 0 else -1.0, None, ALU.mult))
                link(v.tensor_copy(idf[:, 0, :], idi[:]))
                link(v.tensor_scalar(idf[:, 1, :], idf[:, 0, :], 0.0, None, ALU.is_ge))
                link(v.tensor_scalar(idf[:, 2, :], idf[:, 0, :], float(E - 1), None, ALU.is_le))
                link(v.tensor_tensor(idf[:, 1, :], idf[:, 1, :], idf[:, 2, :], ALU.mult))
                link(v.tensor_scalar(idf[:, 0, :], idf[:, 0, :], 0.0, float(E), ALU.max, ALU.min))
                link(v.tensor_scalar(idf[:, 0, :], idf[:, 0, :], float(-E), None, ALU.add))
                link(v.tensor_tensor(idf[:, 0, :], idf[:, 0, :], idf[:, 1, :], ALU.mult))
                link(v.tensor_scalar(idf[:, 0, :], idf[:, 0, :], float(E), float(A), ALU.add, ALU.mult))
                link(v.tensor_scalar(gidx[:], idf[:, 0, :], oi[:], None, ALU.add))
                link(v.tensor_copy(erf_[:, 2, :], eri[:]))
                link(v.tensor_scalar(erf_[:, 0, :], erf_[:, 2, :], eno[:], None, ALU.is_equal))
                link(v.tensor_scalar(erf_[:, 2, :], erf_[:, 2, :], 0.0, float(E - 1), ALU.max, ALU.min))
                link(v.tensor_scalar(erf_[:, 1, :], erf_[:, 2, :], eno[:], None, ALU.is_equal))
                assert n[0] == D_EMB, n[0]
                link(v.tensor_scalar(tanh_b1[:], cols[:, COLS["b1"]], 0.851, None, ALU.mult))
                link(v.tensor_scalar(half_b1[:], cols[:, COLS["b1"]], 0.5, None, ALU.mult))
                link(v.tensor_scalar(half_gb2[:], cols[:, COLS["gate_b2"]], 0.5, None, ALU.mult))
                link(v.tensor_scalar(cols[:, COLS["bq"]], cols[:, COLS["bq"]], 0.25, None, ALU.mult))
                dve.wait_ge(tchain, 2)
                for k in range(KC):
                    link(v.tensor_scalar(scale1[:, k, :], ps_l[:, 0, k * B:(k + 1) * B],
                                         cols[:, COLS["b_scale"].start + k:COLS["b_scale"].start + k + 1], 1.0, ALU.add, ALU.add))
                    link(v.tensor_scalar(shift[:, k, :], ps_l[:, 0, (KC + k) * B:(KC + k + 1) * B],
                                         cols[:, COLS["b_shift"].start + k:COLS["b_shift"].start + k + 1], None, ALU.add))
                link(v.tensor_copy(bias_e[:], ps_l[:, 1, 0:NT]))

        with gs, ExitStack() as scr, nc.Block() as block:
            sel_e = scr.enter_context(nc.sbuf_tensor("sel_e", [2 * R, 1], F32))
            later = scr.enter_context(nc.sbuf_tensor("later", [2 * R, 1], F32))
            sel = scr.enter_context(nc.sbuf_tensor("sel", [2 * R, 2, P], F32))
            sq = scr.enter_context(nc.sbuf_tensor("sq", [2 * R, D], F32))
            pr = scr.enter_context(nc.sbuf_tensor("pr", [2 * R, D], F32))
            g = scr.enter_context(nc.sbuf_tensor("g", [2 * R, 12], F32))
            gs_row = scr.enter_context(nc.semaphore("gs_row"))
            gs_go = scr.enter_context(nc.semaphore("gs_go"))
            gs_sq = scr.enter_context(nc.semaphore("gs_sq"))
            gs_norm = scr.enter_context(nc.semaphore("gs_norm"))
            gs_dve = scr.enter_context(nc.semaphore("gs_dve"))
            gs_mm = scr.enter_context(nc.semaphore("gs_mm"))
            gs_end = scr.enter_context(nc.semaphore("gs_end"))
            GSS = R // NST
            assert GSS == KC
            xta = scr.enter_context(nc.sbuf_tensor("xta", [P, 2, KC, N], F32))
            x_in = [scr.enter_context(nc.semaphore(f"dn_x{b}")) for b in range(2)]
            dn_tr = scr.enter_context(nc.semaphore("dn_tr"))
            dn_xt = scr.enter_context(nc.semaphore("dn_xt"))
            dn_mm = scr.enter_context(nc.semaphore("dn_mm"))
            dn_act = scr.enter_context(nc.semaphore("dn_act"))

            @block.sync
            def _(sp):
                for b in range(2):
                    sp.dma_start(xin[:, b], a["x"][b]).then_inc(x_in[b], 16)
                with sp.Fori(1, NST // 2) as t:
                    for b in range(2):
                        sp.wait_ge(dn_tr, t * (2 * KC) + (b - 1) * KC)
                        sp.dma_start(xin[:, b], a["x"][bass.ds(t * 2 + b, 1)].rearrange("o p i d -> (o p) i d")).then_inc(x_in[b], 16)

            @block.tensor
            def _(pe):
                def rows_out(i, q):
                    pe.wait_ge(gs_go, i + 1)
                    nc.tensor.matmul(ps_o[:, 1, 0:D], sel[:, q, :], uv[:], start=True, stop=True).then_inc(gs_row, 1)
                    nc.tensor.matmul(ps_o[:, 0, 0:D], sel[:, q, :], uv[:], start=True, stop=True).then_inc(gs_row, 1)

                with pe.Fori(0, NST // 2) as t:
                    for b in range(2):
                        s = t * 2 + b
                        rows_out(s * GSS, 0)
                        pe.wait_ge(x_in[b], (t + 1) * 16)
                        for k in range(KC):
                            for i in range(ST):
                                last = nc.tensor.transpose(ps_s[:, k, i * P:(i + 1) * P] if b == 0 else ps_l[:, 2 + k, i * P:(i + 1) * P],
                                                           xin[:, b, i, k * P:(k + 1) * P], ident[:])
                            last.then_inc(dn_tr, 1)
                        rows_out(s * GSS + 1, 1)
                        pe.wait_ge(dn_xt, (s + 1) * KC)
                        pe.wait_ge(dn_act, t * 2 + 1)
                        ps = ps_l[:, b]
                        for h in range(TILE_B):
                            for k in range(KC):
                                xv = xta[:, b, k].rearrange("p (i h q) -> p i h q", i=ST, h=TILE_B)
                                last = nc.tensor.matmul(ps[h * A:(h + 1) * A, 0:ST * S], wdown[:, k, :], xv[:, :, h, :],
                                                        start=(k == 0), stop=(k == KC - 1))
                        last.then_inc(dn_mm, 1)
                pe.wait_ge(gs_end, 3)
                for m in range(KC):
                    nc.tensor.matmul(ps_s[:, 0, m * R:(m + 1) * R], vcopy[:, m * P:(m + 1) * P], uv[0:R, 0:R],
                                     start=True, stop=True)
                for m in range(KC):
                    last = nc.tensor.matmul(ps_s[:, 1, m * D:(m + 1) * D], vcopy[:, m * P:(m + 1) * P], uv[0:R, :],
                                            start=True, stop=True)
                last.then_inc(gs_mm, 1)
                pe.wait_ge(gs_end, 5)
                for m in range(KC):
                    for k in range(KC):
                        last = nc.tensor.matmul(ps_o[:, 0, m * R:(m + 1) * R], basis_t[:, k, m * P:(m + 1) * P],
                                                basis_r[:, k, :], start=(k == 0), stop=(k == KC - 1))
                last.then_inc(gs_mm, 1)

            @block.vector
            def _(dve):
                v = nc.vector

                def pick(q, base):
                    v.tensor_scalar(sel_e[:], rmod[:], cnt[:], None, ALU.is_equal).then_inc(gs_dve, 1)
                    dve.wait_ge(gs_dve, base + 1)
                    v.tensor_scalar(sel[:, q, :], gmask[:], sel_e[:], None, ALU.mult).then_inc(gs_dve, 1)

                pick(0, 0)
                dve.wait_ge(gs_dve, 2)
                v.tensor_scalar(sel_e[:], sel_e[:], 1.0, None, ALU.mult).then_inc(gs_go, 1)
                with dve.Fori(0, NST // 2) as t:
                    for b in range(2):
                        s = t * 2 + b
                        for q in range(GSS):
                            i = s * GSS + q
                            base = i * GSD + 2
                            v.tensor_scalar(later[:], rmod[:], cnt[:], None, ALU.is_gt).then_inc(gs_dve, 1)
                            v.tensor_scalar(cnt[:], cnt[:], 1.0, None, ALU.add).then_inc(gs_dve, 1)
                            dve.wait_ge(gs_dve, base + 2)
                            pick(1 - q, base + 2)
                            if q == 1:
                                for k in range(KC):
                                    dve.wait_ge(dn_tr, s * KC + (k + 1))
                                    v.tensor_copy(xta[:, b, k, :], ps_s[:, k, :] if b == 0 else ps_l[:, 2 + k, :]).then_inc(dn_xt, 1)
                            dve.wait_ge(gs_row, i * 2 + 2)
                            v.tensor_tensor(pr[:], ps_o[0:2 * R, 0, 0:D], uv[:], ALU.mult).then_inc(gs_dve, 1)
                            dve.wait_ge(gs_dve, base + 5)
                            v.reduce_sum(g[:, 3:4], pr[:], axis=AX).then_inc(gs_dve, 1)
                            dve.wait_ge(gs_dve, base + 6)
                            v.tensor_scalar(g[:, 5:6], g[:, 3:4], later[:], -1.0, ALU.mult, ALU.mult).then_inc(gs_dve, 1)
                            dve.wait_ge(gs_norm, i * 2 + 2)
                            v.reciprocal(g[:, 4:5], g[:, 2:3]).then_inc(gs_dve, 1)
                            dve.wait_ge(gs_dve, base + 8)
                            v.tensor_scalar(g[:, 6:7], g[:, 5:6], g[:, 4:5], g[:, 4:5], ALU.mult, ALU.mult).then_inc(gs_dve, 1)
                            dve.wait_ge(gs_dve, base + 9)
                            v.scalar_tensor_tensor(uv[:], ps_o[0:2 * R, 0, 0:D], g[:, 6:7], uv[:], ALU.mult, ALU.add).then_inc(gs_go, 1)
                            dve.wait_ge(gs_go, i + 2)
                dve.wait_ge(gs_norm, 2 * R + 2)
                v.reciprocal(g[:, 11:12], g[:, 10:11]).then_inc(gs_end, 1)
                dve.wait_ge(gs_end, 1)
                v.tensor_scalar(uv[:], uv[:], g[:, 11:12], None, ALU.mult).then_inc(gs_end, 1)
                dve.wait_ge(gs_end, 2)
                v.tensor_copy(vcopy[:], uv[R:2 * R, :]).then_inc(gs_end, 1)
                dve.wait_ge(gs_mm, 1)
                v.tensor_copy(basis_r[:], ps_s[:, 0, 0:KC * R].rearrange("p (k r) -> p k r", k=KC)).then_inc(gs_end, 1)
                v.tensor_copy(basis_t[:], ps_s[:, 1, :].rearrange("p (k d) -> p k d", k=KC)).then_inc(gs_end, 1)
                dve.wait_ge(gs_mm, 2)
                v.tensor_copy(basis_p[:], ps_o[:, 0, 0:KC * R].rearrange("p (k r) -> p k r", k=KC)).then_inc(gs_end, 1)
                dve.wait_ge(gs_end, 6)

            @block.scalar
            def _(act):
                nc.scalar.activation(spare[:, 0:1], cols[:, COLS["down_b"]], ACT.Gelu).then_inc(dn_act, 1)
                with act.Fori(0, NST // 2) as t:
                    for b in range(2):
                        s = t * 2 + b
                        for q in range(GSS):
                            act.wait_ge(gs_row, (s * GSS + q) * 2 + 1)
                            nc.scalar.activation(sq[:], ps_o[0:2 * R, 1, 0:D], ACT.Square, accum_out=g[:, 0:1]).then_inc(gs_sq, 1)
                            if q == GSS - 1:
                                act.wait_ge(dn_mm, s + 1)
                                nc.scalar.activation(gel[:, bass.ds(s, 1), :], ps_l[:, b:b + 1, 0:ST * S], ACT.Gelu,
                                                     bias=cols[:, COLS["down_b"]]).then_inc(dn_act, 1)
                act.wait_ge(gs_go, R + 1)
                nc.scalar.activation(sq[:], uv[:], ACT.Square, accum_out=g[:, 8:9]).then_inc(gs_sq, 1)

            @block.gpsimd
            def _(pool):
                with pool.Fori(0, R) as i:
                    pool.wait_ge(gs_sq, i + 1)
                    nc.gpsimd.tensor_tensor(g[:, 1:2], g[:, 0:1], halfs[:], ALU.pow).then_inc(gs_norm, 1)
                    pool.wait_ge(gs_norm, i * 2 + 1)
                    nc.gpsimd.tensor_tensor(g[:, 2:3], g[:, 1:2], gseps[:], ALU.add).then_inc(gs_norm, 1)
                pool.wait_ge(gs_sq, R + 1)
                nc.gpsimd.tensor_tensor(g[:, 9:10], g[:, 8:9], halfs[:], ALU.pow).then_inc(gs_norm, 1)
                pool.wait_ge(gs_norm, 2 * R + 1)
                nc.gpsimd.tensor_tensor(g[:, 10:11], g[:, 9:10], gseps[:], ALU.add).then_inc(gs_norm, 1)

        fs = [sb(f"fs{i}", [P, H, S]) for i in range(ST)]
        wsel = sb("wsel", [P, ST, A])
        gnow = sb("gnow", [P, ST], I32)
        gcur = sb("gcur", [P, ST * S])
        eh = sb("eh", [P, ST, P])
        tok = sb("tok", [P, ST, D])
        xt = sb("xt", [P, KC, N])
        xres = sb("xres", [P, KC, N])
        qtok = sb("qtok", [P, ST, H, TILE_B, DH])
        ktok = sb("ktok", [P, ST, H, TILE_B, DH])
        qbd = sb("qbd", [P, ST, SLOTS, P])
        kbd = sb("kbd", [P, ST, SLOTS, GRP, S])
        vbd = sb("vbd", [P, ST, H // 2, TILE_B, 2, VW])
        ptr = sb("ptr", [P, 2, H // 2, P])
        ctok = sb("ctok", [P, ST, D])
        ctx_t = sb("ctx_t", [P, KC, N])
        yt = sb("yt", [P, KC, N])
        ptok = sb("ptok", [P, ST, D])
        ht = sb("ht", [P, KC, N])
        tz = sb("tz", [P, 2, 2, N])
        x2 = sb("x2", [P, ST, D])
        swp = big[:, 4:6, :].rearrange("p f (i d) -> p (f i) d", i=2)
        x2t = ht
        pj = sb("pj", [R + 2, N])
        ob = xin[:, 1]
        mx = sb("mx", [P, ST, H])
        rc = sb("rc", [P, 2, H // 2])
        fst, pst = sb("fst", [P, 2, ST, 6]), sb("pst", [P, ST, 6])
        fmv, pmv = sb("fmv", [P, 2, ST, 2]), sb("pmv", [P, ST, 2])
        frs, prs = sb("frs", [P, 2, 2, ST]), sb("prs", [P, 2, ST])
        pooled = sb("pooled", [P, KC, STB])
        h1 = sb("h1", [A, STB])
        h1x = big[0:A, 6, :].rearrange("a (b q) -> a b q", b=STB)
        gt = sb("gt", [P, ST])
        stren = sb("stren", [P, ST])

        zeroed = sem("zeroed")
        x_in, g_in, o_out = sem("x_in"), sem("g_in"), sem("o_out")
        f_in = [sem(f"f_in{i}") for i in range(ST)]
        T = range(ST)
        front_pe = Done(sem("front_pe"), ["ex", "up0", "up1", "xr0", "xr1", "q0", "q1", "k0", "k1", "v0", "v1",
                                          "qt0", "qt1", "qt2", "qt3", "kt0", "kt1"])
        front_dve = Done(sem("front_dve"), ["ex", "up0", "up1", "stat0", "aggr0", "norm0", "stat1", "aggr1", "norm1",
                                            "xs0", "xs1", "v0", "v1", "qt0", "qt1", "qt2", "qt3", "kt0", "kt1"])
        front_pool = Done(sem("front_pool"), ["eps0", "rstd0", "gamma", "beta", "eps1", "rstd1",
                                              "sh0", "sh1"])
        fetch_pool = Done(sem("fetch_pool"), ["gnow", "gcur", "upb"])
        front_act = Done(sem("front_act"), ["q0", "q1", "k0", "k1"])
        att_pe = Done(sem("att_pe"), ["sc0", "sc1", "ta0", "tb0", "sc2", "oa0", "ob0", "ta1", "tb1", "sc3", "oa1", "ob1",
                                      "ta2", "tb2", "oa2", "ob2", "ta3", "tb3", "oa3", "ob3", "ct0", "ct1"])
        att_dve = Done(sem("att_dve"), ["add0", "max0", "add1", "max1", "add2", "max2", "ra0", "ca0", "rb0", "cb0",
                                        "add3", "max3", "ra1", "ca1", "rb1", "cb1", "ra2", "ca2", "rb2", "cb2",
                                        "ra3", "ca3", "rb3", "cb3"])
        att_pool = Done(sem("att_pool"), ["sub0", "sub1", "xres", "sub2", "sub3"])
        att_act = Done(sem("att_act"), ["exp0", "ta0", "tb0", "exp1", "ta1", "tb1", "exp2", "ta2", "tb2", "exp3",
                                        "ta3", "tb3", "ct0", "ct1"])
        post_pe = Done(sem("post_pe"), ["wo0", "wo1", "yr0", "yr1", "hr0", "hr1"] + [f"w1_{f}" for f in range(FC)]
                       + ["w2_0", "w2_1"])
        post_dve = Done(sem("post_dve"), ["wo0", "wo1", "stat", "aggr", "norm", "h0", "h1"]
                        + [f"ff{f}" for f in range(FC)] + ["w2_0", "w2_1"])
        post_pool = Done(sem("post_pool"), ["eps", "rstd"])
        post_act = Done(sem("post_act"), ["y0", "y1"] + [f"w1_{f}" for f in range(FC)])
        rear_pe = Done(sem("rear_pe"), ["y2r0", "y2r1", "x2r0", "x2r1", "proj", "g1", "g2", "resp0", "resp1"])
        rear_dve = Done(sem("rear_dve"), ["rot0", "rot1", "pool", "h1x", "str", "resp0", "resp1"])
        rear_pool = Done(sem("rear_pool"), ["x2"])
        rear_act = Done(sem("rear_act"), ["x2t0", "x2t1", "pj", "h1", "g2"])
        ring = ["y2r0", "y2r1", "wo0", "wo1", "ex", "yr0", "yr1", "x2r0", "x2r1", "up0", "up1", "ta0", "tb0",
                "proj", "g1", "g2", "ta1", "tb1", "hr0", "hr1", "resp0", "resp1", "w1_0", "w1_1", "w1_2", "w1_3",
                "ta2", "tb2", "w1_4", "w1_5", "xr0", "xr1", "w1_6", "w1_7", "ta3", "tb3", "q0", "q1", "k0", "k1",
                "w2_0", "v0", "v1", "qt0", "qt1", "qt2", "qt3", "ct0", "ct1", "kt0", "w2_1", "kt1"]
        assert len(set(ring)) == len(ring) and len(ring) % 4 == 0
        bank_of = {use: i % 4 for i, use in enumerate(ring)}

        def rb(use):
            return ps_l[:, bank_of[use], :]

        block = ctx.enter_context(nc.Block())

        def col(name, k=0):
            c = COLS[name].start + k
            return cols[:, c:c + 1]

        def pos(slot, g):
            return g % 2, (g // 2) * SLOTS * S + slot * S

        @block.sync
        def _(sp):
            def bias_load(i, tile):
                sp.dma_start(fs[i][:], a["fside"][bass.ds(tile, 1)].rearrange("o p h k -> (o p) h k")).then_inc(f_in[i], 16)

            def x_load(s):
                sp.dma_start(xin[:, 0], a["x"][bass.ds(s, 1)].rearrange("o p i d -> (o p) i d")).then_inc(x_in, 16)

            def rnd(j, front, att_next, rear):
                if front:
                    sp.wait_ge(front_dve.sem, front_dve.at("up1", j))
                    x_load(j + 1)
                for i in T:
                    if att_next:
                        sp.wait_ge(att_pe.sem, att_pe.at(f"tb{i}", j))
                        bias_load(i, (j + 1) * ST + i)
                if rear:
                    store(j - 2)

            def store(s):
                sp.wait_ge(rear_dve.sem, rear_dve.at("resp1", s))
                sp.dma_start(out[bass.ds(s, 1)].rearrange("o p i d -> (o p) i d"), ob).then_inc(o_out, 16)

            x_load(0)
            for i in T:
                bias_load(i, i)
            rnd(0, True, True, False)
            rnd(1, True, True, False)
            with sp.Fori(2, NST - 1) as j:
                rnd(j, True, True, True)
            rnd(NST - 1, False, False, True)
            rnd(NST, False, False, True)
            store(NST - 1)
            sp.wait_ge(o_out, 16 * (NST + 1))

        @block.tensor
        def _(pe):
            mm, tr = nc.tensor.matmul, nc.tensor.transpose
            user = {}

            def bank(use, done, step, s, j):
                b = bank_of[use]
                if b in user:
                    last, last_step, back = user[b]
                    pe.wait_ge(last.sem, last.at(last_step, j + back))
                user[b] = (done, step, s - j if isinstance(j, int) else BACK[id(done)])
                return ps_l[:, b]

            BACK = {id(front_dve): 1, id(front_act): 1, id(att_act): 0, id(post_dve): -1, id(post_act): -1,
                    id(rear_dve): -2, id(rear_act): -2}

            def scores(i, s, j):
                if i == 0:
                    pe.wait_ge(front_dve.sem, front_dve.at("kt1", s))
                    prev = ("add3", s - 1)
                else:
                    prev = (f"add{i - 1}", s)
                if not (isinstance(s, int) and s == 0 and i == 0):
                    pe.wait_ge(att_dve.sem, att_dve.at(*prev))
                mv = maskneg[:, bass.ds(s * ST + i, 1), :].to_broadcast([P, H // 2, S])
                for b in range(2):
                    mm(ps_s[:, b, :], ident16[:], mv, start=True, stop=False)
                for slot in range(SLOTS):
                    for b in range(2):
                        last = mm(ps_s[:, b, :].rearrange("p (g s k) -> p g s k", g=2, s=SLOTS)[:, :, slot, :],
                                  qbd[:, i, slot, :], kbd[:, i, slot, b:GRP:2, :],
                                  start=False, stop=(slot == SLOTS - 1))
                last.then_inc(*att_pe.step(f"sc{i}"))

            def probs_t(i, s, j):
                pe.wait_ge(att_act.sem, att_act.at(f"exp{i}", s))
                p2 = fs[i][:].rearrange("p (m t) k -> p m (t k)", t=2)
                for b, n in ((0, "ta"), (1, "tb")):
                    ps = bank(f"{n}{i}", att_act, f"{n}{i}", s, j)
                    for m in range(4):
                        last = tr(ps[:, m * P:(m + 1) * P], p2[:, b * 4 + m, :], ident[:])
                    last.then_inc(*att_pe.step(f"{n}{i}"))

            def context(i, s, j):
                if i == 0:
                    pe.wait_ge(front_dve.sem, front_dve.at("v1", s))
                for b, n, r in ((0, "oa", "a"), (1, "ob", "b")):
                    pe.wait_ge(att_act.sem, att_act.at(f"t{r}{i}", s))
                    if i > 0:
                        pe.wait_ge(att_dve.sem, att_dve.at(f"c{r}{i - 1}", s))
                    elif not (isinstance(s, int) and s == 0):
                        pe.wait_ge(att_dve.sem, att_dve.at(f"c{r}3", s - 1))
                    for m in range(4):
                        w = TILE_B * 2 * VW
                        last = mm(ps_o[:, b, m * w:(m + 1) * w], ptr[:, i % 2, b * 4 + m, :],
                                  vbd[:, i, b * 4 + m], start=True, stop=True)
                    last.then_inc(*att_pe.step(f"{n}{i}"))

            def context_t(s, j):
                for c in range(KC):
                    ps = bank(f"ct{c}", att_act, f"ct{c}", s, j)
                    pe.wait_ge(att_dve.sem, att_dve.at("cb3", s))
                    for i in T:
                        last = tr(ps[:, i * P:(i + 1) * P], ctok[:, i, c * P:(c + 1) * P], ident[:])
                    last.then_inc(*att_pe.step(f"ct{c}"))

            def expert(s, j):
                ps = bank("ex", front_dve, "ex", s, j)
                pe.wait_ge(g_in, (s + 1) * (16 * ST))
                pe.wait_ge(fetch_pool.sem, fetch_pool.at("gcur", s))
                tr(ps[:, ST * S:ST * S + P], ident[:], ident[:])
                for i in T:
                    for h in range(TILE_B):
                        r = slice(h * A, (h + 1) * A)
                        last = mm(ps[r, i * S:(i + 1) * S], wsel[r, i, :], gcur[r, i * S:(i + 1) * S], start=True, stop=True)
                last.then_inc(*front_pe.step("ex"))

            def up(s, j):
                pe.wait_ge(front_dve.sem, front_dve.at("ex", s))
                for b in range(2):
                    ps = bank(f"up{b}", front_dve, f"up{b}", s, j)
                    for i in range(2):
                        last = mm(ps[:, i * D:(i + 1) * D], eh[:, 2 * b + i, :], wup[:], start=True, stop=True)
                    last.then_inc(*front_pe.step(f"up{b}"))

            def x_by_feature(s, j):
                pe.wait_ge(front_dve.sem, front_dve.at("norm1", s))
                for c in range(KC):
                    ps = bank(f"xr{c}", front_dve, f"xs{c}", s, j)
                    for i in T:
                        last = tr(ps[:, i * P:(i + 1) * P], tok[:, i, c * P:(c + 1) * P], ident[:])
                    last.then_inc(*front_pe.step(f"xr{c}"))

            def project(name, w, done, s, j):
                pe.wait_ge(front_pool.sem, front_pool.at("sh1", s))
                for b in range(2):
                    ps = bank(f"{name}{b}", done, f"{name}{b}", s, j)
                    for i in range(2):
                        for k in range(KC):
                            last = mm(ps[:, i * D:(i + 1) * D], xt[:, k, (2 * b + i) * P:(2 * b + i + 1) * P], w[:, k, :],
                                      start=(k == 0), stop=(k == KC - 1))
                    last.then_inc(*front_pe.step(f"{name}{b}"))

            def queries_t(s, j):
                for i in T:
                    ps = bank(f"qt{i}", front_dve, f"qt{i}", s, j)
                    pe.wait_ge(front_act.sem, front_act.at(f"q{i // 2}", s))
                    for slot in range(SLOTS):
                        last = tr(ps[:, slot * P:(slot + 1) * P],
                                  qtok[:, i, slot * GRP:(slot + 1) * GRP].rearrange("p g h d -> p (g h d)"), ident[:])
                    last.then_inc(*front_pe.step(f"qt{i}"))

            def keys_t(b, s, j):
                if True:
                    ps = bank(f"kt{b}", front_dve, f"kt{b}", s, j)
                    pe.wait_ge(front_act.sem, front_act.at(f"k{b}", s))
                    for i in range(2):
                        for slot in range(SLOTS):
                            c = (i * SLOTS + slot) * S
                            last = mm(ps[:, c:c + S], ktok[:, 2 * b + i, slot * GRP:(slot + 1) * GRP].rearrange("p g h d -> p (g h d)"),
                                      fold[:], start=True, stop=True)
                    last.then_inc(*front_pe.step(f"kt{b}"))

            def by_feature(name, w, src, kc, done, out_name, m, s, j):
                ps = bank(name, done, out_name, s, j)
                for k in range(kc):
                    last = mm(ps[:], w[:, k, m * P:(m + 1) * P], src[:, k, :], start=(k == 0), stop=(k == kc - 1))
                last.then_inc(*post_pe.step(name))

            def out_proj(s, j):
                pe.wait_ge(att_act.sem, att_act.at("ct1", s))
                for m in range(KC):
                    by_feature(f"wo{m}", wo, ctx_t, KC, post_dve, f"wo{m}", m, s, j)

            def to_tokens(name, pe_done, done, out_name, need, s, j):
                pe.wait_ge(post_dve.sem, post_dve.at(need, s))
                for b in range(2):
                    ps = bank(f"{name}{b}", done, f"{out_name}{b}", s, j)
                    for i in range(2):
                        for c in range(KC):
                            t = 2 * b + i
                            last = tr(ps[:, (i * KC + c) * P:(i * KC + c + 1) * P], yt[:, c, t * P:(t + 1) * P], ident[:])
                    last.then_inc(*pe_done.step(f"{name}{b}"))

            def to_features(name, src, pe_done, done, out_name, s, j):
                for c in range(KC):
                    ps = bank(f"{name}{c}", done, f"{out_name}{c}", s, j)
                    for i in T:
                        last = tr(ps[:, i * P:(i + 1) * P], src[:, i, c * P:(c + 1) * P], ident[:])
                    last.then_inc(*pe_done.step(f"{name}{c}"))

            def ff1(fr, s, j):
                for f in fr:
                    if f == 0:
                        pe.wait_ge(post_dve.sem, post_dve.at("h1", s))
                    by_feature(f"w1_{f}", w1, ht, KC, post_act, f"w1_{f}", f, s, j)

            def ff2(m, s, j):
                if m == 0:
                    pe.wait_ge(post_dve.sem, post_dve.at(f"ff{FC - 1}", s))
                if True:
                    by_feature(f"w2_{m}", w2, big, FC, post_dve, f"w2_{m}", m, s, j)

            def gate1(s, j):
                ps = bank("g1", rear_act, "h1", s, j)
                pe.wait_ge(rear_dve.sem, rear_dve.at("pool", s))
                for k in range(KC):
                    last = mm(ps[0:A, 0:STB], gate_w1[:, k, :], pooled[:, k, :], start=(k == 0), stop=(k == KC - 1))
                last.then_inc(*rear_pe.step("g1"))

            def basis_proj(s, j):
                ps = bank("proj", rear_act, "pj", s, j)
                for k in range(KC):
                    last = mm(ps[0:R, :], basis_p[:, k, :], x2t[:, k, :], start=(k == 0), stop=(k == KC - 1))
                last.then_inc(*rear_pe.step("proj"))

            def gate2(s, j):
                ps = bank("g2", rear_act, "g2", s, j)
                pe.wait_ge(rear_dve.sem, rear_dve.at("h1x", s))
                hx = h1x.rearrange("a b q -> a (b q)")
                for i in T:
                    last = mm(ps[:, i:i + 1], hx[:, i * P:(i + 1) * P], cols[0:A, COLS["gate_w2"]], start=True, stop=True)
                last.then_inc(*rear_pe.step("g2"))

            def response(s, j):
                for b in range(2):
                    ps = bank(f"resp{b}", rear_dve, f"resp{b}", s, j)
                    pe.wait_ge(rear_act.sem, rear_act.at("pj", s))
                    for i in range(2):
                        t = 2 * b + i
                        last = mm(ps[:, i * D:(i + 1) * D], pj[:, t * P:(t + 1) * P], resp[:], start=True, stop=True)
                    last.then_inc(*rear_pe.step(f"resp{b}"))

            def rnd(j, front, att, post, rear):
                f, p, r = j + 1, j - 1, j - 2
                for b, (done, step, back) in user.items():
                    user[b] = done, step, back - 1
                if rear: to_tokens("y2r", rear_pe, rear_dve, "rot", "w2_1", r, j)
                if post: out_proj(p, j)
                if att: scores(0, j, j)
                if front: expert(f, j)
                if post: to_tokens("yr", post_pe, post_act, "y", "wo1", p, j)
                if att: scores(1, j, j)
                if rear:
                    pe.wait_ge(rear_pool.sem, rear_pool.at("x2", r))
                    to_features("x2r", x2, rear_pe, rear_act, "x2t", r, j)
                if front: up(f, j)
                if att: probs_t(0, j, j)
                if rear:
                    pe.wait_ge(rear_act.sem, rear_act.at("x2t1", r))
                    basis_proj(r, j)
                    gate1(r, j)
                if att: scores(2, j, j); context(0, j, j)
                if rear: gate2(r, j)
                if att: probs_t(1, j, j)
                if post:
                    pe.wait_ge(post_dve.sem, post_dve.at("norm", p))
                    to_features("hr", ptok, post_pe, post_dve, "h", p, j)
                if rear: response(r, j)
                if att: scores(3, j, j); context(1, j, j)
                if post: ff1(range(0, 4), p, j)
                if att: probs_t(2, j, j)
                if post: ff1(range(4, 6), p, j)
                if att: context(2, j, j)
                if front: x_by_feature(f, j)
                if post: ff1(range(6, FC), p, j)
                if att: probs_t(3, j, j)
                if front: project("q", wq, front_act, f, j); project("k", wk, front_act, f, j)
                if att: context(3, j, j)
                if post: ff2(0, p, j)
                if front:
                    project("v", wv, front_dve, f, j)
                    queries_t(f, j)
                if att: context_t(j, j)
                if front: keys_t(0, f, j)
                if post: ff2(1, p, j)
                if front: keys_t(1, f, j)

            pe.wait_ge(zeroed, 6)
            rnd(-1, True, False, False, False)
            rnd(0, True, True, False, False)
            rnd(1, True, True, True, False)
            with pe.Fori(2, NST - 1) as j:
                rnd(j, True, True, True, True)
            rnd(NST - 1, False, True, True, True)
            rnd(NST, False, False, True, True)
            rnd(NST + 1, False, False, False, True)

        @block.vector
        def _(dve):
            v = nc.vector

            def softmax(i, s):
                dve.wait_ge(att_pe.sem, att_pe.at(f"sc{i}", s))
                dve.wait_ge(f_in[i], (s + 1) * 16)
                flat = fs[i][:].rearrange("p h k -> p (h k)")
                v.tensor_tensor(flat, ps_s[:].rearrange("p b n -> p (b n)"), flat, ALU.add).then_inc(*att_dve.step(f"add{i}"))
                dve.wait_ge(att_dve.sem, att_dve.at(f"add{i}", s))
                v.reduce_max(mx[:, i, :], fs[i][:], axis=AX).then_inc(*att_dve.step(f"max{i}"))

            def context(i, s):
                for b, r in ((0, "a"), (1, "b")):
                    dve.wait_ge(att_pe.sem, att_pe.at(f"o{r}{i}", s))
                    o = ps_o[:, b, 0:4 * TILE_B * 2 * VW].rearrange("p (m h t w) -> p m h t w", m=4, h=TILE_B, t=2)
                    for h in range(TILE_B):
                        rows_h = slice(h * S, (h + 1) * S)
                        last = v.reciprocal(rc[rows_h, b, :].rearrange("p (m t) -> p m t", t=2), o[rows_h, :, h, :, DH])
                    last.then_inc(*att_dve.step(f"r{r}{i}"))
                    dve.wait_ge(att_dve.sem, att_dve.at(f"r{r}{i}", s))
                    for h in range(TILE_B):
                        rows_h = slice(h * S, (h + 1) * S)
                        last = v.tensor_tensor(
                            ctok[rows_h, i, b * P:(b + 1) * P].rearrange("p (m t w) -> p m t w", m=4, t=2),
                            o[rows_h, :, h, :, 0:DH],
                            rc[rows_h, b, :].rearrange("p (m t) -> p m t", t=2).unsqueeze(3).to_broadcast([S, 4, 2, DH]), ALU.mult)
                    last.then_inc(*att_dve.step(f"c{r}{i}"))

            def expert(s):
                dve.wait_ge(front_pe.sem, front_pe.at("ex", s))
                for h in range(TILE_B):
                    r = slice(h * A, (h + 1) * A)
                    last = v.tensor_tensor(eh[r, :, h * S:(h + 1) * S], rb("ex")[r, 0:ST * S].rearrange("p (i q) -> p i q", i=ST),
                                           bias_e[r, bass.ds(s * ST, ST)].unsqueeze(2).to_broadcast([A, ST, S]), ALU.add)
                last.then_inc(*front_dve.step("ex"))

            def up(s):
                dve.wait_ge(fetch_pool.sem, fetch_pool.at("upb", s))
                for b in range(2):
                    dve.wait_ge(front_pe.sem, front_pe.at(f"up{b}", s))
                    v.tensor_tensor(tok[:, 2 * b:2 * b + 2, :], rb(f"up{b}").rearrange("p (i d) -> p i d", i=2),
                                    xin[:, 0, 2 * b:2 * b + 2, :], ALU.add).then_inc(*front_dve.step(f"up{b}"))

            def stats(src, st, mv, done, n, s, need):
                dve.wait_ge(*need)
                for i in T:
                    last = v.bn_stats(st[:, i, :], src[:, i, :])
                last.then_inc(*done.step(f"stat{n}"))
                dve.wait_ge(done.sem, done.at(f"stat{n}", s))
                v.memset(spare[:, 3 + (0 if n == "" else 1 + n):4 + (0 if n == "" else 1 + n)], 0.0)
                for i in T:
                    last = v.bn_aggr(mv[:, i, :], st[:, i, :])
                last.then_inc(*done.step(f"aggr{n}"))

            def norm(src, mv, rs, done, n, pool, s):
                dve.wait_ge(pool.sem, pool.at(f"rstd{n}", s))
                for i in T:
                    last = v.tensor_scalar(src[:, i, :], src[:, i, :], mv[:, i, 0:1], rs[:, i:i + 1], ALU.subtract, ALU.mult)
                last.then_inc(*done.step(f"norm{n}"))

            def modulate(s):
                for c in range(KC):
                    dve.wait_ge(front_pe.sem, front_pe.at(f"xr{c}", s))
                    v.tensor_tensor(xt[:, c, :].rearrange("p (b q) -> p b q", b=STB), rb(f"xr{c}").rearrange("p (b q) -> p b q", b=STB),
                                    scale1[:, c, bass.ds(s * STB, STB)].unsqueeze(2).to_broadcast([P, STB, S]),
                                    ALU.mult).then_inc(*front_dve.step(f"xs{c}"))

            def values(s):
                for b in range(2):
                    dve.wait_ge(front_pe.sem, front_pe.at(f"v{b}", s))
                    ps = rb(f"v{b}").rearrange("p (i m t w) -> p i m t w", i=2, t=2, w=DH)
                    for h in range(TILE_B):
                        for t in range(2):
                            last = v.tensor_copy(vbd[t * S:(t + 1) * S, 2 * b:2 * b + 2, :, h, t, 0:DH], ps[h * S:(h + 1) * S, :, :, t, :])
                    last.then_inc(*front_dve.step(f"v{b}"))

            def queries(s):
                for i in T:
                    dve.wait_ge(front_pe.sem, front_pe.at(f"qt{i}", s))
                    v.scalar_tensor_tensor(qbd[:, i].rearrange("p s (h q) -> p (s h) q", h=TILE_B),
                                           rb(f"qt{i}").rearrange("p (s q) -> p s q", q=S), 0.25,
                                           cols[:, COLS["bq"]].unsqueeze(2).to_broadcast([P, 2 * SLOTS, S]),
                                           ALU.mult, ALU.add).then_inc(*front_dve.step(f"qt{i}"))

            def keys(b, s):
                dve.wait_ge(front_pe.sem, front_pe.at(f"kt{b}", s))
                for g in range(GRP):
                    rg = slice(32 * g, 32 * g + 32)
                    last = v.tensor_tensor(kbd[rg, 2 * b:2 * b + 2, :, g, :], rb(f"kt{b}")[rg].rearrange("p (i s q) -> p i s q", i=2, q=S),
                                           cols[rg, COLS["bk"]].unsqueeze(1).unsqueeze(3).to_broadcast([32, 2, SLOTS, S]), ALU.add)
                last.then_inc(*front_dve.step(f"kt{b}"))

            def out_proj(s):
                dve.wait_ge(att_pool.sem, att_pool.at("xres", s))
                for m in range(KC):
                    dve.wait_ge(post_pe.sem, post_pe.at(f"wo{m}", s))
                    v.scalar_tensor_tensor(yt[:, m, :], rb(f"wo{m}"), col("bo", m), xres[:, m, :], ALU.add,
                                           ALU.add).then_inc(*post_dve.step(f"wo{m}"))

            def h_t(s):
                for c in range(KC):
                    dve.wait_ge(post_pe.sem, post_pe.at(f"hr{c}", s))
                    v.tensor_scalar(ht[:, c, :], rb(f"hr{c}"), col("g2", c), col("beta2", c), ALU.mult,
                                    ALU.add).then_inc(*post_dve.step(f"h{c}"))

            def ff(fr, s):
                for f in fr:
                    dve.wait_ge(post_act.sem, post_act.at(f"w1_{f}", s))
                    v.scalar_tensor_tensor(big[:, f, :], tz[:, f % 2, 0, :], 1.0, tz[:, f % 2, 1, :], ALU.add,
                                           ALU.mult).then_inc(*post_dve.step(f"ff{f}"))

            def ff2(m, s):
                dve.wait_ge(post_pe.sem, post_pe.at(f"w2_{m}", s))
                v.scalar_tensor_tensor(yt[:, m, :], rb(f"w2_{m}"), col("b2", m), yt[:, m, :], ALU.add,
                                       ALU.add).then_inc(*post_dve.step(f"w2_{m}"))

            def rotate(s):
                for b in range(2):
                    dve.wait_ge(rear_pe.sem, rear_pe.at(f"y2r{b}", s))
                    v.tensor_tensor(x2[:, 2 * b:2 * b + 2, :].rearrange("p i (n w) -> p i n w", w=4),
                                    rb(f"y2r{b}").rearrange("p (i n w) -> p i n w", i=2, w=4),
                                    rot_c[:, bass.ds(s * ST + 2 * b, 2), :].unsqueeze(2).to_broadcast([P, 2, D // 4, 4]), ALU.mult)
                    for i in range(2):
                        last = v.tensor_tensor(swp[:, 2 * b + i, :].rearrange("p (n r w) -> p n r w", r=2, w=2),
                                               rb(f"y2r{b}")[:, i * D:(i + 1) * D].rearrange("p (n r w) -> p n r w", r=2, w=2)[:, :, :, ::-1],
                                               rot_s[:, bass.ds(s * ST + 2 * b + i, 1), :].rearrange("p o (r w) -> p o r w", r=2)
                                               .to_broadcast([P, D // 4, 2, 2]), ALU.mult)
                    last.then_inc(*rear_dve.step(f"rot{b}"))

            def pool(s):
                dve.wait_ge(rear_act.sem, rear_act.at("x2t1", s))
                v.reduce_sum(pooled[:], x2t[:].rearrange("p k (b q) -> p k b q", q=S), axis=AX).then_inc(*rear_dve.step("pool"))

            def hidden(s):
                dve.wait_ge(rear_act.sem, rear_act.at("h1", s))
                v.tensor_copy(h1x, h1[:].unsqueeze(2).to_broadcast([A, STB, S])).then_inc(*rear_dve.step("h1x"))

            def strength(s):
                dve.wait_ge(rear_act.sem, rear_act.at("g2", s))
                v.scalar_tensor_tensor(stren[:], gt[:], 1.0, modh[:, bass.ds(s * ST, ST)], ALU.add,
                                       ALU.mult).then_inc(*rear_dve.step("str"))

            def response(s):
                dve.wait_ge(rear_dve.sem, rear_dve.at("str", s))
                dve.wait_ge(o_out, (s + 1) * 16)
                for b in range(2):
                    dve.wait_ge(rear_pe.sem, rear_pe.at(f"resp{b}", s))
                    for i in range(2):
                        t = 2 * b + i
                        last = v.scalar_tensor_tensor(ob[:, t, :], rb(f"resp{b}")[:, i * D:(i + 1) * D], stren[:, t:t + 1], x2[:, t, :],
                                                      ALU.mult, ALU.add)
                    last.then_inc(*rear_dve.step(f"resp{b}"))

            def rnd(j, front, att, post, rear):
                f, p, r = j + 1, j - 1, j - 2
                if rear: rotate(r)
                if post: out_proj(p)
                if att: softmax(0, j)
                if front: expert(f)
                if att: softmax(1, j)
                if front: up(f)
                if rear: pool(r)
                if post:
                    stats(ptok, pst, pmv, post_dve, "", p, (post_act.sem, post_act.at("y1", p)))
                if post: norm(ptok, pmv, prs[:, 1], post_dve, "", post_pool, p)
                if rear: hidden(r)
                if att: softmax(2, j)
                if post: h_t(p)
                if front: stats(tok, fst[:, 0], fmv[:, 0], front_dve, 0, f, (front_dve.sem, front_dve.at("up1", f)))
                if att: context(0, j)
                if rear:
                    strength(r)
                    response(r)
                if att: softmax(3, j)
                if front: norm(tok, fmv[:, 0], frs[:, 0, 1], front_dve, 0, front_pool, f)
                if att: context(1, j)
                if post: ff(range(0, 4), p)
                if front:
                    stats(tok, fst[:, 1], fmv[:, 1], front_dve, 1, f, (front_pool.sem, front_pool.at("beta", f)))
                    norm(tok, fmv[:, 1], frs[:, 1, 1], front_dve, 1, front_pool, f)
                if post: ff(range(4, 6), p)
                if att: context(2, j)
                if front: modulate(f)
                if post: ff(range(6, FC), p)
                if att: context(3, j)
                if post: ff2(0, p)
                if front:
                    values(f)
                    queries(f)
                    keys(0, f)
                if post: ff2(1, p)
                if front: keys(1, f)

            v.memset(eh[:], 0.0).then_inc(zeroed, 1)
            v.memset(ob[:, 0, 0:1], 0.0).then_inc(o_out, 16)
            v.memset(vbd[:], 0.0).then_inc(zeroed, 1)
            v.memset(pj[:], 1.0)
            v.memset(qtok[:], 0.0)
            v.memset(kbd[:], 0.0).then_inc(zeroed, 1)
            v.memset(ktok[:], 0.0).then_inc(zeroed, 1)
            dve.wait_ge(zeroed, 4)
            for h in range(TILE_B):
                for t in range(2):
                    last = v.memset(vbd[t * S:(t + 1) * S, :, :, h, t, DH:VW], 1.0)
            last.then_inc(zeroed, 2)
            dve.wait_ge(zeroed, 6)
            rnd(-1, True, False, False, False)
            rnd(0, True, True, False, False)
            rnd(1, True, True, True, False)
            with dve.Fori(2, NST - 1) as j:
                rnd(j, True, True, True, True)
            rnd(NST - 1, False, True, True, True)
            rnd(NST, False, False, True, True)
            rnd(NST + 1, False, False, False, True)

        @block.scalar
        def _(act):
            fn = nc.scalar.activation

            def exp(i, s):
                act.wait_ge(att_pool.sem, att_pool.at(f"sub{i}", s))
                fn(fs[i][:], fs[i][:], ACT.Exp).then_inc(*att_act.step(f"exp{i}"))

            def probs(i, s):
                for b, n in ((0, "ta"), (1, "tb")):
                    act.wait_ge(att_pe.sem, att_pe.at(f"{n}{i}", s))
                    fn(ptr[:, i % 2, b * 4:(b + 1) * 4, :].rearrange("p m q -> p (m q)"), rb(f"{n}{i}"), ACT.Copy).then_inc(*att_act.step(f"{n}{i}"))

            def context_t(s):
                for c in range(KC):
                    act.wait_ge(att_pe.sem, att_pe.at(f"ct{c}", s))
                    fn(ctx_t[:, c, :], rb(f"ct{c}"), ACT.Identity, bias=col("bv", c)).then_inc(*att_act.step(f"ct{c}"))

            def tokens(name, dst, s):
                for b in range(2):
                    act.wait_ge(front_pe.sem, front_pe.at(f"{name}{b}", s))
                    for h in range(TILE_B):
                        r = slice(h * S, (h + 1) * S)
                        last = fn(dst[r, 2 * b:2 * b + 2, :, h, :], rb(f"{name}{b}")[r, :].rearrange("p (i n w) -> p i n w", i=2, w=DH), ACT.Copy)
                    last.then_inc(*front_act.step(f"{name}{b}"))

            def y(s):
                for b in range(2):
                    act.wait_ge(post_pe.sem, post_pe.at(f"yr{b}", s))
                    fn(ptok[:, 2 * b:2 * b + 2, :], rb(f"yr{b}").rearrange("p (i d) -> p i d", i=2), ACT.Copy).then_inc(*post_act.step(f"y{b}"))

            def ff(fr, s):
                for f in fr:
                    act.wait_ge(post_pe.sem, post_pe.at(f"w1_{f}", s))
                    if f >= 2:
                        act.wait_ge(post_dve.sem, post_dve.at(f"ff{f - 2}", s))
                    fn(tz[:, f % 2, 0, :], rb(f"w1_{f}"), ACT.Tanh, bias=tanh_b1[:, f:f + 1], scale=0.851)
                    fn(tz[:, f % 2, 1, :], rb(f"w1_{f}"), ACT.Identity, bias=half_b1[:, f:f + 1], scale=0.5).then_inc(*post_act.step(f"w1_{f}"))

            def x2_t(s):
                for c in range(KC):
                    act.wait_ge(rear_pe.sem, rear_pe.at(f"x2r{c}", s))
                    fn(x2t[:, c, :], rb(f"x2r{c}"), ACT.Copy).then_inc(*rear_act.step(f"x2t{c}"))

            def gate1(s):
                act.wait_ge(rear_pe.sem, rear_pe.at("proj", s))
                fn(pj[0:R, :], rb("proj")[0:R, :], ACT.Copy).then_inc(*rear_act.step("pj"))
                act.wait_ge(rear_pe.sem, rear_pe.at("g1", s))
                fn(h1[:], rb("g1")[0:A, 0:STB], ACT.Relu, bias=cols[0:A, COLS["gate_b1"]], scale=1.0 / S).then_inc(*rear_act.step("h1"))

            def gate2(s):
                act.wait_ge(rear_pe.sem, rear_pe.at("g2", s))
                fn(gt[:], rb("g2")[:, 0:ST], ACT.Tanh, bias=half_gb2[:], scale=0.5).then_inc(*rear_act.step("g2"))

            def rnd(j, front, att, post, rear):
                f, p, r = j + 1, j - 1, j - 2
                if post: y(p)
                if att: exp(0, j)
                if rear: x2_t(r)
                if att: probs(0, j); exp(1, j)
                if rear: gate1(r); gate2(r)
                if att: probs(1, j); exp(2, j)
                if post: ff(range(0, 4), p)
                if att: probs(2, j); exp(3, j)
                if post: ff(range(4, FC), p)
                if att: probs(3, j)
                if front: tokens("q", qtok, f); tokens("k", ktok, f)
                if att: context_t(j)

            act.wait_ge(zeroed, 6)
            rnd(-1, True, False, False, False)
            rnd(0, True, True, False, False)
            rnd(1, True, True, True, False)
            with act.Fori(2, NST - 1) as j:
                rnd(j, True, True, True, True)
            rnd(NST - 1, False, True, True, True)
            rnd(NST, False, False, True, True)
            rnd(NST + 1, False, False, False, True)

        @block.gpsimd
        def _(pool):
            gp = nc.gpsimd

            def carry_pool(k):
                gp.tensor_tensor(spare[:, k:k + 1], neghalf[:, 0:1], neghalf[:, 0:1], ALU.mult)

            def gather(s):
                if not (isinstance(s, int) and s == 0):
                    pool.wait_ge(front_pe.sem, front_pe.at("ex", s - 1))
                    carry_pool(0)
                gp.tensor_copy(gnow[:], gidx[:, bass.ds(s * ST, ST)]).then_inc(*fetch_pool.step("gnow"))
                pool.wait_ge(fetch_pool.sem, fetch_pool.at("gnow", s))
                carry_pool(1)
                for i in T:
                    gp.indirect_dma_start(out=wsel[:, i, :], out_offset=None, in_=a["expert_w"],
                                          in_offset=bass.IndirectOffsetOnAxis(ap=gnow[:, i:i + 1], axis=0)
                                          ).then_inc(g_in, 16)
                gp.tensor_copy(gcur[:], gel[:, bass.ds(s, 1), :].rearrange("p o n -> p (o n)")).then_inc(*fetch_pool.step("gcur"))

            def up_bias(s):
                pool.wait_ge(x_in, (s + 1) * 16)
                gp.tensor_tensor(xin[:, 0], xin[:, 0], rows[:, 2:3, :].to_broadcast([P, ST, D]), ALU.add).then_inc(*fetch_pool.step("upb"))

            def rstd(mv, rs, dve_done, pool_done, n, s):
                pool.wait_ge(dve_done.sem, dve_done.at(f"aggr{n}", s))
                gp.tensor_tensor(rs[:, 0, :], mv[:, :, 1], eps[:], ALU.add).then_inc(*pool_done.step(f"eps{n}"))
                pool.wait_ge(pool_done.sem, pool_done.at(f"eps{n}", s))
                gp.tensor_tensor(rs[:, 1, :], rs[:, 0, :], neghalf[:], ALU.pow).then_inc(*pool_done.step(f"rstd{n}"))

            def affine(s):
                pool.wait_ge(front_dve.sem, front_dve.at("norm0", s))
                gp.tensor_tensor(tok[:], tok[:], rows[:, 0:1, :].to_broadcast([P, ST, D]), ALU.mult).then_inc(*front_pool.step("gamma"))
                pool.wait_ge(front_pool.sem, front_pool.at("gamma", s))
                gp.tensor_tensor(tok[:], tok[:], rows[:, 1:2, :].to_broadcast([P, ST, D]), ALU.add).then_inc(*front_pool.step("beta"))

            def shifts(s):
                for c in range(KC):
                    pool.wait_ge(front_dve.sem, front_dve.at(f"xs{c}", s))
                    xv = xt[:, c, :].rearrange("p (b q) -> p b q", b=STB)
                    gp.tensor_tensor(xv, xv, shift[:, c, bass.ds(s * STB, STB)].unsqueeze(2).to_broadcast([P, STB, S]),
                                     ALU.add).then_inc(*front_pool.step(f"sh{c}"))

            def sub(i, s):
                pool.wait_ge(att_dve.sem, att_dve.at(f"max{i}", s))
                gp.tensor_tensor(fs[i][:], fs[i][:], mx[:, i, :].unsqueeze(2).to_broadcast([P, H, S]),
                                 ALU.subtract).then_inc(*att_pool.step(f"sub{i}"))

            def residual(s):
                if not (isinstance(s, int) and s == 0):
                    pool.wait_ge(post_dve.sem, post_dve.at("wo1", s - 1))
                    carry_pool(2)
                gp.tensor_copy(xres[:], xt[:]).then_inc(*att_pool.step("xres"))

            def x2_sum(s):
                pool.wait_ge(rear_dve.sem, rear_dve.at("rot1", s))
                gp.tensor_tensor(x2[:], x2[:], swp, ALU.add).then_inc(*rear_pool.step("x2"))

            def rnd(j, front, att, post, rear, fetch=True):
                f, p, r = j + 1, j - 1, j - 2
                if rear: x2_sum(r)
                if att: sub(0, j)
                if att: sub(1, j)
                if post: rstd(pmv, prs, post_dve, post_pool, "", p)
                if att: residual(j); sub(2, j)
                if fetch: gather(f + 1)
                if front: rstd(fmv[:, 0], frs[:, 0], front_dve, front_pool, 0, f)
                if att: sub(3, j)
                if front:
                    affine(f)
                    rstd(fmv[:, 1], frs[:, 1], front_dve, front_pool, 1, f)
                    shifts(f)
                if fetch: up_bias(f + 1)

            gather(0)
            up_bias(0)
            rnd(-1, True, False, False, False)
            rnd(0, True, True, False, False)
            rnd(1, True, True, True, False)
            with pool.Fori(2, NST - 2) as j:
                rnd(j, True, True, True, True)
            rnd(NST - 2, True, True, True, True, fetch=False)
            rnd(NST - 1, False, True, True, True, fetch=False)
            rnd(NST, False, False, True, True, fetch=False)
            rnd(NST + 1, False, False, False, True, fetch=False)


D_RED = 14
D_EMB = 38
GSD = 9


def kernel(x, itok_B_0_15, itok_B_34_63, fside_Bx16xSxS_0, condB_theta, condB_phi, condB_safetyscore, mask_Bx1xSxS_bk0,
           L0_cond_down_W, L0_cond_down_b, L0_cond_up_W, L0_cond_up_b, L0_cond_expert_W, L0_cond_expert_b,
           L0_cond_domain_emb, L0_cond_ln_gamma, L0_cond_ln_beta, L1_cond_W_ada, L1_cond_b_ada, L1_cond_Wq, L1_cond_bq,
           L1_cond_Wk, L1_cond_bk, L1_cond_Wv, L1_cond_bv, L1_cond_Wo, L1_cond_bo, L1_cond_W1, L1_cond_b1, L1_cond_W2,
           L1_cond_b2, L1_cond_g2, L1_cond_beta2, L3_cond_U, L3_cond_V, L3_cond_safety_bias, L3_cond_gate_w1,
           L3_cond_gate_b1, L3_cond_gate_w2, L3_cond_gate_b2, L3_cond_resp_w, L3_cond_resp_b):
    import concourse.bacc as bacc
    from concourse.bass_utils import run_bass_kernel_spmd

    f32 = np.float32
    arr = lambda t: np.asarray(t)
    slots = np.arange(H).reshape(SLOTS, GRP)
    n_of = np.empty((SLOTS, GRP), int)
    for slot in range(SLOTS):
        for g in range(GRP):
            n_of[slot, g] = (g % 2) * (H // 2) + (g // 2) * SLOTS + slot
    order = np.argsort(n_of.ravel())
    block_head = n_of.ravel()
    qk_cols = (block_head[:, None] * DH + np.arange(DH)).ravel()

    def by_slot(vec):
        v = arr(vec).astype(f32)[qk_cols].reshape(SLOTS, GRP, 1, DH)
        return np.broadcast_to(v, (SLOTS, GRP, TILE_B, DH)).transpose(1, 2, 3, 0).reshape(P, SLOTS)

    def chunks(vec):
        return arr(vec).reshape(-1, P).T

    def padded(vec):
        c = np.zeros((P, 1), f32)
        c[:len(vec), 0] = vec
        return c

    bq = np.zeros((GRP, TILE_B, DH, SLOTS, TILE_B), f32)
    bq_rows = by_slot(L1_cond_bq).reshape(GRP, TILE_B, DH, SLOTS)
    for h in range(TILE_B):
        bq[:, h, :, :, h] = bq_rows[:, h]
    half = D // 2
    freq = np.exp(np.arange(half, dtype=f32) * f32(-np.log(10000.0) / (half - 1))).astype(f32)
    parts = {
        "bk": by_slot(L1_cond_bk), "bq": bq.reshape(P, 2 * SLOTS), "bv": chunks(L1_cond_bv), "bo": chunks(L1_cond_bo),
        "b1": chunks(L1_cond_b1), "b2": chunks(L1_cond_b2), "g2": chunks(L1_cond_g2), "beta2": chunks(L1_cond_beta2),
        "b_scale": chunks(arr(L1_cond_b_ada)[:D]), "b_shift": chunks(arr(L1_cond_b_ada)[D:]),
        "gate_b1": padded(arr(L3_cond_gate_b1)), "down_b": np.tile(arr(L0_cond_down_b), TILE_B)[:, None],
        "gate_b2": np.broadcast_to(arr(L3_cond_gate_b2)[None], (P, 1)), "freq": freq[:, None],
        "gate_w2": padded(arr(L3_cond_gate_w2)[0]),
    }
    by_tile = lambda t: np.repeat(arr(t).reshape(NT, TILE_B), S, axis=1).T
    data = {
        "x": arr(x).reshape(NST, ST, P, D).transpose(0, 2, 1, 3),
        "fside": arr(fside_Bx16xSxS_0).reshape(NT, TILE_B, H, S, S).transpose(0, 1, 3, 2, 4).reshape(NT, P, H, S),
        "mask": arr(mask_Bx1xSxS_bk0).reshape(NT, P, S).transpose(1, 0, 2),
        "tstep": np.broadcast_to(arr(itok_B_34_63)[None], (P, B)),
        "tokf": np.stack([by_tile(condB_theta), by_tile(condB_phi), by_tile(condB_safetyscore)], 1),
        "ids_tok": by_tile(itok_B_0_15),
        "ids_row": np.broadcast_to(arr(itok_B_0_15)[None], (E, B)),
        "etab": np.stack([arr(L0_cond_expert_b), arr(L0_cond_domain_emb)], 1),
        "expert_w": np.concatenate([arr(L0_cond_expert_W).transpose(0, 2, 1).reshape(E * A, A), np.eye(A, dtype=f32)]),
        "wdown": arr(L0_cond_down_W).T, "wup": arr(L0_cond_up_W).T,
        "rows": np.broadcast_to(np.stack([arr(L0_cond_ln_gamma), arr(L0_cond_ln_beta), arr(L0_cond_up_b)])[None], (P, 3, D)),
        "wada": arr(L1_cond_W_ada),
        "wq": arr(L1_cond_Wq)[:, qk_cols], "wk": arr(L1_cond_Wk)[:, qk_cols], "wv": arr(L1_cond_Wv), "wo": arr(L1_cond_Wo),
        "w1": arr(L1_cond_W1), "w2": arr(L1_cond_W2),
        "gate_w1": arr(L3_cond_gate_w1).T,
        "resp": np.concatenate([arr(L3_cond_resp_w).T, arr(L3_cond_resp_b)[None], arr(L3_cond_safety_bias)[None]]),
        "uv": np.concatenate([arr(L3_cond_U).T, arr(L3_cond_V).T]),
        "cols": np.concatenate([parts[n] for n in COLS], 1),
    }
    nc = bacc.Bacc("TRN2", target_bir_lowering=False, num_devices=1)
    arrays, args = {}, {}
    for name, t in data.items():
        t = np.ascontiguousarray(t)
        arrays[f"in_{name}"] = t
        args[name] = nc.dram_tensor(f"in_{name}", t.shape, mybir.dt.from_np(t.dtype), kind="ExternalInput").ap()
    out = nc.dram_tensor("out_0", (NST, P, ST, D), F32, kind="ExternalOutput").ap()
    build(nc, args, out)
    r = run_bass_kernel_spmd(nc, [arrays], core_ids=[0])
    got = r.results[0]["out_0"]
    return got.transpose(0, 2, 1, 3).reshape(B, S, D)
```

```python
from contextlib import ExitStack

import numpy as np

import concourse.bass as bass
from concourse import mybir

ALU = mybir.AluOpType
ACT = mybir.ActivationFunctionType
AX = mybir.AxisListType.X
F32 = mybir.dt.float32
F32R = mybir.dt.float32r
BF16 = mybir.dt.bfloat16
I32 = mybir.dt.int32
U8 = mybir.dt.uint8

P = 128
B, S, D = 128, 64, 256
H, DH = 16, 16
A = 64
E = 16
F = 1024
R = 32
KC = D // P
FC = F // P
HF = FC // 2
TILE_B = P // S
NT = B // TILE_B
ST = 4
NST = NT // ST
STB = ST * TILE_B
N = ST * P
SLOTS = 4
GRP = 4
VW = DH + 1
LN_EPS = 1e-5
GS_EPS = 1e-8
MASKED = -1e30
TWO_PI = (6.28125, 1.93500518798828125e-3, 3.0199159819567e-7)
PI_IN = 3.1415925

COLS = {}
_at = 0
for _name, _n in (("bk", SLOTS), ("bq", 2 * SLOTS), ("bv", KC), ("bo", KC), ("b1", FC), ("b2", KC), ("g2", KC),
                  ("beta2", KC), ("b_scale", KC), ("b_shift", KC), ("gate_b1", 1), ("down_b", 1), ("gate_b2", 1),
                  ("freq", 1), ("gate_w2", 1)):
    COLS[_name] = slice(_at, _at + _n)
    _at += _n
NCOL = _at


class Done:

    def __init__(self, sem, steps):
        self.sem, self.steps, self.per, self.next = sem, steps, len(steps), 0

    def at(self, step, rnd):
        return rnd * self.per + (self.steps.index(step) + 1)

    def step(self, step):
        assert self.steps[self.next % self.per] == step, (step, self.steps[self.next % self.per])
        self.next += 1
        return self.sem, 1


def tiles(*names, n=ST):
    return [f"{name}{i}" for i in range(n) for name in names]


def build(nc, a, out):
    ctx = ExitStack()
    with ctx:
        def sb(name, shape, dt=F32):
            return ctx.enter_context(nc.sbuf_tensor(name, shape, dt))

        def sem(name):
            return ctx.enter_context(nc.semaphore(name))

        ps_s = ctx.enter_context(nc.psum_tensor("ps_s", [P, 2, 512], F32))
        ps_o = ctx.enter_context(nc.psum_tensor("ps_o", [P, 2, 512], F32))
        ps_l = ctx.enter_context(nc.psum_tensor("ps_l", [P, 4, 512], F32))

        wq, wk, wv = (sb(n, [P, KC, D]) for n in ("wq", "wk", "wv"))
        woh, wol = sb("woh", [P, KC, D], F32R), sb("wol", [P, KC, D], F32R)
        w1h, w1l = sb("w1h", [P, KC, F], F32R), sb("w1l", [P, KC, F], F32R)
        w2h, w2l = sb("w2h", [P, FC, D], F32R), sb("w2l", [P, FC, D], F32R)
        wdown = sb("wdown", [P, KC, A])
        wup = sb("wup", [P, D])
        gate_w1 = sb("gate_w1", [P, KC, A])
        resp = sb("resp", [R + 2, D])
        basis_p = sb("basis_p", [P, KC, R])
        cols = sb("cols", [P, NCOL])
        rows = sb("rows", [P, 3, D])
        ident = sb("ident", [P, P])
        ident16 = sb("ident16", [P, P], BF16)
        fold = sb("fold", [P, S])
        tanh_b1 = sb("tanh_b1", [P, FC])
        half_b1 = sb("half_b1", [P, FC])
        half_gb2 = sb("half_gb2", [P, 1])
        scale1 = sb("scale1", [P, KC, B])
        shift = sb("shift", [P, KC, B])
        bias_e = sb("bias_e", [P, NT])
        gidx = sb("gidx", [P, NT], I32)
        maskneg = sb("maskneg", [P, NT, S], BF16)
        rot_c = sb("rot_c", [P, NT, 4])
        rot_s = sb("rot_s", [P, NT, 4])
        modh = sb("modh", [P, NT])
        neghalf = sb("neghalf", [P, ST])
        eps = sb("eps", [P, ST])
        spare = sb("spare", [P, 6])
        gel = nc.dram_tensor("gel", (NST, P, ST * S), F32, kind="Internal").ap()
        xin = sb("xin", [P, 2, ST, D])

        eh = sb("eh", [P, ST, P])
        qtok = sb("qtok", [P, ST, H, TILE_B, DH])
        ktok = sb("ktok", [P, ST, H, TILE_B, DH])
        kbd = sb("kbd", [P, ST, SLOTS, 2, S])
        vbd = sb("vbd", [P, ST, H // 2, TILE_B, 2, VW])
        pj = sb("pj", [R + 2, N])

        gs = ExitStack()
        uv = gs.enter_context(nc.sbuf_tensor("uv", [2 * R, D], F32))
        vcopy = gs.enter_context(nc.sbuf_tensor("vcopy", [R, D], F32))
        basis_t = gs.enter_context(nc.sbuf_tensor("basis_t", [P, KC, D], F32))
        basis_r = gs.enter_context(nc.sbuf_tensor("basis_r", [P, KC, R], F32))
        gmask = gs.enter_context(nc.sbuf_tensor("gmask", [2 * R, P], F32))
        rmod = gs.enter_context(nc.sbuf_tensor("rmod", [2 * R, 1], F32))
        cnt = gs.enter_context(nc.sbuf_tensor("cnt", [2 * R, 1], F32))
        halfs = gs.enter_context(nc.sbuf_tensor("halfs", [2 * R, 1], F32))
        gseps = gs.enter_context(nc.sbuf_tensor("gseps", [2 * R, 1], F32))
        scr = ExitStack()
        with scr, nc.Block() as block:
            def tmp(name, shape, dt=F32):
                return scr.enter_context(nc.sbuf_tensor(name, shape, dt))

            loaded = scr.enter_context(nc.semaphore("loaded"))
            made = scr.enter_context(nc.semaphore("made"))
            dchain = scr.enter_context(nc.semaphore("dchain"))
            pchain = scr.enter_context(nc.semaphore("pchain"))
            achain = scr.enter_context(nc.semaphore("achain"))
            tchain = scr.enter_context(nc.semaphore("tchain"))
            whigh = scr.enter_context(nc.semaphore("whigh"))

            wo = tmp("wo", [P, KC, D])
            w1 = tmp("w1", [P, KC, F])
            w2 = tmp("w2", [P, FC, D])
            wada = tmp("wada", [P, KC, 2 * D])
            mask8 = tmp("mask8", [P, NT, S], U8)
            ti = tmp("ti", [P, B], I32)
            ang = tmp("ang", [P, 3, B])
            red = tmp("red", [P, 3, B])
            kf = tmp("kf", [P, 3, B])
            ki = tmp("ki", [P, 3, B], I32)
            sc = tmp("sc", [P, 2, 3, B])
            th = tmp("th", [P, 2, B])
            emb = tmp("emb", [P, 2, B])
            tokf = tmp("tokf", [P, 3, NT])
            idi = tmp("idi", [P, NT], I32)
            idf = tmp("idf", [P, 4, NT])
            oi = tmp("oi", [P, 1])
            eri = tmp("eri", [E, B], I32)
            erf_ = tmp("erf", [E, 3, B])
            etab = tmp("etab", [E, 2, A])
            eno = tmp("eno", [E, 1])

            loads = [
                (wq[:], a["wq"].rearrange("(c p) n -> p c n", p=P)), (wk[:], a["wk"].rearrange("(c p) n -> p c n", p=P)),
                (wv[:], a["wv"].rearrange("(c p) n -> p c n", p=P)), (wo[:], a["wo"].rearrange("(c p) n -> p c n", p=P)),
                (w1[:], a["w1"].rearrange("(c p) n -> p c n", p=P)), (w2[:], a["w2"].rearrange("(c p) n -> p c n", p=P)),
                (wdown[:], a["wdown"].rearrange("(c p) n -> p c n", p=P)),
                (gate_w1[:], a["gate_w1"].rearrange("(c p) n -> p c n", p=P)),
                (wada[:], a["wada"].rearrange("(c p) n -> p c n", p=P)),
                (wup[0:A, :], a["wup"]), (wup[A:P, :], a["wup"]), (resp[:], a["resp"]), (cols[:], a["cols"]),
                (rows[:], a["rows"]), (mask8[:], a["mask"]), (uv[:], a["uv"]), (ti[:], a["tstep"]),
                (tokf[:], a["tokf"]), (idi[:], a["ids_tok"]), (eri[:], a["ids_row"]), (etab[:], a["etab"]),
            ]
            LOADS = 16 * len(loads)

            @block.sync
            def _(sp):
                for dst, src in loads:
                    sp.dma_start(dst, src).then_inc(loaded, 16)

            @block.gpsimd
            def _(pool):
                n = [0]

                def link(ins):
                    n[0] += 1
                    ins.then_inc(pchain, 1)
                    pool.wait_ge(pchain, n[0])

                link(nc.gpsimd.memset(ident[:], 0.0))
                link(nc.gpsimd.affine_select(out=ident[:], in_=ident[:], compare_op=ALU.not_equal, fill=1.0, base=0,
                                             pattern=[[-1, P]], channel_multiplier=1))
                link(nc.gpsimd.tensor_copy(ident16[:], ident[:]))
                link(nc.gpsimd.tensor_copy(fold[0:S, :], ident[0:S, 0:S]))
                link(nc.gpsimd.tensor_copy(fold[S:P, :], ident[S:P, S:P]))
                link(nc.gpsimd.memset(gmask[:], 0.0))
                link(nc.gpsimd.memset(gmask[0:R, 0:R], 1.0))
                link(nc.gpsimd.memset(gmask[R:2 * R, R:2 * R], 1.0))
                link(nc.gpsimd.iota(rmod[0:R, :], pattern=[[0, 1]], base=0, channel_multiplier=1,
                                    allow_small_or_imprecise_dtypes=True))
                link(nc.gpsimd.iota(rmod[R:2 * R, :], pattern=[[0, 1]], base=0, channel_multiplier=1,
                                    allow_small_or_imprecise_dtypes=True))
                link(nc.gpsimd.iota(oi[0:A, :], pattern=[[0, 1]], base=0, channel_multiplier=1,
                                    allow_small_or_imprecise_dtypes=True))
                link(nc.gpsimd.iota(oi[A:P, :], pattern=[[0, 1]], base=0, channel_multiplier=1,
                                    allow_small_or_imprecise_dtypes=True))
                link(nc.gpsimd.iota(eno[:], pattern=[[0, 1]], base=0, channel_multiplier=1,
                                    allow_small_or_imprecise_dtypes=True))
                link(nc.gpsimd.memset(cnt[:], 0.0))
                link(nc.gpsimd.memset(neghalf[:], -0.5))
                link(nc.gpsimd.memset(eps[:], LN_EPS))
                link(nc.gpsimd.memset(gseps[:], GS_EPS))
                nc.gpsimd.memset(halfs[:], 0.5).then_inc(made, 1)
                for k, (w, high, low) in enumerate(((wo, woh, wol), (w1, w1h, w1l), (w2, w2h, w2l))):
                    pool.wait_ge(loaded, LOADS)
                    pool.wait_ge(whigh, k + 1)
                    nc.gpsimd.tensor_tensor(low[:], w[:], high[:].bitcast(F32), ALU.subtract)
                for buf in (eh, qtok, ktok, kbd, vbd):
                    nc.gpsimd.memset(buf[:], 0.0)
                link(nc.gpsimd.memset(pj[:], 1.0))
                for h in range(TILE_B):
                    for t in range(2):
                        link(nc.gpsimd.memset(vbd[t * S:(t + 1) * S, :, :, h, t, DH:VW], 1.0))

            @block.tensor
            def _(pe):
                pe.wait_ge(loaded, LOADS)
                pe.wait_ge(made, 1)
                pe.wait_ge(dchain, D_EMB)
                for m in range(2 * KC):
                    for k in range(KC):
                        last = nc.tensor.matmul(ps_l[:, 0, m * B:(m + 1) * B], wada[:, k, m * P:(m + 1) * P], emb[:, k, :],
                                                start=(k == 0), stop=(k == KC - 1))
                last.then_inc(tchain, 1)
                hot = erf_[:].rearrange("e t (j h) -> e t j h", h=TILE_B)
                for h in range(TILE_B):
                    for t in range(2):
                        last = nc.tensor.matmul(ps_l[h * A:(h + 1) * A, 1, 0:NT], etab[:, t, :], hot[:, t, :, h],
                                                start=(t == 0), stop=(t == 1))
                last.then_inc(tchain, 1)

            @block.scalar
            def _(act):
                act.wait_ge(loaded, LOADS)
                nc.scalar.activation(woh[:], wo[:], ACT.Copy).then_inc(whigh, 1)
                nc.scalar.activation(w1h[:], w1[:], ACT.Copy).then_inc(whigh, 1)
                nc.scalar.activation(w2h[:], w2[:], ACT.Copy).then_inc(whigh, 1)
                act.wait_ge(dchain, D_RED)
                nc.scalar.activation(sc[:, 0], red[:], ACT.Sin).then_inc(achain, 1)
                nc.scalar.activation(sc[:, 1], kf[:], ACT.Sin).then_inc(achain, 1)
                act.wait_ge(achain, 2)
                nc.scalar.activation(th[:], sc[:, :, 0, :], ACT.Tanh, scale=0.5).then_inc(achain, 1)
                nc.scalar.activation(modh[:], tokf[:, 2, :], ACT.Tanh, scale=0.5).then_inc(achain, 1)

            @block.vector
            def _(dve):
                n = [0]

                def link(ins):
                    n[0] += 1
                    ins.then_inc(dchain, 1)
                    dve.wait_ge(dchain, n[0])

                v = nc.vector
                dve.wait_ge(loaded, LOADS)
                dve.wait_ge(made, 1)
                link(v.tensor_scalar(maskneg[:], mask8[:], MASKED, None, ALU.mult))
                link(v.tensor_copy(ang[:, 0, :], ti[:]))
                link(v.tensor_scalar(ang[:, 0, :], ang[:, 0, :], 40.0, cols[:, COLS["freq"]], ALU.mult, ALU.mult))
                link(v.memset(ang[:, 1:3, NT:B], 0.0))
                link(v.tensor_copy(ang[:, 1:3, 0:NT], tokf[:, 0:2, :]))
                link(v.tensor_scalar(kf[:], ang[:], 1.0 / (2.0 * np.pi), None, ALU.mult))
                link(v.tensor_copy(ki[:], kf[:]))
                link(v.tensor_copy(kf[:], ki[:]))
                src = ang
                for part in TWO_PI:
                    link(v.scalar_tensor_tensor(red[:], kf[:], -part, src[:], ALU.mult, ALU.add))
                    src = red
                link(v.tensor_scalar(red[:], red[:], PI_IN, -PI_IN, ALU.min, ALU.max))
                link(v.scalar_tensor_tensor(kf[:], red[:], -1.0, red[:], ALU.mult, ALU.max))
                link(v.tensor_scalar(kf[:], kf[:], -1.0, float(np.pi / 2), ALU.mult, ALU.add))
                assert n[0] == D_RED, n[0]
                dve.wait_ge(achain, 4)
                link(v.tensor_scalar(th[:], th[:], 0.5, 0.5, ALU.mult, ALU.add))
                link(v.tensor_tensor(emb[:], th[:], sc[:, :, 0, :], ALU.mult))
                link(v.tensor_scalar(modh[:], modh[:], 0.25, 0.25, ALU.mult, ALU.add))
                for j, ang_no in ((0, 1), (2, 2)):
                    for q in range(2):
                        link(v.tensor_copy(rot_c[:, :, j + q], sc[:, 1, ang_no, 0:NT]))
                        link(v.tensor_scalar(rot_s[:, :, j + q], sc[:, 0, ang_no, 0:NT], 1.0 if q == 0 else -1.0, None, ALU.mult))
                link(v.tensor_copy(idf[:, 0, :], idi[:]))
                link(v.tensor_scalar(idf[:, 1, :], idf[:, 0, :], 0.0, None, ALU.is_ge))
                link(v.tensor_scalar(idf[:, 2, :], idf[:, 0, :], float(E - 1), None, ALU.is_le))
                link(v.tensor_tensor(idf[:, 1, :], idf[:, 1, :], idf[:, 2, :], ALU.mult))
                link(v.tensor_scalar(idf[:, 0, :], idf[:, 0, :], 0.0, float(E), ALU.max, ALU.min))
                link(v.tensor_scalar(idf[:, 0, :], idf[:, 0, :], float(-E), None, ALU.add))
                link(v.tensor_tensor(idf[:, 0, :], idf[:, 0, :], idf[:, 1, :], ALU.mult))
                link(v.tensor_scalar(idf[:, 0, :], idf[:, 0, :], float(E), float(A), ALU.add, ALU.mult))
                link(v.tensor_scalar(gidx[:], idf[:, 0, :], oi[:], None, ALU.add))
                link(v.tensor_copy(erf_[:, 2, :], eri[:]))
                link(v.tensor_scalar(erf_[:, 0, :], erf_[:, 2, :], eno[:], None, ALU.is_equal))
                link(v.tensor_scalar(erf_[:, 2, :], erf_[:, 2, :], 0.0, float(E - 1), ALU.max, ALU.min))
                link(v.tensor_scalar(erf_[:, 1, :], erf_[:, 2, :], eno[:], None, ALU.is_equal))
                assert n[0] == D_EMB, n[0]
                link(v.tensor_scalar(tanh_b1[:], cols[:, COLS["b1"]], 0.851, None, ALU.mult))
                link(v.tensor_scalar(half_b1[:], cols[:, COLS["b1"]], 0.5, None, ALU.mult))
                link(v.tensor_scalar(half_gb2[:], cols[:, COLS["gate_b2"]], 0.5, None, ALU.mult))
                link(v.tensor_scalar(cols[:, COLS["bq"]], cols[:, COLS["bq"]], 0.25, None, ALU.mult))
                dve.wait_ge(tchain, 2)
                for k in range(KC):
                    link(v.tensor_scalar(scale1[:, k, :], ps_l[:, 0, k * B:(k + 1) * B],
                                         cols[:, COLS["b_scale"].start + k:COLS["b_scale"].start + k + 1], 1.0, ALU.add, ALU.add))
                    link(v.tensor_scalar(shift[:, k, :], ps_l[:, 0, (KC + k) * B:(KC + k + 1) * B],
                                         cols[:, COLS["b_shift"].start + k:COLS["b_shift"].start + k + 1], None, ALU.add))
                link(v.tensor_copy(bias_e[:], ps_l[:, 1, 0:NT]))

        with gs, ExitStack() as scr, nc.Block() as block:
            sel_e = scr.enter_context(nc.sbuf_tensor("sel_e", [2 * R, 1], F32))
            later = scr.enter_context(nc.sbuf_tensor("later", [2 * R, 1], F32))
            sel = scr.enter_context(nc.sbuf_tensor("sel", [2 * R, 2, P], F32))
            sq = scr.enter_context(nc.sbuf_tensor("sq", [2 * R, D], F32))
            pr = scr.enter_context(nc.sbuf_tensor("pr", [2 * R, D], F32))
            g = scr.enter_context(nc.sbuf_tensor("g", [2 * R, 12], F32))
            gs_row = scr.enter_context(nc.semaphore("gs_row"))
            gs_go = scr.enter_context(nc.semaphore("gs_go"))
            gs_sq = scr.enter_context(nc.semaphore("gs_sq"))
            gs_norm = scr.enter_context(nc.semaphore("gs_norm"))
            gs_dve = scr.enter_context(nc.semaphore("gs_dve"))
            gs_mm = scr.enter_context(nc.semaphore("gs_mm"))
            gs_end = scr.enter_context(nc.semaphore("gs_end"))
            STEPS = R // NST
            assert STEPS == KC
            xta = scr.enter_context(nc.sbuf_tensor("xta", [P, 2, KC, N], F32))
            gout = scr.enter_context(nc.sbuf_tensor("gout", [P, 2, ST * S], F32))
            gel_out = [scr.enter_context(nc.semaphore(f"gel_out{b}")) for b in range(2)]
            x_in = [scr.enter_context(nc.semaphore(f"dn_x{b}")) for b in range(2)]
            dn_tr = scr.enter_context(nc.semaphore("dn_tr"))
            dn_xt = scr.enter_context(nc.semaphore("dn_xt"))
            dn_mm = scr.enter_context(nc.semaphore("dn_mm"))
            dn_act = scr.enter_context(nc.semaphore("dn_act"))

            @block.sync
            def _(sp):
                def gel_store(s, b):
                    sp.wait_ge(dn_act, s + 2)
                    sp.dma_start(gel[bass.ds(s, 1)].rearrange("o p n -> (o p) n"), gout[:, b, :]).then_inc(gel_out[b], 16)

                for b in range(2):
                    sp.dma_start(xin[:, b], a["x"][b]).then_inc(x_in[b], 16)
                with sp.Fori(1, NST // 2) as t:
                    for b in range(2):
                        sp.wait_ge(dn_tr, t * (2 * KC) + (b - 1) * KC)
                        sp.dma_start(xin[:, b], a["x"][bass.ds(t * 2 + b, 1)].rearrange("o p i d -> (o p) i d")).then_inc(x_in[b], 16)
                        gel_store(t * 2 + (b - 2), b)
                for b in range(2):
                    gel_store(NST - 2 + b, b)
                for b in range(2):
                    sp.wait_ge(gel_out[b], 16 * (NST // 2 + 1))

            @block.tensor
            def _(pe):
                def rows_out(i, q):
                    pe.wait_ge(gs_go, i + 1)
                    nc.tensor.matmul(ps_o[:, 0, 0:D], sel[:, q, :], uv[:], start=True, stop=True).then_inc(gs_row, 1)

                with pe.Fori(0, NST // 2) as t:
                    for b in range(2):
                        s = t * 2 + b
                        rows_out(s * STEPS, 0)
                        pe.wait_ge(x_in[b], (t + 1) * 16)
                        for k in range(KC):
                            for i in range(ST):
                                last = nc.tensor.transpose(ps_s[:, k, i * P:(i + 1) * P] if b == 0 else ps_l[:, 2 + k, i * P:(i + 1) * P],
                                                           xin[:, b, i, k * P:(k + 1) * P], ident[:])
                            last.then_inc(dn_tr, 1)
                        rows_out(s * STEPS + 1, 1)
                        pe.wait_ge(dn_xt, (s + 1) * KC)
                        pe.wait_ge(dn_act, t * 2 + 1)
                        ps = ps_l[:, b]
                        for h in range(TILE_B):
                            for k in range(KC):
                                xv = xta[:, b, k].rearrange("p (i h q) -> p i h q", i=ST, h=TILE_B)
                                last = nc.tensor.matmul(ps[h * A:(h + 1) * A, 0:ST * S], wdown[:, k, :], xv[:, :, h, :],
                                                        start=(k == 0), stop=(k == KC - 1))
                        last.then_inc(dn_mm, 1)
                pe.wait_ge(gs_end, 3)
                for m in range(KC):
                    nc.tensor.matmul(ps_s[:, 0, m * R:(m + 1) * R], vcopy[:, m * P:(m + 1) * P], uv[0:R, 0:R],
                                     start=True, stop=True)
                for m in range(KC):
                    last = nc.tensor.matmul(ps_s[:, 1, m * D:(m + 1) * D], vcopy[:, m * P:(m + 1) * P], uv[0:R, :],
                                            start=True, stop=True)
                last.then_inc(gs_mm, 1)
                pe.wait_ge(gs_end, 5)
                for m in range(KC):
                    for k in range(KC):
                        last = nc.tensor.matmul(ps_o[:, 0, m * R:(m + 1) * R], basis_t[:, k, m * P:(m + 1) * P],
                                                basis_r[:, k, :], start=(k == 0), stop=(k == KC - 1))
                last.then_inc(gs_mm, 1)

            @block.vector
            def _(dve):
                v = nc.vector

                def pick(q, base):
                    v.tensor_scalar(sel_e[:], rmod[:], cnt[:], None, ALU.is_equal).then_inc(gs_dve, 1)
                    dve.wait_ge(gs_dve, base + 1)
                    v.tensor_scalar(sel[:, q, :], gmask[:], sel_e[:], None, ALU.mult).then_inc(gs_dve, 1)

                pick(0, 0)
                dve.wait_ge(gs_dve, 2)
                v.tensor_scalar(sel_e[:], sel_e[:], 1.0, None, ALU.mult).then_inc(gs_go, 1)
                with dve.Fori(0, NST // 2) as t:
                    for b in range(2):
                        s = t * 2 + b
                        for q in range(STEPS):
                            i = s * STEPS + q
                            base = i * GSD + 2
                            v.tensor_scalar(later[:], rmod[:], cnt[:], None, ALU.is_gt).then_inc(gs_dve, 1)
                            v.tensor_scalar(cnt[:], cnt[:], 1.0, None, ALU.add).then_inc(gs_dve, 1)
                            dve.wait_ge(gs_dve, base + 2)
                            pick(1 - q, base + 2)
                            if q == 1:
                                for k in range(KC):
                                    dve.wait_ge(dn_tr, s * KC + (k + 1))
                                    v.tensor_copy(xta[:, b, k, :], ps_s[:, k, :] if b == 0 else ps_l[:, 2 + k, :]).then_inc(dn_xt, 1)
                            dve.wait_ge(gs_sq, i + 1)
                            v.tensor_tensor(pr[:], ps_o[0:2 * R, 0, 0:D], uv[:], ALU.mult).then_inc(gs_dve, 1)
                            dve.wait_ge(gs_dve, base + 5)
                            v.reduce_sum(g[:, 3:4], pr[:], axis=AX).then_inc(gs_dve, 1)
                            dve.wait_ge(gs_dve, base + 6)
                            v.tensor_scalar(g[:, 5:6], g[:, 3:4], later[:], -1.0, ALU.mult, ALU.mult).then_inc(gs_dve, 1)
                            dve.wait_ge(gs_norm, i * 2 + 2)
                            v.reciprocal(g[:, 4:5], g[:, 2:3]).then_inc(gs_dve, 1)
                            dve.wait_ge(gs_dve, base + 8)
                            v.tensor_scalar(g[:, 6:7], g[:, 5:6], g[:, 4:5], g[:, 4:5], ALU.mult, ALU.mult).then_inc(gs_dve, 1)
                            dve.wait_ge(gs_dve, base + 9)
                            v.scalar_tensor_tensor(uv[:], ps_o[0:2 * R, 0, 0:D], g[:, 6:7], uv[:], ALU.mult, ALU.add).then_inc(gs_go, 1)
                            dve.wait_ge(gs_go, i + 2)
                dve.wait_ge(gs_norm, 2 * R + 2)
                v.reciprocal(g[:, 11:12], g[:, 10:11]).then_inc(gs_end, 1)
                dve.wait_ge(gs_end, 1)
                v.tensor_scalar(uv[:], uv[:], g[:, 11:12], None, ALU.mult).then_inc(gs_end, 1)
                dve.wait_ge(gs_end, 2)
                v.tensor_copy(vcopy[:], uv[R:2 * R, :]).then_inc(gs_end, 1)
                dve.wait_ge(gs_mm, 1)
                v.tensor_copy(basis_r[:], ps_s[:, 0, 0:KC * R].rearrange("p (k r) -> p k r", k=KC)).then_inc(gs_end, 1)
                v.tensor_copy(basis_t[:], ps_s[:, 1, :].rearrange("p (k d) -> p k d", k=KC)).then_inc(gs_end, 1)
                dve.wait_ge(gs_mm, 2)
                v.tensor_copy(basis_p[:], ps_o[:, 0, 0:KC * R].rearrange("p (k r) -> p k r", k=KC)).then_inc(gs_end, 1)
                dve.wait_ge(gs_end, 6)

            @block.scalar
            def _(act):
                for b in range(2):
                    nc.scalar.activation(spare[:, 1 + b:2 + b], cols[:, COLS["down_b"]], ACT.Copy).then_inc(gel_out[b], 16)
                nc.scalar.activation(spare[:, 0:1], cols[:, COLS["down_b"]], ACT.Gelu).then_inc(dn_act, 1)
                with act.Fori(0, NST // 2) as t:
                    for b in range(2):
                        s = t * 2 + b
                        for q in range(STEPS):
                            act.wait_ge(gs_row, s * STEPS + (q + 1))
                            nc.scalar.activation(sq[:], ps_o[0:2 * R, 0, 0:D], ACT.Square, accum_out=g[:, 0:1]).then_inc(gs_sq, 1)
                            if q == STEPS - 1:
                                act.wait_ge(dn_mm, s + 1)
                                act.wait_ge(gel_out[b], (t + 1) * 16)
                                nc.scalar.activation(gout[:, b, :], ps_l[:, b, 0:ST * S], ACT.Gelu,
                                                     bias=cols[:, COLS["down_b"]]).then_inc(dn_act, 1)
                act.wait_ge(gs_go, R + 1)
                nc.scalar.activation(sq[:], uv[:], ACT.Square, accum_out=g[:, 8:9]).then_inc(gs_sq, 1)

            @block.gpsimd
            def _(pool):
                with pool.Fori(0, R) as i:
                    pool.wait_ge(gs_sq, i + 1)
                    nc.gpsimd.tensor_tensor(g[:, 1:2], g[:, 0:1], halfs[:], ALU.pow).then_inc(gs_norm, 1)
                    pool.wait_ge(gs_norm, i * 2 + 1)
                    nc.gpsimd.tensor_tensor(g[:, 2:3], g[:, 1:2], gseps[:], ALU.add).then_inc(gs_norm, 1)
                pool.wait_ge(gs_sq, R + 1)
                nc.gpsimd.tensor_tensor(g[:, 9:10], g[:, 8:9], halfs[:], ALU.pow).then_inc(gs_norm, 1)
                pool.wait_ge(gs_norm, 2 * R + 1)
                nc.gpsimd.tensor_tensor(g[:, 10:11], g[:, 9:10], gseps[:], ALU.add).then_inc(gs_norm, 1)

        fs = [sb(f"fs{i}", [P, H, S]) for i in range(ST)]
        wsel = sb("wsel", [P, ST, A])
        gnow = sb("gnow", [P, ST], I32)
        gcur = sb("gcur", [P, ST * S])
        tok = sb("tok", [P, ST, D])
        xt = sb("xt", [P, KC, N])
        xres = sb("xres", [P, KC, N])
        qbd = sb("qbd", [P, ST, SLOTS, P])
        ptr = sb("ptr", [P, 2, H // 2, P])
        ctok = sb("ctok", [P, ST, D])
        yt = sb("yt", [P, KC, N])
        ht = sb("ht", [P, KC, N])
        hh, hl = sb("hh", [P, KC, N], F32R), sb("hl", [P, KC, N], F32R)
        bigh, bigl = sb("bigh", [P, HF, N], F32R), sb("bigl", [P, HF, N], F32R)
        tz = sb("tz", [P, 2, 2, N])
        x2 = sb("x2", [P, ST, D])
        swp = tz[:, 0].rearrange("p f (i d) -> p (f i) d", i=2)
        x2t = ht
        ctx_h, ctx_l = hh, hl
        ptok = ctok
        ob = xin[:, 1]
        mx = sb("mx", [P, ST, H])
        rc = sb("rc", [P, 2, H // 2])
        fst, pst = sb("fst", [P, 2, ST, 6]), sb("pst", [P, ST, 6])
        fmv, pmv = sb("fmv", [P, 2, ST, 2]), sb("pmv", [P, ST, 2])
        frs, prs = sb("frs", [P, 2, 2, ST]), sb("prs", [P, 2, ST])
        pooled = sb("pooled", [P, KC, STB])
        h1 = sb("h1", [A, STB])
        h1x = tz[0:A, 1, 0].rearrange("a (b q) -> a b q", b=STB)
        gt = sb("gt", [P, ST])
        stren = sb("stren", [P, ST])

        x_in, gel_in, g_in, o_out = sem("x_in"), sem("gel_in"), sem("g_in"), sem("o_out")
        f_in = [sem(f"f_in{i}") for i in range(ST)]
        T = range(ST)
        front_pe = Done(sem("front_pe"), ["ex", "up0", "up1", "xr0", "xr1", "q0", "q1", "k0", "k1", "v0", "v1",
                                          "qt0", "qt1", "qt2", "qt3", "kt0", "kt1"])
        front_dve = Done(sem("front_dve"), ["ex", "up0", "up1", "stat0", "aggr0", "norm0", "beta", "stat1", "aggr1", "norm1",
                                            "xs0", "xs1", "v0", "v1", "qt0", "qt1", "qt2", "qt3", "kt0", "kt1"])
        front_pool = Done(sem("front_pool"), ["eps0", "rstd0", "eps1", "rstd1",
                                              "sh0", "sh1"])
        fetch_pool = Done(sem("fetch_pool"), ["gnow", "upb"])
        front_act = Done(sem("front_act"), ["q0", "q1", "k0", "k1"])
        att_pe = Done(sem("att_pe"), ["sc0", "sc1", "ta0", "tb0", "oa0", "ob0", "sc2", "ta1", "tb1", "sc3", "oa1", "ob1",
                                      "ta2", "tb2", "oa2", "ob2", "ta3", "tb3", "oa3", "ob3", "ct0", "ct1"])
        att_dve = Done(sem("att_dve"), ["add0", "max0", "add1", "max1", "add2", "max2", "ra0", "ca0", "rb0", "cb0",
                                        "ra1", "ca1", "rb1", "cb1", "add3", "max3", "ra2", "ca2", "rb2", "cb2",
                                        "ra3", "ca3", "rb3", "cb3", "ctl0", "ctl1"])
        att_pool = Done(sem("att_pool"), ["sub0", "sub1", "xres", "sub2", "sub3"])
        att_act = Done(sem("att_act"), ["exp0", "ta0", "tb0", "exp1", "ta1", "tb1", "exp2", "ta2", "tb2", "exp3",
                                        "ta3", "tb3", "ct0", "ct1"])
        w1s = [[f"w1_{f}" for f in range(half * HF, (half + 1) * HF)] for half in range(2)]
        post_pe = Done(sem("post_pe"), ["wo0", "wo1", "yr0", "yr1", "hr0", "hr1"] + w1s[0] + ["w2a_0", "w2a_1"]
                       + w1s[1] + ["w2b_0", "w2b_1"])
        ffs = [[f"ff{f}" for f in range(half * HF, (half + 1) * HF)] for half in range(2)]
        post_dve = Done(sem("post_dve"), ["wo0", "wo1", "stat", "aggr", "norm", "h0", "h1", "hl0", "hl1"] + ffs[0]
                        + ["w2a_0", "w2a_1"] + ffs[1] + ["w2b_0", "w2b_1"])
        post_pool = Done(sem("post_pool"), ["eps", "rstd"] + [f"lo{f}" for f in range(FC)])
        post_act = Done(sem("post_act"), ["y0", "y1", "hh0", "hh1"]
                        + ["w1_0", "w1_1", "hi0", "w1_2", "hi1", "w1_3", "hi2", "hi3"]
                        + ["w1_4", "w1_5", "hi4", "w1_6", "hi5", "w1_7", "hi6", "hi7"])
        rear_pe = Done(sem("rear_pe"), ["y2r0", "y2r1", "x2r0", "x2r1", "proj", "g1", "g2", "resp0", "resp1"])
        rear_dve = Done(sem("rear_dve"), ["rot0", "rot1", "pool", "h1x", "str", "resp0", "resp1"])
        rear_pool = Done(sem("rear_pool"), ["x2"])
        rear_act = Done(sem("rear_act"), ["x2t0", "x2t1", "pj", "h1", "g2"])
        ring = ["y2r0", "y2r1", "wo0", "wo1", "ex", "yr0", "yr1", "x2r0", "x2r1", "up0", "up1", "ta0", "tb0",
                "proj", "hr0", "hr1", "ta1", "tb1", "w1_0", "w1_1", "w1_2", "w1_3",
                "w2a_0", "ta2", "tb2", "w2a_1", "xr0", "xr1", "w1_4", "w1_5", "w1_6", "w1_7", "ta3", "tb3",
                "q0", "q1", "k0", "k1", "g1", "g2", "resp0", "resp1", "w2b_0", "v0", "v1", "qt0", "qt1", "ct0", "ct1",
                "qt2", "qt3", "kt0", "w2b_1", "kt1"]
        bank_of = {use: i % 4 for i, use in enumerate(ring)}
        bank_of["y2r0"], bank_of["y2r1"] = 2, 1
        bank_of["wo0"], bank_of["wo1"] = 0, 3
        for use in ring[ring.index("proj"):]:
            bank_of[use] = (0, 3, 2, 1)[bank_of[use]]

        def rb(use):
            return ps_l[:, bank_of[use], :]

        block = ctx.enter_context(nc.Block())

        def col(name, k=0):
            c = COLS[name].start + k
            return cols[:, c:c + 1]

        @block.sync
        def _(sp):
            def bias_load(i, tile):
                sp.dma_start(fs[i][:], a["fside"][bass.ds(tile, 1)].rearrange("o p h k -> (o p) h k")).then_inc(f_in[i], 16)

            def x_load(s):
                sp.dma_start(gcur[:], gel[bass.ds(s, 1)].rearrange("o p n -> (o p) n")).then_inc(gel_in, 16)
                sp.dma_start(xin[:, 0], a["x"][bass.ds(s, 1)].rearrange("o p i d -> (o p) i d")).then_inc(x_in, 16)

            def rnd(j, front, att_next, rear):
                if front:
                    sp.wait_ge(front_dve.sem, front_dve.at("up1", j))
                    x_load(j + 1)
                for i in T:
                    if att_next:
                        sp.wait_ge(att_pe.sem, att_pe.at(f"tb{i}", j))
                        bias_load(i, (j + 1) * ST + i)
                if rear:
                    store(j - 2)

            def store(s):
                sp.wait_ge(rear_dve.sem, rear_dve.at("resp1", s))
                sp.dma_start(out[bass.ds(s, 1)].rearrange("o p i d -> (o p) i d"), ob).then_inc(o_out, 16)

            x_load(0)
            for i in T:
                bias_load(i, i)
            rnd(0, True, True, False)
            rnd(1, True, True, False)
            with sp.Fori(2, NST - 1) as j:
                rnd(j, True, True, True)
            rnd(NST - 1, False, False, True)
            rnd(NST, False, False, True)
            store(NST - 1)
            sp.wait_ge(o_out, 16 * (NST + 1))

        @block.tensor
        def _(pe):
            mm, tr = nc.tensor.matmul, nc.tensor.transpose
            user = {}

            def bank(use, done, step, s, j):
                b = bank_of[use]
                if b in user:
                    last, last_step, back = user[b]
                    pe.wait_ge(last.sem, last.at(last_step, j + back))
                user[b] = (done, step, s - j if isinstance(j, int) else BACK[id(done)])
                return ps_l[:, b]

            BACK = {id(front_dve): 1, id(front_act): 1, id(att_act): 0, id(att_dve): 0, id(post_dve): -1, id(post_act): -1,
                    id(rear_dve): -2, id(rear_act): -2}

            def scores(i, s, j):
                if i == 0:
                    pe.wait_ge(front_dve.sem, front_dve.at("kt1", s))
                    prev = ("add3", s - 1)
                else:
                    prev = (f"add{i - 1}", s)
                if not (isinstance(s, int) and s == 0 and i == 0):
                    pe.wait_ge(att_dve.sem, att_dve.at(*prev))
                mv = maskneg[:, bass.ds(s * ST + i, 1), :].to_broadcast([P, H // 2, S])
                for b in range(2):
                    mm(ps_s[:, b, :], ident16[:], mv, start=True, stop=False)
                for slot in range(SLOTS):
                    for b in range(2):
                        hb = slice(64 * b, 64 * b + 64)
                        last = mm(ps_s[:, b, :].rearrange("p (g s k) -> p g s k", g=2, s=SLOTS)[:, :, slot, :],
                                  qbd[hb, i, slot, :], kbd[hb, i, slot], start=False, stop=(slot == SLOTS - 1))
                last.then_inc(*att_pe.step(f"sc{i}"))

            def probs_t(i, s, j):
                pe.wait_ge(att_act.sem, att_act.at(f"exp{i}", s))
                p2 = fs[i][:].rearrange("p (m t) k -> p m (t k)", t=2)
                for b, n in ((0, "ta"), (1, "tb")):
                    ps = bank(f"{n}{i}", att_act, f"{n}{i}", s, j)
                    for m in range(4):
                        last = tr(ps[:, m * P:(m + 1) * P], p2[:, b * 4 + m, :], ident[:])
                    last.then_inc(*att_pe.step(f"{n}{i}"))

            def context(i, s, j):
                if i == 0:
                    pe.wait_ge(front_dve.sem, front_dve.at("v1", s))
                for b, n, r in ((0, "oa", "a"), (1, "ob", "b")):
                    pe.wait_ge(att_act.sem, att_act.at(f"t{r}{i}", s))
                    if i > 0:
                        pe.wait_ge(att_dve.sem, att_dve.at(f"c{r}{i - 1}", s))
                    elif not (isinstance(s, int) and s == 0):
                        pe.wait_ge(att_dve.sem, att_dve.at(f"c{r}3", s - 1))
                    for m in range(4):
                        w = TILE_B * 2 * VW
                        last = mm(ps_o[:, b, m * w:(m + 1) * w], ptr[:, i % 2, b * 4 + m, :],
                                  vbd[:, i, b * 4 + m], start=True, stop=True)
                    last.then_inc(*att_pe.step(f"{n}{i}"))

            def context_t(s, j):
                for c in range(KC):
                    ps = bank(f"ct{c}", att_dve, f"ctl{c}", s, j)
                    pe.wait_ge(att_dve.sem, att_dve.at("cb3", s))
                    for i in T:
                        last = tr(ps[:, i * P:(i + 1) * P], ctok[:, i, c * P:(c + 1) * P], ident[:])
                    last.then_inc(*att_pe.step(f"ct{c}"))

            def expert(s, j):
                ps = bank("ex", front_dve, "ex", s, j)
                pe.wait_ge(g_in, (s + 1) * (16 * ST))
                pe.wait_ge(gel_in, (s + 1) * 16)
                tr(ps[:, ST * S:ST * S + P], ident[:], ident[:])
                for i in T:
                    for h in range(TILE_B):
                        r = slice(h * A, (h + 1) * A)
                        last = mm(ps[r, i * S:(i + 1) * S], wsel[r, i, :], gcur[r, i * S:(i + 1) * S], start=True, stop=True)
                last.then_inc(*front_pe.step("ex"))

            def up(s, j):
                pe.wait_ge(front_dve.sem, front_dve.at("ex", s))
                for b in range(2):
                    ps = bank(f"up{b}", front_dve, f"up{b}", s, j)
                    for i in range(2):
                        last = mm(ps[:, i * D:(i + 1) * D], eh[:, 2 * b + i, :], wup[:], start=True, stop=True)
                    last.then_inc(*front_pe.step(f"up{b}"))

            def x_by_feature(s, j):
                pe.wait_ge(front_dve.sem, front_dve.at("norm1", s))
                for c in range(KC):
                    ps = bank(f"xr{c}", front_dve, f"xs{c}", s, j)
                    for i in T:
                        last = tr(ps[:, i * P:(i + 1) * P], tok[:, i, c * P:(c + 1) * P], ident[:])
                    last.then_inc(*front_pe.step(f"xr{c}"))

            def project(name, w, done, s, j):
                pe.wait_ge(front_pool.sem, front_pool.at("sh1", s))
                for b in range(2):
                    ps = bank(f"{name}{b}", done, f"{name}{b}", s, j)
                    for i in range(2):
                        for k in range(KC):
                            last = mm(ps[:, i * D:(i + 1) * D], xt[:, k, (2 * b + i) * P:(2 * b + i + 1) * P], w[:, k, :],
                                      start=(k == 0), stop=(k == KC - 1))
                    last.then_inc(*front_pe.step(f"{name}{b}"))

            def queries_t(tt, s, j):
                for i in tt:
                    ps = bank(f"qt{i}", front_dve, f"qt{i}", s, j)
                    pe.wait_ge(front_act.sem, front_act.at(f"q{i // 2}", s))
                    for slot in range(SLOTS):
                        last = tr(ps[:, slot * P:(slot + 1) * P],
                                  qtok[:, i, slot * GRP:(slot + 1) * GRP].rearrange("p g h d -> p (g h d)"), ident[:])
                    last.then_inc(*front_pe.step(f"qt{i}"))

            def keys_t(b, s, j):
                ps = bank(f"kt{b}", front_dve, f"kt{b}", s, j)
                pe.wait_ge(front_act.sem, front_act.at(f"k{b}", s))
                for i in range(2):
                    for slot in range(SLOTS):
                        c = (i * SLOTS + slot) * S
                        last = mm(ps[:, c:c + S], ktok[:, 2 * b + i, slot * GRP:(slot + 1) * GRP].rearrange("p g h d -> p (g h d)"),
                                  fold[:], start=True, stop=True)
                last.then_inc(*front_pe.step(f"kt{b}"))

            def out_proj(s, j):
                pe.wait_ge(att_act.sem, att_act.at("ct1", s))
                for m in range(KC):
                    by_parts(f"wo{m}", woh, wol, range(KC), ctx_h, ctx_l, (att_dve, "ctl1"), post_dve, m, s, j)

            def to_tokens(name, pe_done, done, out_name, need, s, j):
                pe.wait_ge(post_dve.sem, post_dve.at(need, s))
                for b in range(2):
                    ps = bank(f"{name}{b}", done, f"{out_name}{b}", s, j)
                    for i in range(2):
                        for c in range(KC):
                            t = 2 * b + i
                            last = tr(ps[:, (i * KC + c) * P:(i * KC + c + 1) * P], yt[:, c, t * P:(t + 1) * P], ident[:])
                    last.then_inc(*pe_done.step(f"{name}{b}"))

            def to_features(name, src, pe_done, done, out_name, s, j):
                for c in range(KC):
                    ps = bank(f"{name}{c}", done, f"{out_name}{c}", s, j)
                    for i in T:
                        last = tr(ps[:, i * P:(i + 1) * P], src[:, i, c * P:(c + 1) * P], ident[:])
                    last.then_inc(*pe_done.step(f"{name}{c}"))

            def by_parts(name, wh, wl, w_k, xh, xl, need, done, m, s, j):
                ps = bank(name, done, name, s, j)
                for p, (w, x) in enumerate(((wh, xh), (wl, xh), (wh, xl))):
                    if p == 2:
                        pe.wait_ge(need[0].sem, need[0].at(need[1], s))
                    for i, k in enumerate(w_k):
                        last = mm(ps[:], w[:, k, m * P:(m + 1) * P], x[:, i, :], start=(p == 0 and i == 0),
                                  stop=(p == 2 and i == len(w_k) - 1))
                last.then_inc(*post_pe.step(name))

            def ff1(fr, s, j):
                for f in fr:
                    if f == 0:
                        pe.wait_ge(post_act.sem, post_act.at("hh1", s))
                    by_parts(f"w1_{f}", w1h, w1l, range(KC), hh, hl, (post_dve, "hl1"), post_act, f, s, j)

            def ff2(half, m, s, j):
                if m == 0:
                    pe.wait_ge(post_act.sem, post_act.at(f"hi{(half + 1) * HF - 1}", s))
                by_parts(f"w2{'ab'[half]}_{m}", w2h, w2l, range(half * HF, (half + 1) * HF), bigh, bigl,
                         (post_pool, f"lo{(half + 1) * HF - 1}"), post_dve, m, s, j)

            def gate1(s, j):
                ps = bank("g1", rear_act, "h1", s, j)
                pe.wait_ge(rear_dve.sem, rear_dve.at("pool", s))
                for k in range(KC):
                    last = mm(ps[0:A, 0:STB], gate_w1[:, k, :], pooled[:, k, :], start=(k == 0), stop=(k == KC - 1))
                last.then_inc(*rear_pe.step("g1"))

            def basis_proj(s, j):
                ps = bank("proj", rear_act, "pj", s, j)
                for k in range(KC):
                    last = mm(ps[0:R, :], basis_p[:, k, :], x2t[:, k, :], start=(k == 0), stop=(k == KC - 1))
                last.then_inc(*rear_pe.step("proj"))

            def gate2(s, j):
                ps = bank("g2", rear_act, "g2", s, j)
                pe.wait_ge(rear_dve.sem, rear_dve.at("h1x", s))
                hx = h1x.rearrange("a b q -> a (b q)")
                for i in T:
                    last = mm(ps[:, i:i + 1], hx[:, i * P:(i + 1) * P], cols[0:A, COLS["gate_w2"]], start=True, stop=True)
                last.then_inc(*rear_pe.step("g2"))

            def response(s, j):
                for b in range(2):
                    ps = bank(f"resp{b}", rear_dve, f"resp{b}", s, j)
                    pe.wait_ge(rear_act.sem, rear_act.at("pj", s))
                    for i in range(2):
                        t = 2 * b + i
                        last = mm(ps[:, i * D:(i + 1) * D], pj[:, t * P:(t + 1) * P], resp[:], start=True, stop=True)
                    last.then_inc(*rear_pe.step(f"resp{b}"))

            def rnd(j, front, att, post, rear):
                f, p, r = j + 1, j - 1, j - 2
                for b, (done, step, back) in user.items():
                    user[b] = done, step, back - 1
                if rear: to_tokens("y2r", rear_pe, rear_dve, "rot", "w2b_1", r, j)
                if post: out_proj(p, j)
                if att: scores(0, j, j)
                if front: expert(f, j)
                if post: to_tokens("yr", post_pe, post_act, "y", "wo1", p, j)
                if att: scores(1, j, j)
                if rear:
                    pe.wait_ge(rear_pool.sem, rear_pool.at("x2", r))
                    to_features("x2r", x2, rear_pe, rear_act, "x2t", r, j)
                if front: up(f, j)
                if att: probs_t(0, j, j)
                if rear:
                    pe.wait_ge(rear_act.sem, rear_act.at("x2t1", r))
                    basis_proj(r, j)
                if att: context(0, j, j)
                if post:
                    pe.wait_ge(post_dve.sem, post_dve.at("norm", p))
                    to_features("hr", ptok, post_pe, post_dve, "h", p, j)
                if att: scores(2, j, j); probs_t(1, j, j)
                if post: ff1(range(HF), p, j)
                if att: scores(3, j, j); context(1, j, j)
                if post: ff2(0, 0, p, j)
                if att: probs_t(2, j, j)
                if post: ff2(0, 1, p, j)
                if att: context(2, j, j)
                if front: x_by_feature(f, j)
                if post: ff1(range(HF, FC), p, j)
                if att: probs_t(3, j, j)
                if front: project("q", wq, front_act, f, j); project("k", wk, front_act, f, j)
                if rear: gate1(r, j)
                if att: context(3, j, j)
                if rear: gate2(r, j); response(r, j)
                if post: ff2(1, 0, p, j)
                if front:
                    project("v", wv, front_dve, f, j)
                    queries_t((0, 1), f, j)
                if att: context_t(j, j)
                if front: queries_t((2, 3), f, j); keys_t(0, f, j)
                if post: ff2(1, 1, p, j)
                if front: keys_t(1, f, j)

            rnd(-1, True, False, False, False)
            rnd(0, True, True, False, False)
            rnd(1, True, True, True, False)
            with pe.Fori(2, NST - 1) as j:
                rnd(j, True, True, True, True)
            rnd(NST - 1, False, True, True, True)
            rnd(NST, False, False, True, True)
            rnd(NST + 1, False, False, False, True)

        @block.vector
        def _(dve):
            v = nc.vector

            def softmax(i, s):
                dve.wait_ge(att_pe.sem, att_pe.at(f"sc{i}", s))
                dve.wait_ge(f_in[i], (s + 1) * 16)
                flat = fs[i][:].rearrange("p h k -> p (h k)")
                v.tensor_tensor(flat, ps_s[:].rearrange("p b n -> p (b n)"), flat, ALU.add).then_inc(*att_dve.step(f"add{i}"))
                dve.wait_ge(att_dve.sem, att_dve.at(f"add{i}", s))
                v.reduce_max(mx[:, i, :], fs[i][:], axis=AX).then_inc(*att_dve.step(f"max{i}"))

            def context(i, s):
                for b, r in ((0, "a"), (1, "b")):
                    dve.wait_ge(att_pe.sem, att_pe.at(f"o{r}{i}", s))
                    o = ps_o[:, b, 0:4 * TILE_B * 2 * VW].rearrange("p (m h t w) -> p m h t w", m=4, h=TILE_B, t=2)
                    for h in range(TILE_B):
                        rows_h = slice(h * S, (h + 1) * S)
                        last = v.reciprocal(rc[rows_h, b, :].rearrange("p (m t) -> p m t", t=2), o[rows_h, :, h, :, DH])
                    last.then_inc(*att_dve.step(f"r{r}{i}"))
                    dve.wait_ge(att_dve.sem, att_dve.at(f"r{r}{i}", s))
                    for h in range(TILE_B):
                        rows_h = slice(h * S, (h + 1) * S)
                        last = v.tensor_tensor(
                            ctok[rows_h, i, b * P:(b + 1) * P].rearrange("p (m t w) -> p m t w", m=4, t=2),
                            o[rows_h, :, h, :, 0:DH],
                            rc[rows_h, b, :].rearrange("p (m t) -> p m t", t=2).unsqueeze(3).to_broadcast([S, 4, 2, DH]), ALU.mult)
                    last.then_inc(*att_dve.step(f"c{r}{i}"))

            def expert(s):
                dve.wait_ge(front_pe.sem, front_pe.at("ex", s))
                for h in range(TILE_B):
                    r = slice(h * A, (h + 1) * A)
                    last = v.tensor_tensor(eh[r, :, h * S:(h + 1) * S], rb("ex")[r, 0:ST * S].rearrange("p (i q) -> p i q", i=ST),
                                           bias_e[r, bass.ds(s * ST, ST)].unsqueeze(2).to_broadcast([A, ST, S]), ALU.add)
                last.then_inc(*front_dve.step("ex"))

            def up(s):
                dve.wait_ge(fetch_pool.sem, fetch_pool.at("upb", s))
                for b in range(2):
                    dve.wait_ge(front_pe.sem, front_pe.at(f"up{b}", s))
                    v.tensor_tensor(tok[:, 2 * b:2 * b + 2, :], rb(f"up{b}").rearrange("p (i d) -> p i d", i=2),
                                    xin[:, 0, 2 * b:2 * b + 2, :], ALU.add).then_inc(*front_dve.step(f"up{b}"))

            def stats(src, st, mv, done, n, s, need):
                dve.wait_ge(*need)
                for i in T:
                    last = v.bn_stats(st[:, i, :], src[:, i, :])
                last.then_inc(*done.step(f"stat{n}"))
                dve.wait_ge(done.sem, done.at(f"stat{n}", s))
                v.memset(spare[:, 3 + (0 if n == "" else 1 + n):4 + (0 if n == "" else 1 + n)], 0.0)
                for i in T:
                    last = v.bn_aggr(mv[:, i, :], st[:, i, :])
                last.then_inc(*done.step(f"aggr{n}"))

            def norm(src, mv, rs, done, n, pool, s):
                dve.wait_ge(pool.sem, pool.at(f"rstd{n}", s))
                for i in T:
                    last = v.tensor_scalar(src[:, i, :], src[:, i, :], mv[:, i, 0:1], rs[:, i:i + 1], ALU.subtract, ALU.mult)
                last.then_inc(*done.step(f"norm{n}"))

            def times_gamma(s):
                dve.wait_ge(front_dve.sem, front_dve.at("aggr0", s))
                for i in T:
                    last = v.scalar_tensor_tensor(tok[:, i, :], tok[:, i, :], fmv[:, 0, i, 0:1], rows[:, 0, :], ALU.subtract, ALU.mult)
                last.then_inc(*front_dve.step("norm0"))

            def plus_beta(s):
                dve.wait_ge(front_dve.sem, front_dve.at("norm0", s))
                dve.wait_ge(front_pool.sem, front_pool.at("rstd0", s))
                for i in T:
                    last = v.scalar_tensor_tensor(tok[:, i, :], tok[:, i, :], frs[:, 0, 1, i:i + 1], rows[:, 1, :], ALU.mult, ALU.add)
                last.then_inc(*front_dve.step("beta"))

            def modulate(s):
                for c in range(KC):
                    dve.wait_ge(front_pe.sem, front_pe.at(f"xr{c}", s))
                    v.tensor_tensor(xt[:, c, :].rearrange("p (b q) -> p b q", b=STB), rb(f"xr{c}").rearrange("p (b q) -> p b q", b=STB),
                                    scale1[:, c, bass.ds(s * STB, STB)].unsqueeze(2).to_broadcast([P, STB, S]),
                                    ALU.mult).then_inc(*front_dve.step(f"xs{c}"))

            def values(s):
                for b in range(2):
                    dve.wait_ge(front_pe.sem, front_pe.at(f"v{b}", s))
                    ps = rb(f"v{b}").rearrange("p (i m t w) -> p i m t w", i=2, t=2, w=DH)
                    for h in range(TILE_B):
                        for t in range(2):
                            last = v.tensor_copy(vbd[t * S:(t + 1) * S, 2 * b:2 * b + 2, :, h, t, 0:DH], ps[h * S:(h + 1) * S, :, :, t, :])
                    last.then_inc(*front_dve.step(f"v{b}"))

            def context_low(s):
                for c in range(KC):
                    dve.wait_ge(att_act.sem, att_act.at(f"ct{c}", s))
                    v.scalar_tensor_tensor(ctx_l[:, c, :], rb(f"ct{c}"), col("bv", c), ctx_h[:, c, :].bitcast(F32), ALU.add,
                                           ALU.subtract).then_inc(*att_dve.step(f"ctl{c}"))

            def queries(tt, s):
                for i in tt:
                    dve.wait_ge(front_pe.sem, front_pe.at(f"qt{i}", s))
                    v.scalar_tensor_tensor(qbd[:, i].rearrange("p s (h q) -> p (s h) q", h=TILE_B),
                                           rb(f"qt{i}").rearrange("p (s q) -> p s q", q=S), 0.25,
                                           cols[:, COLS["bq"]].unsqueeze(2).to_broadcast([P, 2 * SLOTS, S]),
                                           ALU.mult, ALU.add).then_inc(*front_dve.step(f"qt{i}"))

            def keys(b, s):
                dve.wait_ge(front_pe.sem, front_pe.at(f"kt{b}", s))
                for g in range(GRP):
                    rg = slice(32 * g, 32 * g + 32)
                    last = v.tensor_tensor(kbd[rg, 2 * b:2 * b + 2, :, g % 2, :], rb(f"kt{b}")[rg].rearrange("p (i s q) -> p i s q", i=2, q=S),
                                           cols[rg, COLS["bk"]].unsqueeze(1).unsqueeze(3).to_broadcast([32, 2, SLOTS, S]), ALU.add)
                last.then_inc(*front_dve.step(f"kt{b}"))

            def out_proj(s):
                dve.wait_ge(att_pool.sem, att_pool.at("xres", s))
                for m in range(KC):
                    dve.wait_ge(post_pe.sem, post_pe.at(f"wo{m}", s))
                    v.scalar_tensor_tensor(yt[:, m, :], rb(f"wo{m}"), col("bo", m), xres[:, m, :], ALU.add,
                                           ALU.add).then_inc(*post_dve.step(f"wo{m}"))

            def h_t(s):
                if not (isinstance(s, int) and s == 0):
                    dve.wait_ge(rear_dve.sem, rear_dve.at("pool", s - 1))
                for c in range(KC):
                    dve.wait_ge(post_pe.sem, post_pe.at(f"hr{c}", s))
                    v.tensor_scalar(ht[:, c, :], rb(f"hr{c}"), col("g2", c), col("beta2", c), ALU.mult,
                                    ALU.add).then_inc(*post_dve.step(f"h{c}"))

            def h_low(s):
                for c in range(KC):
                    dve.wait_ge(post_act.sem, post_act.at(f"hh{c}", s))
                    v.tensor_tensor(hl[:, c, :], ht[:, c, :], hh[:, c, :].bitcast(F32), ALU.subtract).then_inc(*post_dve.step(f"hl{c}"))

            def ff(fr, s):
                for f in fr:
                    dve.wait_ge(post_act.sem, post_act.at(f"w1_{f}", s))
                    if f >= 2:
                        dve.wait_ge(post_pool.sem, post_pool.at(f"lo{f - 2}", s))
                    v.scalar_tensor_tensor(ht[:, f % 2, :], tz[:, f % 2, 0, :], 1.0, tz[:, f % 2, 1, :], ALU.add,
                                           ALU.mult).then_inc(*post_dve.step(f"ff{f}"))

            def ff2a(s):
                for m in range(KC):
                    dve.wait_ge(post_pe.sem, post_pe.at(f"w2a_{m}", s))
                    v.tensor_tensor(yt[:, m, :], rb(f"w2a_{m}"), yt[:, m, :], ALU.add).then_inc(*post_dve.step(f"w2a_{m}"))

            def ff2b(m, s):
                dve.wait_ge(post_pe.sem, post_pe.at(f"w2b_{m}", s))
                v.scalar_tensor_tensor(yt[:, m, :], rb(f"w2b_{m}"), col("b2", m), yt[:, m, :], ALU.add,
                                       ALU.add).then_inc(*post_dve.step(f"w2b_{m}"))

            def rotate(s):
                for b in range(2):
                    dve.wait_ge(rear_pe.sem, rear_pe.at(f"y2r{b}", s))
                    v.tensor_tensor(x2[:, 2 * b:2 * b + 2, :].rearrange("p i (n w) -> p i n w", w=4),
                                    rb(f"y2r{b}").rearrange("p (i n w) -> p i n w", i=2, w=4),
                                    rot_c[:, bass.ds(s * ST + 2 * b, 2), :].unsqueeze(2).to_broadcast([P, 2, D // 4, 4]), ALU.mult)
                    for i in range(2):
                        last = v.tensor_tensor(swp[:, 2 * b + i, :].rearrange("p (n r w) -> p n r w", r=2, w=2),
                                               rb(f"y2r{b}")[:, i * D:(i + 1) * D].rearrange("p (n r w) -> p n r w", r=2, w=2)[:, :, :, ::-1],
                                               rot_s[:, bass.ds(s * ST + 2 * b + i, 1), :].rearrange("p o (r w) -> p o r w", r=2)
                                               .to_broadcast([P, D // 4, 2, 2]), ALU.mult)
                    last.then_inc(*rear_dve.step(f"rot{b}"))

            def pool(s):
                dve.wait_ge(rear_act.sem, rear_act.at("x2t1", s))
                v.reduce_sum(pooled[:], x2t[:].rearrange("p k (b q) -> p k b q", q=S), axis=AX).then_inc(*rear_dve.step("pool"))

            def hidden(s):
                dve.wait_ge(rear_act.sem, rear_act.at("h1", s))
                v.tensor_copy(h1x, h1[:].unsqueeze(2).to_broadcast([A, STB, S])).then_inc(*rear_dve.step("h1x"))

            def strength(s):
                dve.wait_ge(rear_act.sem, rear_act.at("g2", s))
                v.scalar_tensor_tensor(stren[:], gt[:], 1.0, modh[:, bass.ds(s * ST, ST)], ALU.add,
                                       ALU.mult).then_inc(*rear_dve.step("str"))

            def response(s):
                dve.wait_ge(rear_dve.sem, rear_dve.at("str", s))
                dve.wait_ge(o_out, (s + 1) * 16)
                for b in range(2):
                    dve.wait_ge(rear_pe.sem, rear_pe.at(f"resp{b}", s))
                    for i in range(2):
                        t = 2 * b + i
                        last = v.scalar_tensor_tensor(ob[:, t, :], rb(f"resp{b}")[:, i * D:(i + 1) * D], stren[:, t:t + 1], x2[:, t, :],
                                                      ALU.mult, ALU.add)
                    last.then_inc(*rear_dve.step(f"resp{b}"))

            def rnd(j, front, att, post, rear):
                f, p, r = j + 1, j - 1, j - 2
                if rear: rotate(r)
                if post: out_proj(p)
                if att: softmax(0, j)
                if front: expert(f)
                if post:
                    stats(ptok, pst, pmv, post_dve, "", p, (post_act.sem, post_act.at("y1", p)))
                if att: softmax(1, j)
                if front: up(f)
                if post: norm(ptok, pmv, prs[:, 1], post_dve, "", post_pool, p)
                if rear: pool(r)
                if post: h_t(p)
                if front: stats(tok, fst[:, 0], fmv[:, 0], front_dve, 0, f, (front_dve.sem, front_dve.at("up1", f)))
                if post: h_low(p)
                if att: softmax(2, j)
                if post: ff(range(0, 2), p)
                if att: context(0, j)
                if post: ff(range(2, HF), p)
                if front:
                    times_gamma(f)
                    plus_beta(f)
                    stats(tok, fst[:, 1], fmv[:, 1], front_dve, 1, f, (front_dve.sem, front_dve.at("beta", f)))
                if att: context(1, j)
                if front: norm(tok, fmv[:, 1], frs[:, 1, 1], front_dve, 1, front_pool, f)
                if post: ff2a(p)
                if att: softmax(3, j)
                if front: modulate(f)
                if att: context(2, j)
                if post: ff(range(HF, FC), p)
                if rear: hidden(r)
                if att: context(3, j)
                if rear: strength(r); response(r)
                if post: ff2b(0, p)
                if front:
                    values(f)
                    queries((0, 1), f)
                if att: context_low(j)
                if front:
                    queries((2, 3), f)
                    keys(0, f)
                if post: ff2b(1, p)
                if front: keys(1, f)

            v.memset(ob[:, 0, 0:1], 0.0).then_inc(o_out, 16)
            rnd(-1, True, False, False, False)
            rnd(0, True, True, False, False)
            rnd(1, True, True, True, False)
            with dve.Fori(2, NST - 1) as j:
                rnd(j, True, True, True, True)
            rnd(NST - 1, False, True, True, True)
            rnd(NST, False, False, True, True)
            rnd(NST + 1, False, False, False, True)

        @block.scalar
        def _(act):
            fn = nc.scalar.activation

            def exp(i, s):
                act.wait_ge(att_pool.sem, att_pool.at(f"sub{i}", s))
                fn(fs[i][:], fs[i][:], ACT.Exp).then_inc(*att_act.step(f"exp{i}"))

            def probs(i, s):
                for b, n in ((0, "ta"), (1, "tb")):
                    act.wait_ge(att_pe.sem, att_pe.at(f"{n}{i}", s))
                    fn(ptr[:, i % 2, b * 4:(b + 1) * 4, :].rearrange("p m q -> p (m q)"), rb(f"{n}{i}"), ACT.Copy).then_inc(*att_act.step(f"{n}{i}"))

            def context_t(s):
                for c in range(KC):
                    act.wait_ge(att_pe.sem, att_pe.at(f"ct{c}", s))
                    fn(ctx_h[:, c, :], rb(f"ct{c}"), ACT.Identity, bias=col("bv", c)).then_inc(*att_act.step(f"ct{c}"))

            def tokens(name, dst, s):
                for b in range(2):
                    act.wait_ge(front_pe.sem, front_pe.at(f"{name}{b}", s))
                    for h in range(TILE_B):
                        r = slice(h * S, (h + 1) * S)
                        last = fn(dst[r, 2 * b:2 * b + 2, :, h, :], rb(f"{name}{b}")[r, :].rearrange("p (i n w) -> p i n w", i=2, w=DH), ACT.Copy)
                    last.then_inc(*front_act.step(f"{name}{b}"))

            def y(s):
                for b in range(2):
                    act.wait_ge(post_pe.sem, post_pe.at(f"yr{b}", s))
                    fn(ptok[:, 2 * b:2 * b + 2, :], rb(f"yr{b}").rearrange("p (i d) -> p i d", i=2), ACT.Copy).then_inc(*post_act.step(f"y{b}"))

            def h_high(s):
                for c in range(KC):
                    act.wait_ge(post_dve.sem, post_dve.at(f"h{c}", s))
                    fn(hh[:, c, :], ht[:, c, :], ACT.Copy).then_inc(*post_act.step(f"hh{c}"))

            def ff(f, s):
                act.wait_ge(post_pe.sem, post_pe.at(f"w1_{f}", s))
                if f >= 2:
                    act.wait_ge(post_dve.sem, post_dve.at(f"ff{f - 2}", s))
                fn(tz[:, f % 2, 0, :], rb(f"w1_{f}"), ACT.Tanh, bias=tanh_b1[:, f:f + 1], scale=0.851)
                fn(tz[:, f % 2, 1, :], rb(f"w1_{f}"), ACT.Identity, bias=half_b1[:, f:f + 1], scale=0.5).then_inc(*post_act.step(f"w1_{f}"))

            def high(f, s):
                act.wait_ge(post_dve.sem, post_dve.at(f"ff{f}", s))
                fn(bigh[:, f % HF, :], ht[:, f % 2, :], ACT.Copy).then_inc(*post_act.step(f"hi{f}"))

            def ff_half(half, s, between=lambda: None):
                a = half * HF
                ff(a, s); ff(a + 1, s); high(a, s); between(); ff(a + 2, s); high(a + 1, s); ff(a + 3, s); high(a + 2, s); high(a + 3, s)

            def x2_t(s):
                for c in range(KC):
                    act.wait_ge(rear_pe.sem, rear_pe.at(f"x2r{c}", s))
                    fn(x2t[:, c, :], rb(f"x2r{c}"), ACT.Copy).then_inc(*rear_act.step(f"x2t{c}"))

            def projected(s):
                act.wait_ge(rear_pe.sem, rear_pe.at("proj", s))
                fn(pj[0:R, :], rb("proj")[0:R, :], ACT.Copy).then_inc(*rear_act.step("pj"))

            def gate1(s):
                act.wait_ge(rear_pe.sem, rear_pe.at("g1", s))
                fn(h1[:], rb("g1")[0:A, 0:STB], ACT.Relu, bias=cols[0:A, COLS["gate_b1"]], scale=1.0 / S).then_inc(*rear_act.step("h1"))

            def gate2(s):
                act.wait_ge(rear_pe.sem, rear_pe.at("g2", s))
                fn(gt[:], rb("g2")[:, 0:ST], ACT.Tanh, bias=half_gb2[:], scale=0.5).then_inc(*rear_act.step("g2"))

            def rnd(j, front, att, post, rear):
                f, p, r = j + 1, j - 1, j - 2
                if post: y(p)
                if att: exp(0, j)
                if rear: x2_t(r)
                if att: probs(0, j); exp(1, j)
                if rear: projected(r)
                if post: h_high(p)
                if att: probs(1, j)
                if post: ff_half(0, p)
                if att: exp(2, j)
                if att: probs(2, j)
                if post: ff_half(1, p, lambda: att and exp(3, j))
                elif att: exp(3, j)
                if att: probs(3, j)
                if front: tokens("q", qtok, f); tokens("k", ktok, f)
                if rear: gate1(r)
                if rear: gate2(r)
                if att: context_t(j)

            rnd(-1, True, False, False, False)
            rnd(0, True, True, False, False)
            rnd(1, True, True, True, False)
            with act.Fori(2, NST - 1) as j:
                rnd(j, True, True, True, True)
            rnd(NST - 1, False, True, True, True)
            rnd(NST, False, False, True, True)
            rnd(NST + 1, False, False, False, True)

        @block.gpsimd
        def _(pool):
            gp = nc.gpsimd

            def carry_pool(k):
                gp.tensor_tensor(spare[:, k:k + 1], neghalf[:, 0:1], neghalf[:, 0:1], ALU.mult)

            def gather(s):
                if not (isinstance(s, int) and s == 0):
                    pool.wait_ge(front_pe.sem, front_pe.at("ex", s - 1))
                    carry_pool(0)
                gp.tensor_copy(gnow[:], gidx[:, bass.ds(s * ST, ST)]).then_inc(*fetch_pool.step("gnow"))
                pool.wait_ge(fetch_pool.sem, fetch_pool.at("gnow", s))
                carry_pool(1)
                for i in T:
                    gp.indirect_dma_start(out=wsel[:, i, :], out_offset=None, in_=a["expert_w"],
                                          in_offset=bass.IndirectOffsetOnAxis(ap=gnow[:, i:i + 1], axis=0)
                                          ).then_inc(g_in, 16)

            def up_bias(s):
                pool.wait_ge(x_in, (s + 1) * 16)
                gp.tensor_tensor(xin[:, 0], xin[:, 0], rows[:, 2:3, :].to_broadcast([P, ST, D]), ALU.add).then_inc(*fetch_pool.step("upb"))

            def rstd(mv, rs, dve_done, pool_done, n, s):
                pool.wait_ge(dve_done.sem, dve_done.at(f"aggr{n}", s))
                gp.tensor_tensor(rs[:, 0, :], mv[:, :, 1], eps[:], ALU.add).then_inc(*pool_done.step(f"eps{n}"))
                pool.wait_ge(pool_done.sem, pool_done.at(f"eps{n}", s))
                gp.tensor_tensor(rs[:, 1, :], rs[:, 0, :], neghalf[:], ALU.pow).then_inc(*pool_done.step(f"rstd{n}"))

            def shifts(s):
                for c in range(KC):
                    pool.wait_ge(front_dve.sem, front_dve.at(f"xs{c}", s))
                    xv = xt[:, c, :].rearrange("p (b q) -> p b q", b=STB)
                    gp.tensor_tensor(xv, xv, shift[:, c, bass.ds(s * STB, STB)].unsqueeze(2).to_broadcast([P, STB, S]),
                                     ALU.add).then_inc(*front_pool.step(f"sh{c}"))

            def sub(i, s):
                pool.wait_ge(att_dve.sem, att_dve.at(f"max{i}", s))
                gp.tensor_tensor(fs[i][:], fs[i][:], mx[:, i, :].unsqueeze(2).to_broadcast([P, H, S]),
                                 ALU.subtract).then_inc(*att_pool.step(f"sub{i}"))

            def residual(s):
                if not (isinstance(s, int) and s == 0):
                    pool.wait_ge(post_dve.sem, post_dve.at("wo1", s - 1))
                    carry_pool(2)
                gp.tensor_copy(xres[:], xt[:]).then_inc(*att_pool.step("xres"))

            def low(fr, s):
                for f in fr:
                    pool.wait_ge(post_act.sem, post_act.at(f"hi{f}", s))
                    gp.tensor_tensor(bigl[:, f % HF, :], ht[:, f % 2, :], bigh[:, f % HF, :].bitcast(F32),
                                     ALU.subtract).then_inc(*post_pool.step(f"lo{f}"))

            def x2_sum(s):
                pool.wait_ge(rear_dve.sem, rear_dve.at("rot1", s))
                gp.tensor_tensor(x2[:], x2[:], swp, ALU.add).then_inc(*rear_pool.step("x2"))

            def rnd(j, front, att, post, rear, fetch=True):
                f, p, r = j + 1, j - 1, j - 2
                if rear: x2_sum(r)
                if att: sub(0, j)
                if post: rstd(pmv, prs, post_dve, post_pool, "", p)
                if att: sub(1, j); residual(j)
                if front: rstd(fmv[:, 0], frs[:, 0], front_dve, front_pool, 0, f)
                if att: sub(2, j)
                if post: low(range(HF), p)
                if front: rstd(fmv[:, 1], frs[:, 1], front_dve, front_pool, 1, f)
                if att: sub(3, j)
                if front: shifts(f)
                if post: low(range(HF, FC), p)
                if fetch: gather(f + 1); up_bias(f + 1)

            gather(0)
            up_bias(0)
            rnd(-1, True, False, False, False)
            rnd(0, True, True, False, False)
            rnd(1, True, True, True, False)
            with pool.Fori(2, NST - 2) as j:
                rnd(j, True, True, True, True)
            rnd(NST - 2, True, True, True, True, fetch=False)
            rnd(NST - 1, False, True, True, True, fetch=False)
            rnd(NST, False, False, True, True, fetch=False)
            rnd(NST + 1, False, False, False, True, fetch=False)


D_RED = 14
D_EMB = 38
GSD = 9


def kernel(x, itok_B_0_15, itok_B_34_63, fside_Bx16xSxS_0, condB_theta, condB_phi, condB_safetyscore, mask_Bx1xSxS_bk0,
           L0_cond_down_W, L0_cond_down_b, L0_cond_up_W, L0_cond_up_b, L0_cond_expert_W, L0_cond_expert_b,
           L0_cond_domain_emb, L0_cond_ln_gamma, L0_cond_ln_beta, L1_cond_W_ada, L1_cond_b_ada, L1_cond_Wq, L1_cond_bq,
           L1_cond_Wk, L1_cond_bk, L1_cond_Wv, L1_cond_bv, L1_cond_Wo, L1_cond_bo, L1_cond_W1, L1_cond_b1, L1_cond_W2,
           L1_cond_b2, L1_cond_g2, L1_cond_beta2, L3_cond_U, L3_cond_V, L3_cond_safety_bias, L3_cond_gate_w1,
           L3_cond_gate_b1, L3_cond_gate_w2, L3_cond_gate_b2, L3_cond_resp_w, L3_cond_resp_b):
    import concourse.bacc as bacc
    from concourse.bass_utils import run_bass_kernel_spmd

    f32 = np.float32
    arr = lambda t: np.asarray(t)
    slots = np.arange(H).reshape(SLOTS, GRP)
    n_of = np.empty((SLOTS, GRP), int)
    for slot in range(SLOTS):
        for g in range(GRP):
            n_of[slot, g] = (g // 2) * (H // 2) + (g % 2) * SLOTS + slot
    order = np.argsort(n_of.ravel())
    block_head = n_of.ravel()
    qk_cols = (block_head[:, None] * DH + np.arange(DH)).ravel()

    def by_slot(vec):
        v = arr(vec).astype(f32)[qk_cols].reshape(SLOTS, GRP, 1, DH)
        return np.broadcast_to(v, (SLOTS, GRP, TILE_B, DH)).transpose(1, 2, 3, 0).reshape(P, SLOTS)

    def chunks(vec):
        return arr(vec).reshape(-1, P).T

    def padded(vec):
        c = np.zeros((P, 1), f32)
        c[:len(vec), 0] = vec
        return c

    bq = np.zeros((GRP, TILE_B, DH, SLOTS, TILE_B), f32)
    bq_rows = by_slot(L1_cond_bq).reshape(GRP, TILE_B, DH, SLOTS)
    for h in range(TILE_B):
        bq[:, h, :, :, h] = bq_rows[:, h]
    half = D // 2
    freq = np.exp(np.arange(half, dtype=f32) * f32(-np.log(10000.0) / (half - 1))).astype(f32)
    parts = {
        "bk": by_slot(L1_cond_bk), "bq": bq.reshape(P, 2 * SLOTS), "bv": chunks(L1_cond_bv), "bo": chunks(L1_cond_bo),
        "b1": chunks(L1_cond_b1), "b2": chunks(L1_cond_b2), "g2": chunks(L1_cond_g2), "beta2": chunks(L1_cond_beta2),
        "b_scale": chunks(arr(L1_cond_b_ada)[:D]), "b_shift": chunks(arr(L1_cond_b_ada)[D:]),
        "gate_b1": padded(arr(L3_cond_gate_b1)), "down_b": np.tile(arr(L0_cond_down_b), TILE_B)[:, None],
        "gate_b2": np.broadcast_to(arr(L3_cond_gate_b2)[None], (P, 1)), "freq": freq[:, None],
        "gate_w2": padded(arr(L3_cond_gate_w2)[0]),
    }
    by_tile = lambda t: np.repeat(arr(t).reshape(NT, TILE_B), S, axis=1).T
    data = {
        "x": arr(x).reshape(NST, ST, P, D).transpose(0, 2, 1, 3),
        "fside": arr(fside_Bx16xSxS_0).reshape(NT, TILE_B, H, S, S).transpose(0, 1, 3, 2, 4).reshape(NT, P, H, S),
        "mask": arr(mask_Bx1xSxS_bk0).reshape(NT, P, S).transpose(1, 0, 2),
        "tstep": np.broadcast_to(arr(itok_B_34_63)[None], (P, B)),
        "tokf": np.stack([by_tile(condB_theta), by_tile(condB_phi), by_tile(condB_safetyscore)], 1),
        "ids_tok": by_tile(itok_B_0_15),
        "ids_row": np.broadcast_to(arr(itok_B_0_15)[None], (E, B)),
        "etab": np.stack([arr(L0_cond_expert_b), arr(L0_cond_domain_emb)], 1),
        "expert_w": np.concatenate([arr(L0_cond_expert_W).transpose(0, 2, 1).reshape(E * A, A), np.eye(A, dtype=f32)]),
        "wdown": arr(L0_cond_down_W).T, "wup": arr(L0_cond_up_W).T,
        "rows": np.broadcast_to(np.stack([arr(L0_cond_ln_gamma), arr(L0_cond_ln_beta), arr(L0_cond_up_b)])[None], (P, 3, D)),
        "wada": arr(L1_cond_W_ada),
        "wq": arr(L1_cond_Wq)[:, qk_cols], "wk": arr(L1_cond_Wk)[:, qk_cols], "wv": arr(L1_cond_Wv), "wo": arr(L1_cond_Wo),
        "w1": arr(L1_cond_W1), "w2": arr(L1_cond_W2),
        "gate_w1": arr(L3_cond_gate_w1).T,
        "resp": np.concatenate([arr(L3_cond_resp_w).T, arr(L3_cond_resp_b)[None], arr(L3_cond_safety_bias)[None]]),
        "uv": np.concatenate([arr(L3_cond_U).T, arr(L3_cond_V).T]),
        "cols": np.concatenate([parts[n] for n in COLS], 1),
    }
    nc = bacc.Bacc("TRN2", target_bir_lowering=False, num_devices=1)
    arrays, args = {}, {}
    for name, t in data.items():
        t = np.ascontiguousarray(t)
        arrays[f"in_{name}"] = t
        args[name] = nc.dram_tensor(f"in_{name}", t.shape, mybir.dt.from_np(t.dtype), kind="ExternalInput").ap()
    out = nc.dram_tensor("out_0", (NST, P, ST, D), F32, kind="ExternalOutput").ap()
    build(nc, args, out)
    r = run_bass_kernel_spmd(nc, [arrays], core_ids=[0])
    got = r.results[0]["out_0"]
    return got.transpose(0, 2, 1, 3).reshape(B, S, D)
```
